# Optimizing a Trainium2 kernel written in Bass

```python
import numpy as np
import jax
import jax.numpy as jnp

def _softmax(x, axis=-1):
    return jax.nn.softmax(x, axis=axis)

def _gelu(x):
    return jax.nn.gelu(x, approximate=True)

def _silu(x):
    return jax.nn.silu(x)

def _sigmoid(x):
    return jax.nn.sigmoid(x)

def _layernorm(x, axis=-1, eps=1e-05):
    m = jnp.mean(x, axis=axis, keepdims=True)
    v = jnp.var(x, axis=axis, keepdims=True)
    return (x - m) / jnp.sqrt(v + eps)

def _scatter_add(tgt, idx, src, axis=0):
    return tgt.at[idx].add(src)

def _segment_sum(src, seg, n):
    return jax.ops.segment_sum(src, seg, n)
kernel_name = 'mk_decoder_preln_d1_seqx_r4_77ebc2'

def setup_inputs(seed: int=0):
    np.random.seed(seed)
    _w = jnp.asarray

    def _rec_inputs():
        import jax
        import jax.numpy as jnp
        _rk = jax.random.key(seed)
        x = -0.0003929 + 0.9999 * jax.random.normal(jax.random.fold_in(_rk, 1), (64, 256, 256), jnp.float32)
        _lenS = 256 - jax.random.randint(jax.random.fold_in(_rk, 7), (64,), 0, max(1, 256 // 4) + 1, jnp.int32)
        _lenS2 = 77 - jax.random.randint(jax.random.fold_in(_rk, 8), (64,), 0, max(1, 77 // 4) + 1, jnp.int32)
        _ctx_768P = jax.random.normal(jax.random.fold_in(_rk, 11), (64, 16, 192), jnp.float32)
        _ctx_768c = jax.random.dirichlet(jax.random.fold_in(_rk, 511), 0.3 * jnp.ones((16,), jnp.float32), (64, 77))
        _ctx_768t = jnp.einsum('bsk,bkd->bsd', _ctx_768c, _ctx_768P)
        _ctx_768t = _ctx_768t * jax.lax.rsqrt(jnp.mean(jnp.square(_ctx_768t)) + 1e-12) * 0.953939
        ctx_768 = 0.00095986 + 0.999812 * (_ctx_768t + 0.3 * jax.random.normal(jax.random.fold_in(_rk, 611), (64, 77, 192), jnp.float32))
        _validS = jnp.arange(256)[None, :] < _lenS[:, None]
        _validS2 = jnp.arange(77)[None, :] < _lenS2[:, None]
        _causal = jnp.tril(jnp.ones((256, 256), dtype=bool))
        mask_BxS2_bf1 = jnp.ones((64, 77), dtype=bool)
        return (x, ctx_768, mask_BxS2_bf1)
    x, ctx_768, mask_BxS2_bf1 = _rec_inputs()

    def _L0_attn_setup():
        import jax, jax.numpy as jnp
        import numpy as np
        HEADS = 16
        EPS = 1e-06
        key = jax.random.key(seed)
        k1, k2, k3, k4 = jax.random.split(key, 4)
        B, N, D = (4, 1024, 256)
        x = jax.random.normal(k1, (B, N, D), dtype=jnp.float32)
        Wqkv = jax.random.normal(k2, (D, 3 * D), dtype=jnp.float32) * D ** (-0.5)
        Wout = jax.random.normal(k3, (D, D), dtype=jnp.float32) * D ** (-0.5)
        bout = jax.random.normal(k4, (D,), dtype=jnp.float32) * 0.01
        return {'x': x, 'Wqkv': Wqkv, 'Wout': Wout, 'bout': bout}
    _L0_attn_all = _L0_attn_setup()
    _L0_attn_in = {k: v for k, v in _L0_attn_all.items() if k in ('Wqkv', 'Wout', 'bout')}
    del _L0_attn_all

    def _L0_xattn_setup():
        import jax, jax.numpy as jnp
        import numpy as np
        DIM = 256
        CTX_DIM = 192
        HEADS = 16
        key = jax.random.key(seed)
        ks = jax.random.split(key, 7)
        B, N, M = (4, 1024, 64)
        x = jax.random.normal(ks[0], (B, N, DIM), dtype=jnp.float32)
        context = jax.random.normal(ks[1], (B, M, CTX_DIM), dtype=jnp.float32)
        context_mask = jnp.ones((B, M), dtype=bool)
        s_d = 1.0 / np.sqrt(DIM)
        s_c = 1.0 / np.sqrt(CTX_DIM)
        Wq = jax.random.normal(ks[2], (DIM, DIM), dtype=jnp.float32) * s_d
        Wk = jax.random.normal(ks[3], (CTX_DIM, DIM), dtype=jnp.float32) * s_c
        Wv = jax.random.normal(ks[4], (CTX_DIM, DIM), dtype=jnp.float32) * s_c
        Wo = jax.random.normal(ks[5], (DIM, DIM), dtype=jnp.float32) * s_d
        return {'x': x, 'context': context, 'context_mask': context_mask, 'Wq': Wq, 'Wk': Wk, 'Wv': Wv, 'Wo': Wo}
    _L0_xattn_all = _L0_xattn_setup()
    _L0_xattn_in = {k: v for k, v in _L0_xattn_all.items() if k in ('Wq', 'Wk', 'Wv', 'Wo')}
    del _L0_xattn_all

    def _L0_ffn_setup():
        import jax, jax.numpy as jnp
        import numpy as np
        BLOCK = 32
        W_BITS = 4
        ACT_BITS = 16

        def act_qdq(x):
            qmax = 2.0 ** (ACT_BITS - 1) - 1.0
            scale = jnp.maximum(jnp.max(jnp.abs(x)) / qmax, 1e-12)
            return jnp.clip(jnp.round(x / scale), -qmax - 1.0, qmax) * scale

        def fixed_qdq_u16(x):
            scale = 1.0 / 65536.0
            return jnp.clip(jnp.round(x / scale), 0.0, 65535.0) * scale

        def lpbq_dequant(w):
            O, I = w.shape
            qmax = 2.0 ** (W_BITS - 1) - 1.0
            wb = w.reshape(O, I // BLOCK, BLOCK)
            s = jnp.maximum(jnp.max(jnp.abs(wb), axis=-1, keepdims=True) / qmax, 1e-12)
            wq = jnp.clip(jnp.round(wb / s), -qmax - 1.0, qmax) * s
            return wq.reshape(O, I)
        key = jax.random.key(seed)
        k1, k2, k3, k4 = jax.random.split(key, 4)
        B, S, H, I = (2, 1024, 256, 768)
        x = jax.random.normal(k1, (B, S, H), jnp.float32)
        w_gate = jax.random.normal(k2, (I, H), jnp.float32) * 0.02
        w_up = jax.random.normal(k3, (I, H), jnp.float32) * 0.02
        w_down = jax.random.normal(k4, (H, I), jnp.float32) * 0.02
        return {'x': x, 'w_gate': w_gate, 'w_up': w_up, 'w_down': w_down}
    _L0_ffn_all = _L0_ffn_setup()
    _L0_ffn_in = {k: v for k, v in _L0_ffn_all.items() if k in ('w_gate', 'w_up', 'w_down')}
    del _L0_ffn_all
    return {'x': x, 'ctx_768': ctx_768, 'mask_BxS2_bf1': mask_BxS2_bf1, 'L0_attn_Wqkv': _L0_attn_in['Wqkv'], 'L0_attn_Wout': _L0_attn_in['Wout'], 'L0_attn_bout': _L0_attn_in['bout'], 'L0_xattn_Wq': _L0_xattn_in['Wq'], 'L0_xattn_Wk': _L0_xattn_in['Wk'], 'L0_xattn_Wv': _L0_xattn_in['Wv'], 'L0_xattn_Wo': _L0_xattn_in['Wo'], 'L0_ffn_w_gate': _L0_ffn_in['w_gate'], 'L0_ffn_w_up': _L0_ffn_in['w_up'], 'L0_ffn_w_down': _L0_ffn_in['w_down']}

def reference(x, ctx_768, mask_BxS2_bf1, L0_attn_Wqkv, L0_attn_Wout, L0_attn_bout, L0_xattn_Wq, L0_xattn_Wk, L0_xattn_Wv, L0_xattn_Wo, L0_ffn_w_gate, L0_ffn_w_up, L0_ffn_w_down):
    import jax
    import jax.numpy as jnp

    def _L0_attn_ref(x, Wqkv, Wout, bout):
        import jax, jax.numpy as jnp
        import numpy as np
        HEADS = 16
        EPS = 1e-06
        B, N, D = x.shape
        H = HEADS
        d = D // H
        qkv = x @ Wqkv
        q, k, v = jnp.split(qkv, 3, axis=-1)
        q = q.reshape(B, N, H, d).transpose(0, 2, 1, 3)
        k = k.reshape(B, N, H, d).transpose(0, 2, 1, 3)
        v = v.reshape(B, N, H, d).transpose(0, 2, 1, 3)
        q = jax.nn.relu(q)
        k = jax.nn.relu(k)
        k_sum = k.sum(axis=2) + EPS
        z = 1.0 / (jnp.einsum('bhnd,bhd->bhn', q, k_sum) + EPS)
        kv = jnp.einsum('bhnd,bhnc->bhdc', k, v)
        out = jnp.einsum('bhnd,bhdc->bhnc', q, kv) * z[..., None]
        out = out.transpose(0, 2, 1, 3).reshape(B, N, D)
        return out @ Wout + bout

    def _L0_xattn_ref(x, context, context_mask, Wq, Wk, Wv, Wo):
        import jax, jax.numpy as jnp
        import numpy as np
        DIM = 256
        CTX_DIM = 192
        HEADS = 16
        B, N, _ = x.shape
        M = context.shape[1]
        hd = DIM // HEADS
        scale = hd ** (-0.5)
        q = (x @ Wq).reshape(B, N, HEADS, hd).transpose(0, 2, 1, 3)
        k = (context @ Wk).reshape(B, M, HEADS, hd).transpose(0, 2, 1, 3)
        v = (context @ Wv).reshape(B, M, HEADS, hd).transpose(0, 2, 1, 3)
        scores = jnp.einsum('bhid,bhjd->bhij', q, k) * scale
        max_neg = -jnp.finfo(scores.dtype).max
        scores = jnp.where(context_mask[:, None, None, :], scores, max_neg)
        attn = jax.nn.softmax(scores, axis=-1)
        out = jnp.einsum('bhij,bhjd->bhid', attn, v)
        out = out.transpose(0, 2, 1, 3).reshape(B, N, DIM)
        return out @ Wo

    def _L0_ffn_ref(x, w_gate, w_up, w_down):
        import jax, jax.numpy as jnp
        import numpy as np
        BLOCK = 32
        W_BITS = 4
        ACT_BITS = 16

        def act_qdq(x):
            qmax = 2.0 ** (ACT_BITS - 1) - 1.0
            scale = jnp.maximum(jnp.max(jnp.abs(x)) / qmax, 1e-12)
            return jnp.clip(jnp.round(x / scale), -qmax - 1.0, qmax) * scale

        def fixed_qdq_u16(x):
            scale = 1.0 / 65536.0
            return jnp.clip(jnp.round(x / scale), 0.0, 65535.0) * scale

        def lpbq_dequant(w):
            O, I = w.shape
            qmax = 2.0 ** (W_BITS - 1) - 1.0
            wb = w.reshape(O, I // BLOCK, BLOCK)
            s = jnp.maximum(jnp.max(jnp.abs(wb), axis=-1, keepdims=True) / qmax, 1e-12)
            wq = jnp.clip(jnp.round(wb / s), -qmax - 1.0, qmax) * s
            return wq.reshape(O, I)
        x = act_qdq(x)
        up = act_qdq(x @ lpbq_dequant(w_up).T)
        gate = act_qdq(x @ lpbq_dequant(w_gate).T)
        sig = fixed_qdq_u16(jax.nn.sigmoid(gate))
        gate = act_qdq(gate * sig)
        o = act_qdq(gate * up)
        return o @ lpbq_dequant(w_down).T
    x = x + _L0_attn_ref(_layernorm(x, axis=-1), L0_attn_Wqkv, L0_attn_Wout, L0_attn_bout)
    x = x + _L0_xattn_ref(_layernorm(x, axis=-1), ctx_768, mask_BxS2_bf1, L0_xattn_Wq, L0_xattn_Wk, L0_xattn_Wv, L0_xattn_Wo)
    x = x + _L0_ffn_ref(_layernorm(x, axis=-1), L0_ffn_w_gate, L0_ffn_w_up, L0_ffn_w_down)
    return x

_drawn_inputs = setup_inputs


def setup_inputs(seed=0):
    import zlib

    import numpy as np

    out = dict(_drawn_inputs(seed))
    spreads = {}
    factors = {'L0_attn_bout': 6.877}
    for name, (base, spread) in spreads.items():
        noise = np.random.default_rng([zlib.crc32(name.encode()), seed]).standard_normal(out[name].shape)
        drawn = base * np.exp(spread * noise) if base else spread * noise
        out[name] = jnp.asarray(drawn.astype(out[name].dtype))
    for name, factor in factors.items():
        out[name] = (out[name] * factor).astype(out[name].dtype)
    return out
```

```python
from contextlib import ExitStack

import concourse.bass as bass
from concourse import mybir

F32 = mybir.dt.float32
BF16 = mybir.dt.bfloat16
F16 = mybir.dt.float16
I16 = mybir.dt.int16
U16 = mybir.dt.uint16
U8 = mybir.dt.uint8
ALU = mybir.AluOpType
ACT = mybir.ActivationFunctionType
AX = mybir.AxisListType
RMAX = bass.bass_isa.ReduceOp.max

P = 128
H = 16
HG = 8
HD = 16
LN_EPS = 1e-5
ATT_EPS = 1e-6
BLOCK = 32
ROUND = 12582912.0
QMAX16 = 32767.0
SMALLEST = 1e-12
MASKED = -(2.0 ** 127)
WTOP = 4096.0
CH = 512


def chunk_slots(J):
    out, at = [], 0
    while at < HG * J:
        rows = min(P, HG * J - at)
        first, last = at // J, (at + rows - 1) // J
        out.append((rows, first, last - first + 1))
        at += rows
    return out


def decoder_layer(nc, x, ctx, mask, wqkv, wout, bout, wq, wk, wv, wo, wgate, wup, wdown, out):
    NB, N, D = x.shape
    J, C = ctx.shape[1], ctx.shape[2]
    F = wgate.shape[0]
    T = NB * N
    NT = N // P
    KC = D // P
    FT = F // P
    NCH = T // CH
    HJ = HG * J
    SLOTS = chunk_slots(J)
    NC = len(SLOTS)
    NSLOT = sum(n for _, _, n in SLOTS)
    assert NT == 2 and KC == 2 and D == H * HD and J <= P and C <= 2 * P and NB % 2 == 0 and NB >= 8

    x2_d = nc.dram_tensor("x2_scratch", (NB, P, NT * D), F32).ap()
    xn_d = nc.dram_tensor("xn_scratch", (NB, P, KC, N), F32).ap()
    g_d = nc.dram_tensor("gate_scratch", (NCH, P, FT * CH), F32).ap()
    p_d = nc.dram_tensor("product_scratch", (NCH * FT // 2, P, 2 * CH), F32).ap()
    mrow_d = nc.dram_tensor("maskrow_scratch", (NB, HJ), BF16).ap()

    top = ExitStack()
    with top:
        def sb_in(stack):
            return lambda name, shape, dt: stack.enter_context(nc.sbuf_tensor(name, shape, dt))

        def sem_in(stack):
            return lambda name: stack.enter_context(nc.semaphore(name))

        keep = sb_in(top)
        ps = top.enter_context(nc.psum_tensor("ps", [P, 8, 512], F32))
        wh = keep("wh", [P, 3, FT * D], F16)
        wl = keep("wl", [P, 3, FT * D], F16)
        wscale = keep("wscale", [P, 3], F32)
        xmax = keep("xmax", [P, NB], F32)

        attention_phase(nc, ps, wh, wl, wscale, xmax, x2_d, xn_d, mrow_d, x, ctx, mask, wqkv, wout, bout,
                        wq, wk, wv, wo, wgate, wup, wdown, sb_in, sem_in)
        feed_forward_phases(nc, top, ps, wh, wl, wscale, xmax, x2_d, xn_d, g_d, p_d, out, NB, NCH, FT, sb_in, sem_in)


def attention_phase(nc, ps, wh, wl, wscale, xmax, x2_d, xn_d, mrow_d, x, ctx, mask, wqkv, wout, bout,
                    wq, wk, wv, wo, wgate, wup, wdown, sb_in, sem_in):
    NB, N, D = x.shape
    J, C = ctx.shape[1], ctx.shape[2]
    F = wgate.shape[0]
    NT, KC, FT = N // P, D // P, F // P
    HJ = HG * J
    SLOTS = chunk_slots(J)
    NC = len(SLOTS)
    OFF = [sum(n for _, _, n in SLOTS[:c]) for c in range(NC + 1)]
    NSLOT = OFF[NC]
    HJP = NC * P
    WB = FT * D // BLOCK
    NG = P + HG
    B1 = 6 if J * 6 <= 512 else 512 // J
    assert B1 == 6 and NC == 5
    stack = ExitStack()
    with stack:
        sb, sem = sb_in(stack), sem_in(stack)
        ident = sb("ident", [P, P], F32)
        identb = sb("identb", [P, P], BF16)
        HM = sb("HM", [P, HG], F32)
        BM = sb("BM", [P, P], F32)
        HRM = sb("HRM", [P, 2 * NSLOT], F32)
        Sel = sb("Sel", [J, HJP], F32)
        maskrow1 = sb("maskrow1", [P, P], BF16)
        wq1 = sb("wq1", [P, KC, 3 * D], F32)
        wo1 = sb("wo1", [P, KC, D], F32)
        wq2 = sb("wq2", [P, KC, D], F32)
        wk2 = sb("wk2", [P, 2, D], F32)
        wv2 = sb("wv2", [P, 2, D], F32)
        wo2 = sb("wo2", [P, KC, D], F32)
        bias = sb("bias", [P, D], F32)
        msk8 = sb("msk8", [P, NB, J], U8)
        mk = sb("mk", [NB, J], U8)
        mkf = sb("mkf", [NB, J], F32)
        mkr = sb("mkr", [NB, HG, J], BF16)
        W3 = sb("W3", [P, 3, FT * D], F32)
        am = sb("am", [P, 3 * WB], F32)
        s3 = sb("s3", [P, 3 * WB], F32)
        rs3 = sb("rs3", [P, 3 * WB], F32)
        sm = sb("sm", [P, 3], F32)
        smx = sb("smx", [P, 3], F32)
        rsm = sb("rsm", [P, 3], F32)
        mhalf = sb("mhalf", [P, NT], F32)
        epst = sb("epst", [P, NT], F32)
        fence = sb("fence", [P, 3], F32)

        xin = [sb(f"xin{i}", [P, NT, D], F32) for i in range(2)]
        ctxin = [sb(f"ctxin{i}", [J, 2 * P], F32) for i in range(2)]
        aug = [sb(f"aug{i}", [P, 2, HJ], BF16) for i in range(2)]
        st = [sb(f"st{i}", [P, NT, 6], F32) for i in range(3)]
        mv = [sb(f"mv{i}", [P, NT, 2], F32) for i in range(3)]
        ve = [sb(f"ve{i}", [P, NT], F32) for i in range(3)]
        rstd = [sb(f"rstd{i}", [P, NT], F32) for i in range(3)]
        xn1 = sb("xn1", [P, NT, D], F32)
        xn2 = sb("xn2", [P, NT, D], F32)
        xn3 = sb("xn3", [P, NT, D], F32)
        xn1T = sb("xn1T", [P, KC, N], F32)
        xn2T = sb("xn2T", [P, KC, N], F32)
        xn3T = sb("xn3T", [P, KC, N], F32)
        qT = sb("qT", [P, KC, N], F32)
        ktok = sb("ktok", [P, NT, D], F32)
        vtok = sb("vtok", [P, NT, 2, P + 1], F32)
        kvbd = sb("kvbd", [P, 2, NG], F32)
        dz = sb("dz", [P, NT, H], F32)
        zz = sb("zz", [P, NT, H], F32)
        otok = sb("otok", [P, NT, D], F32)
        oT = sb("oT", [P, KC, N], F32)
        xb = sb("xb", [P, NT, D], F32)
        x1 = [sb(f"x1_{i}", [P, NT, D], F32) for i in range(2)]
        ctxT = sb("ctxT", [P, 2, J], F32)
        kTm = sb("kTm", [P, 2, J], F32)
        vsb = sb("vsb", [J, D], F32)
        KBD = [sb(f"KBD{i}", [P, 2, HJ], F32) for i in range(2)]
        KBDb = [sb(f"KBDb{i}", [P, 2, HJ], BF16) for i in range(2)]
        Vbd = sb("Vbd", [P, 2 * NSLOT, HD + 1], F32)
        q2T = sb("q2T", [P, KC, N], F32)
        q2Tb = sb("q2Tb", [P, KC, N], BF16)
        mtile = sb("mtile", [P, NT, P], BF16)
        mrow = sb("mrow", [P, N], BF16)
        expT = sb("expT", [P, NC, 2, N], F32)
        rden = sb("rden", [P, NT, H], F32)
        o2 = sb("o2", [P, NT, D], F32)
        o2T = sb("o2T", [P, KC, N], F32)
        x2 = [sb(f"x2_{i}", [P, NT, D], F32) for i in range(2)]

        ld_w = sem("ld_w")
        ld_w3 = sem("ld_w3")
        ld_m = sem("ld_m")
        g_c = sem("g_c")
        v_c = sem("v_c")
        g_smx = sem("g_smx")
        p_wT = sem("p_wT")
        a_wh = sem("a_wh")
        v_wl = sem("v_wl")
        st_m = sem("st_m")
        ld_x, ld_ctx, ld_mrow = ([sem(f"{n}{i}") for i in range(2)] for n in ("ld_x", "ld_ctx", "ld_mrow"))
        st_x2, st_xn = [sem(f"st_x2{i}") for i in range(2)], sem("st_xn")
        v_st = [sem(f"v_st{i}") for i in range(3)]
        v_ag = [sem(f"v_ag{i}") for i in range(3)]
        g_ve = [sem(f"g_ve{i}") for i in range(3)]
        g_rs = [sem(f"g_rs{i}") for i in range(3)]
        v_xn = [sem(f"v_xn{i}") for i in range(3)]
        p_xn = [sem(f"p_xn{i}") for i in range(3)]
        a_xn = [sem(f"a_xn{i}") for i in range(3)]
        p_q, a_q = sem("p_q"), sem("a_q")
        p_kv, a_kv, v_kv = sem("p_kv"), sem("a_kv"), sem("v_kv")
        p_agg, v_bd = sem("p_agg"), sem("v_bd")
        p_num, v_dz, v_z, v_o = sem("p_num"), sem("v_dz"), sem("v_z"), sem("v_o")
        p_oT, a_oT = sem("p_oT"), sem("a_oT")
        p_att, g_xb, v_x1 = sem("p_att"), sem("g_xb"), sem("v_x1")
        p_cT, a_cT = sem("p_cT"), sem("a_cT")
        p_ckv, v_kT, v_v, g_kbd = sem("p_ckv"), sem("v_kT"), sem("v_v"), sem("g_kbd")
        p_vr, v_vbd = sem("p_vr"), sem("v_vbd")
        p_q2, a_q2, v_q2b = sem("p_q2"), sem("a_q2"), sem("v_q2b")
        p_s, v_max = sem("p_s"), sem("v_max")
        p_m, a_m = sem("p_m"), sem("a_m")
        p_sT, a_e = sem("p_sT"), sem("a_e")
        p_av, v_rd, v_o2 = sem("p_av"), sem("v_rd"), sem("v_o2")
        p_o2T, a_o2T = sem("p_o2T"), sem("a_o2T")
        p_out, v_x2 = sem("p_out"), sem("v_x2")
        v_xm = sem("v_xm")

        block = stack.enter_context(nc.Block())

        def ge(eng, s, value):
            if isinstance(value, int) and value <= 0:
                return
            eng.wait_ge(s, value)

        def bodies(eng, body):
            body(-1, 1, -1)
            body(0, 0, 0)
            body(1, 1, 0)
            with eng.Fori(1, NB // 2 - 1) as i:
                body(i * 2, 0, i)
                body(i * 2 + 1, 1, i)
            body(NB - 2, 0, NB // 2 - 1)
            body(NB - 1, 1, NB // 2 - 1)

        def nth(h, par, ahead):
            return h + (par + ahead) // 2 + 1

        def has_s(b):
            return not isinstance(b, int) or b + 1 < NB

        def has_t(b):
            return not isinstance(b, int) or b >= 0

        def has_next(b):
            return not isinstance(b, int) or b + 2 < NB

        def has_prev(b):
            return not isinstance(b, int) or b >= 1

        @block.sync
        def _(sp):
            sp.dma_start(mk[:], mask).then_inc(ld_m, 16)
            sp.dma_start(msk8[:], bass.AP(tensor=mask.tensor, offset=mask.offset, ap=[[0, P], [J, NB], [1, J]])).then_inc(ld_m, 16)

            def load_x(b, par):
                ge(sp, g_xb, b - 1)
                ge(sp, v_xn[0], b - 1)
                sp.dma_start(xin[par][:], x[b].rearrange("(p t) d -> p t d", t=NT)).then_inc(ld_x[par], 16)

            def load_ctx(b, par):
                ge(sp, p_cT, b - 1)
                if isinstance(b, int) and b < 2:
                    sp.wait_ge(g_c, 11)
                sp.dma_start(ctxin[par][:, 0:C], ctx[b]).then_inc(ld_ctx[par], 16)
                ge(sp, p_sT, NC * (b - 1))
                for g in range(2):
                    sp.dma_start(aug[par][32:33, g, :], mrow_d[b:b + 1, :] if isinstance(b, int) else mrow_d[bass.ds(b, 1), :]).then_inc(ld_mrow[par], 16)

            load_x(0, 0)
            load_x(1, 1)
            for k in range(KC):
                sp.dma_start(wq1[:, k, :], wqkv[k * P:(k + 1) * P, :]).then_inc(ld_w, 16)
            sp.dma_start(wo1[:], wout.rearrange("(k p) n -> p k n", p=P)).then_inc(ld_w, 16)
            sp.dma_start(wq2[:], wq.rearrange("(k p) n -> p k n", p=P)).then_inc(ld_w, 16)
            sp.dma_start(wo2[:], wo.rearrange("(k p) n -> p k n", p=P)).then_inc(ld_w, 16)
            sp.wait_ge(g_c, 1)
            for w2, w in ((wk2, wk), (wv2, wv)):
                sp.dma_start(w2[:, 0, :], w[0:P, :]).then_inc(ld_w, 16)
                sp.dma_start(w2[0:C - P, 1, :], w[P:C, :]).then_inc(ld_w, 16)
            sp.dma_start(bias[:], bass.AP(tensor=bout.tensor, offset=bout.offset, ap=[[0, P], [1, D]])).then_inc(ld_w, 16)
            sp.dma_start(W3[:, 0, :].rearrange("p (m i) -> p m i", m=FT), wgate.rearrange("(m p) i -> p m i", p=P)).then_inc(ld_w3, 16)
            sp.dma_start(W3[:, 1, :].rearrange("p (m i) -> p m i", m=FT), wup.rearrange("(m p) i -> p m i", p=P)).then_inc(ld_w3, 16)
            sp.dma_start(W3[:, 2, :].rearrange("p (m i) -> p m i", m=KC), wdown.rearrange("(m p) i -> p m i", p=P)).then_inc(ld_w3, 16)
            sp.wait_ge(v_c, 2)
            sp.dma_start(mrow_d, mkr[:]).then_inc(st_m, 16)
            sp.wait_ge(st_m, 16)
            load_ctx(0, 0)

            def store_xn(b, par):
                sp.wait_ge(a_xn[2], b + 1)
                for k in range(KC):
                    sp.dma_start(xn_d[b][:, k, :], xn3T[:, k, :]).then_inc(st_xn, 16)

            def body(b, par, h):
                if has_next(b) and not (isinstance(b, int) and b < 0):
                    load_x(b + 2, par)
                if has_t(b) and has_s(b):
                    load_ctx(b + 1, 1 - par)
                if has_prev(b):
                    store_xn(b - 1, 1 - par)
                if has_t(b):
                    sp.wait_ge(v_x2, b + 1)
                    sp.dma_start(x2_d[b], x2[par][:].rearrange("p t d -> p (t d)")).then_inc(st_x2[par], 16)

            bodies(sp, body)
            store_xn(NB - 1, 1)
            for i in range(2):
                sp.wait_ge(st_x2[i], 16 * NB // 2)
            sp.wait_ge(st_xn, 16 * KC * NB)

        @block.gpsimd
        def _(gp):
            pool = nc.gpsimd
            pool.memset(wk2[:, 1, :], 0.0)
            pool.memset(wv2[:, 1, :], 0.0).then_inc(g_c, 1)
            pool.memset(ident[:], 0.0)
            pool.memset(identb[:], 0.0)
            pool.memset(HM[:], 1.0)
            pool.memset(HRM[:], 1.0)
            pool.memset(Sel[:], 0.0)
            pool.memset(aug[0][:], 0.0)
            pool.memset(aug[1][:], 0.0)
            pool.memset(maskrow1[:], 0.0)
            pool.memset(mtile[:], 0.0)
            pool.memset(mhalf[:], -0.5)
            pool.memset(epst[:], LN_EPS)
            pool.memset(vtok[:, :, :, P:P + 1], 1.0)
            for i in range(2):
                pool.memset(ctxin[i][:], 0.0)
            pool.memset(Vbd[:], 0.0).then_inc(g_c, 1)
            gp.wait_ge(g_c, 2)
            pool.affine_select(out=ident[:], in_=ident[:], compare_op=ALU.not_equal, fill=1.0, base=0,
                               pattern=[[-1, P]], channel_multiplier=1)
            pool.affine_select(out=identb[:], in_=identb[:], compare_op=ALU.not_equal, fill=1.0, base=0,
                               pattern=[[-1, P]], channel_multiplier=1)
            pool.affine_select(out=maskrow1[:], in_=maskrow1[:], compare_op=ALU.not_equal, fill=1.0, base=-32,
                               pattern=[[0, P]], channel_multiplier=1)
            pool.memset(mtile[:, :, 32:33], 1.0)
            for i in range(2):
                v = aug[i][:].rearrange("p g (h j) -> p g h j", h=HG)
                for g in range(2):
                    pool.affine_select(out=v[:, g], in_=v[:, g], compare_op=ALU.not_equal, fill=-1.0, base=-HG * g,
                                       pattern=[[-1, HG], [0, J]], channel_multiplier=1)
            pool.affine_select(out=HM[:], in_=HM[:], compare_op=ALU.is_ge, fill=0.0, base=0,
                               pattern=[[-HD, HG]], channel_multiplier=1).then_inc(g_c, 1)
            gp.wait_ge(g_c, 3)
            pool.affine_select(out=HM[:], in_=HM[:], compare_op=ALU.is_ge, fill=0.0, base=HD - 1,
                               pattern=[[HD, HG]], channel_multiplier=-1)
            for step in range(2):
                for c, (rows, h0, ns) in enumerate(SLOTS):
                    for g in range(2):
                        v = HRM[:, 2 * OFF[c] + g * ns:2 * OFF[c] + (g + 1) * ns]
                        if step == 0:
                            last = pool.affine_select(out=v, in_=v, compare_op=ALU.is_ge, fill=0.0, base=c * P - J * h0,
                                                      pattern=[[-J, ns]], channel_multiplier=1)
                        else:
                            last = pool.affine_select(out=v, in_=v, compare_op=ALU.is_ge, fill=0.0,
                                                      base=J * h0 + J - 1 - c * P, pattern=[[J, ns]],
                                                      channel_multiplier=-1)
                last.then_inc(g_c, 1)
                gp.wait_ge(g_c, 4 + step)
            pool.tensor_copy(Vbd[:, :, HD:HD + 1], HRM[:, :, None])
            pool.tensor_copy(BM[:].rearrange("p (h i) -> p h i", h=HG), HM[:, :, None].broadcast_to([P, HG, HD])).then_inc(g_c, 1)
            gp.wait_ge(g_c, 6)
            for h in range(HG):
                v = Sel[:, h * J:(h + 1) * J]
                last = pool.affine_select(out=v, in_=v, compare_op=ALU.not_equal, fill=1.0, base=0,
                                          pattern=[[-1, J]], channel_multiplier=1)
            last.then_inc(g_c, 5)
            gp.wait_ge(v_c, 5)
            pool.partition_all_reduce(smx[:], sm[:], P, RMAX).then_inc(g_smx, 1)

            def ln_scale(i, b):
                gp.wait_ge(v_ag[i], b + 1)
                pool.tensor_tensor(ve[i][:], mv[i][:, :, 1], epst[:], ALU.add).then_inc(g_ve[i], 1)
                gp.wait_ge(g_ve[i], b + 1)
                ge(gp, v_xn[i], b)
                pool.tensor_tensor(rstd[i][:], ve[i][:], mhalf[:], ALU.pow).then_inc(g_rs[i], 1)

            def add_bias(b, par, use):
                gp.wait_ge(ld_x[par], 16 * use)
                ge(gp, v_x1, b)
                pool.tensor_tensor(xb[:], xin[par][:], bias[:, None, :].broadcast_to([P, NT, D]), ALU.add).then_inc(g_xb, 1)

            def keys(b, par):
                gp.wait_ge(v_kT, b + 1)
                ge(gp, p_sT, NC * (b - 1))
                kb = kTm[:, :, None, :].broadcast_to([P, 2, HG, J])
                hb = HM[:, None, :, None].broadcast_to([P, 2, HG, J])
                pool.tensor_tensor(KBD[par][:].rearrange("p g (h j) -> p g h j", h=HG), kb, hb, ALU.mult)
                pool.tensor_tensor(KBDb[par][:].rearrange("p g (h j) -> p g h j", h=HG), kb, hb, ALU.mult).then_inc(g_kbd, 1)

            ln_scale(0, 0)
            gp.wait_ge(ld_w, 16 * 10)

            def body(b, par, h):
                if has_t(b):
                    keys(b, par)
                if has_s(b):
                    add_bias(b + 1, 1 - par, nth(h, par, 1))
                if has_s(b):
                    ln_scale(1, b + 1)
                if has_next(b):
                    ln_scale(0, b + 2)
                if has_t(b):
                    ln_scale(2, b)

            bodies(gp, body)

        @block.vector
        def _(dve):
            vec = nc.vector
            dve.wait_ge(ld_m, 32)
            vec.tensor_scalar(mkf[:], mk[:], -1.0, -MASKED, ALU.add, ALU.mult).then_inc(v_c, 1)
            dve.wait_ge(v_c, 1)
            vec.tensor_copy(mkr[:], mkf[:, None, :].broadcast_to([NB, HG, J])).then_inc(v_c, 1)

            def stats(i, b, src):
                ge(dve, v_xn[i], b)
                for t in range(NT):
                    last = vec.bn_stats(st[i][:, t, :], src[:, t, :])
                last.then_inc(v_st[i], 1)

            def aggregate(i, b):
                dve.wait_ge(v_st[i], b + 1)
                vec.tensor_copy(fence[:, i:i + 1], mhalf[:, 0:1])
                for t in range(NT):
                    last = vec.bn_aggr(mv[i][:, t, :], st[i][:, t, :])
                last.then_inc(v_ag[i], 1)

            def normalise(i, b, src, dst):
                dve.wait_ge(g_rs[i], b + 1)
                ge(dve, p_xn[i], b)
                for t in range(NT):
                    last = vec.tensor_scalar(dst[:, t, :], src[:, t, :], mv[i][:, t, 0:1], rstd[i][:, t:t + 1],
                                             ALU.subtract, ALU.mult)
                last.then_inc(v_xn[i], 1)

            dve.wait_ge(g_c, 2)
            dve.wait_ge(ld_x[0], 16)
            stats(0, 0, xin[0])
            aggregate(0, 0)
            dve.wait_ge(ld_w3, 48)
            vec.tensor_reduce(am[:], W3[:].rearrange("p w (n k) -> p (w n) k", k=BLOCK), AX.X, ALU.max,
                              apply_absolute_value=True).then_inc(v_c, 1)
            dve.wait_ge(v_c, 3)
            vec.tensor_scalar(s3[:], am[:], 1.0 / 7.0, SMALLEST, ALU.mult, ALU.max).then_inc(v_c, 1)
            dve.wait_ge(v_c, 4)
            vec.tensor_reduce(sm[:], s3[:].rearrange("p (w n) -> p w n", w=3), AX.X, ALU.max).then_inc(v_c, 1)
            normalise(0, 0, xin[0], xn1)
            vec.reciprocal(rs3[:], s3[:]).then_inc(v_c, 1)
            dve.wait_ge(v_c, 6)
            w3 = W3[:].rearrange("p w (n k) -> p (w n) k", k=BLOCK)
            rb = rs3[:, :, None].broadcast_to([P, 3 * WB, BLOCK])
            vec.tensor_tensor(w3, w3, rb, ALU.mult).then_inc(v_c, 1)
            dve.wait_ge(v_c, 7)
            vec.tensor_scalar(W3[:], W3[:], ROUND, -ROUND, ALU.add, ALU.add).then_inc(v_c, 1)
            dve.wait_ge(v_c, 8)
            vec.tensor_scalar(W3[:], W3[:], 7.0, -8.0, ALU.min, ALU.max).then_inc(v_c, 1)
            dve.wait_ge(g_smx, 1)
            vec.reciprocal(rsm[:], smx[:]).then_inc(v_c, 1)
            dve.wait_ge(v_c, 10)
            vec.tensor_scalar(wscale[:], smx[:], 1.0 / WTOP, None, ALU.mult)
            for w in range(3):
                last = vec.tensor_scalar(s3[:, w * WB:(w + 1) * WB], s3[:, w * WB:(w + 1) * WB], rsm[:, w:w + 1], WTOP,
                                         ALU.mult, ALU.mult)
            last.then_inc(v_c, 1)
            dve.wait_ge(v_c, 11)
            vec.tensor_tensor(w3, w3, s3[:, :, None].broadcast_to([P, 3 * WB, BLOCK]), ALU.mult).then_inc(v_c, 1)
            for n in range(3 * 3):
                w, f = n // 3, n % 3
                dve.wait_ge(a_wh, n + 1)
                vec.tensor_tensor(wl[:, w, f * 512:(f + 1) * 512], ps[:, n % 8, :], wh[:, w, f * 512:(f + 1) * 512],
                                  ALU.subtract).then_inc(v_wl, 1)

            dve.wait_ge(g_c, 11)

            def body(b, par, h):
                s, t_ = has_s(b), has_t(b)
                if t_:
                    dve.wait_ge(p_ckv, b + 1)
                    ge(dve, g_kbd, b)
                    vec.tensor_tensor(kTm[:], ps[:, 4, 0:2 * J].rearrange("p (g j) -> p g j", g=2),
                                      (msk8[:, b:b + 1, :] if isinstance(b, int) else msk8[:, bass.ds(b, 1), :]).broadcast_to([P, 2, J]),
                                      ALU.mult).then_inc(v_kT, 1)
                    ge(dve, p_vr, b)
                    vec.tensor_copy(vsb[:], ps[0:J, 4, 256:512]).then_inc(v_v, 1)
                if s:
                    dve.wait_ge(p_kv, b + 2)
                    ge(dve, p_agg, b + 1)
                    vec.tensor_scalar(ktok[:, 1, :], ps[:, 2, 0:D], 0.0, None, ALU.max)
                    vec.tensor_copy(vtok[:, 1, :, 0:P], ps[:, 2, D:2 * D].rearrange("p (g c) -> p g c", g=2)).then_inc(v_kv, 1)
                if t_:
                    dve.wait_ge(p_vr, b + 1)
                    ge(dve, p_av, b)
                    vec.tensor_tensor(Vbd[:, :, 0:HD], ps[:, 3, 0:2 * NSLOT * HD].rearrange("p (s i) -> p s i", i=HD),
                                      HRM[:, :, None].broadcast_to([P, 2 * NSLOT, HD]), ALU.mult).then_inc(v_vbd, 1)
                if s:
                    dve.wait_ge(p_agg, b + 2)
                    ge(dve, p_num, b + 1)
                    a = ps[:, 1, 0:2 * (P + 1)].rearrange("p (g c) -> p g c", g=2)
                    vec.tensor_tensor(kvbd[:, :, 0:P], a[:, :, 0:P], BM[:, None, :].broadcast_to([P, 2, P]), ALU.mult)
                    vec.scalar_tensor_tensor(out=kvbd[:, :, P:NG], in0=a[:, :, P:P + 1].broadcast_to([P, 2, HG]),
                                             scalar=ATT_EPS, in1=HM[:, None, :].broadcast_to([P, 2, HG]),
                                             op0=ALU.add, op1=ALU.mult).then_inc(v_bd, 1)
                if t_:
                    dve.wait_ge(a_q2, b + 1)
                    ge(dve, p_s, 2 * b)
                    vec.tensor_copy(q2Tb[:], q2T[:]).then_inc(v_q2b, 1)

                def maxima(t):
                    dve.wait_ge(p_s, 2 * b + t + 1)
                    ge(dve, p_m, b)
                    vec.tensor_reduce(mtile[:, t, 0:2 * B1].rearrange("p (k h) -> p k h", k=2),
                                      ps[:, 5:7, 0:B1 * J].rearrange("p k (h j) -> p k h j", j=J), AX.X, ALU.max)
                    vec.tensor_reduce(mtile[:, t, 2 * B1:H], ps[:, 7, 0:(H - 2 * B1) * J].rearrange("p (h j) -> p h j", j=J),
                                      AX.X, ALU.max).then_inc(v_max, 1)

                if t_:
                    maxima(0)
                if s:
                    dve.wait_ge(p_num, b + 2)
                    ge(dve, v_o, b + 1)
                    vec.tensor_scalar(dz[:].rearrange("p t (g h) -> p t g h", g=2),
                                      ps[:, 0:3:2, 0:2 * NG].rearrange("p t (g c) -> p t g c", g=2)[:, :, :, P:NG],
                                      ATT_EPS, None, ALU.add).then_inc(v_dz, 1)
                    dve.wait_ge(v_dz, b + 2)
                    vec.reciprocal(zz[:], dz[:]).then_inc(v_z, 1)
                    dve.wait_ge(v_z, b + 2)
                    ge(dve, p_oT, b + 1)
                    for t in range(NT):
                        last = vec.tensor_tensor(
                            otok[:, t, :].rearrange("p (g h i) -> p g h i", g=2, h=HG),
                            ps[:, 2 * t, 0:2 * NG].rearrange("p (g c) -> p g c", g=2)[:, :, 0:P].rearrange("p g (h i) -> p g h i", h=HG),
                            zz[:, t, :].rearrange("p (g h) -> p g h", g=2)[:, :, :, None].broadcast_to([P, 2, HG, HD]), ALU.mult)
                    last.then_inc(v_o, 1)
                if t_:
                    maxima(1)
                    dve.wait_ge(p_av, b + 1)
                    av = ps[:, 6:8, 0:H * (HD + 1)].rearrange("p t (h i) -> p t h i", i=HD + 1)
                    ge(dve, v_o2, b)
                    vec.reciprocal(rden[:], av[:, :, :, HD]).then_inc(v_rd, 1)
                    dve.wait_ge(v_rd, b + 1)
                    ge(dve, p_o2T, b)
                    vec.tensor_tensor(o2[:].rearrange("p t (h i) -> p t h i", h=H), av[:, :, :, 0:HD],
                                      rden[:, :, :, None].broadcast_to([P, NT, H, HD]), ALU.mult).then_inc(v_o2, 1)
                if s:
                    dve.wait_ge(p_att, b + 2)
                    dve.wait_ge(g_xb, b + 2)
                    vec.tensor_tensor(x1[1 - par][:], ps[:, 0, :].rearrange("p (t d) -> p t d", t=NT), xb[:], ALU.add).then_inc(v_x1, 1)
                    dve.wait_ge(v_x1, b + 2)
                    stats(1, b + 1, x1[1 - par])
                if has_next(b):
                    dve.wait_ge(ld_x[par], 16 * nth(h, par, 2))
                    stats(0, b + 2, xin[par])
                if s:
                    aggregate(1, b + 1)
                if has_next(b):
                    aggregate(0, b + 2)
                if t_:
                    dve.wait_ge(p_out, b + 1)
                    ge(dve, st_x2[par], 16 * (nth(h, par, 0) - 1))
                    vec.tensor_tensor(x2[par][:], ps[:, 4, :].rearrange("p (t d) -> p t d", t=NT), x1[par][:], ALU.add).then_inc(v_x2, 1)
                    dve.wait_ge(v_x2, b + 1)
                    stats(2, b, x2[par])
                    aggregate(2, b)
                if s:
                    normalise(1, b + 1, x1[1 - par], xn2)
                if has_next(b):
                    normalise(0, b + 2, xin[par], xn1)
                if t_:
                    normalise(2, b, x2[par], xn3)
                    dve.wait_ge(v_xn[2], b + 1)
                    vec.tensor_reduce(xmax[:, b:b + 1] if isinstance(b, int) else xmax[:, bass.ds(b, 1)], xn3[:], AX.XY, ALU.max,
                                      apply_absolute_value=True).then_inc(v_xm, 1)

            bodies(dve, body)

        @block.scalar
        def _(act):
            sc = nc.scalar
            for n in range(3 * 3):
                w, f = n // 3, n % 3
                act.wait_ge(p_wT, n + 1)
                sc.activation(wh[:, w, f * 512:(f + 1) * 512], ps[:, n % 8, :], ACT.Copy).then_inc(a_wh, 1)

            def copy_xn(i, b, bank, dst):
                act.wait_ge(p_xn[i], b + 1)
                sc.activation(dst[:].rearrange("p k n -> p (k n)"), ps[:, bank, :], ACT.Copy).then_inc(a_xn[i], 1)

            def body(b, par, h):
                s, t_ = has_s(b), has_t(b)
                if s:
                    ge(act, p_kv, b + 1)
                    copy_xn(0, b + 1, 0, xn1T)
                if has_prev(b):
                    ge(act, st_xn, 16 * KC * (b - 1))
                    copy_xn(2, b - 1, 3, xn3T)
                if t_:
                    act.wait_ge(p_cT, b + 1)
                    ge(act, p_ckv, b)
                    sc.activation(ctxT[:].rearrange("p k j -> p (k j)"), ps[:, 3, 0:2 * J], ACT.Copy).then_inc(a_cT, 1)
                if s:
                    act.wait_ge(p_q, b + 2)
                    ge(act, p_num, b + 1)
                    sc.activation(qT[:].rearrange("p k n -> p (k n)"), ps[:, 1, :], ACT.Relu).then_inc(a_q, 1)
                    act.wait_ge(p_kv, b + 2)
                    ge(act, p_agg, b + 1)
                    sc.activation(ktok[:, 0, :], ps[:, 0, 0:D], ACT.Relu)
                    sc.activation(vtok[:, 0, :, 0:P], ps[:, 0, D:2 * D].rearrange("p (g c) -> p g c", g=2), ACT.Copy).then_inc(a_kv, 1)
                if t_:
                    ge(act, p_q2, b)
                    copy_xn(1, b, 3, xn2T)
                    act.wait_ge(p_q2, b + 1)
                    ge(act, p_sT, NC * b)
                    ge(act, v_q2b, b)
                    sc.activation(q2T[:].rearrange("p k n -> p (k n)"), ps[:, 4, :], ACT.Copy, scale=float(HD) ** -0.5).then_inc(a_q2, 1)
                if s:
                    act.wait_ge(p_oT, b + 2)
                    ge(act, p_att, b + 1)
                    sc.activation(oT[:].rearrange("p k n -> p (k n)"), ps[:, 1, :], ACT.Copy).then_inc(a_oT, 1)
                if t_:
                    act.wait_ge(p_m, b + 1)
                    sc.activation(mrow[:], ps[:, 3, 0:N // 2].bitcast(BF16), ACT.Copy).then_inc(a_m, 1)
                    ge(act, p_av, b)
                    for c, (rows, h0, ns) in enumerate(SLOTS):
                        act.wait_ge(p_sT, NC * b + c + 1)
                        sc.activation(expT[0:rows, c, :, :], ps[0:rows, (5, 6, 7, 4, 5)[c], :].rearrange("p (g n) -> p g n", g=2),
                                      ACT.Exp).then_inc(a_e, 1)
                    act.wait_ge(p_o2T, b + 1)
                    ge(act, p_out, b)
                    sc.activation(o2T[:].rearrange("p k n -> p (k n)"), ps[:, 3, :], ACT.Copy).then_inc(a_o2T, 1)

            bodies(act, body)
            sc_b = NB - 1
            act.wait_ge(st_xn, 16 * KC * sc_b)
            copy_xn(2, sc_b, 3, xn3T)

        @block.tensor
        def _(pe):
            te = nc.tensor
            pe.wait_ge(g_c, 11)
            pe.wait_ge(v_c, 12)
            for n in range(3 * 3):
                w, f = n // 3, n % 3
                ge(pe, v_wl, n - 7)
                for q in range(4):
                    at = 4 * f + q
                    if w < 2:
                        k, m = at // FT, at % FT
                        src = W3[:, w, m * D + k * P:m * D + (k + 1) * P]
                    else:
                        k, m = at // KC, at % KC
                        src = W3[:, w, m * F + k * P:m * F + (k + 1) * P]
                    last = te.transpose(ps[:, n % 8, q * P:(q + 1) * P], src, ident[:])
                last.then_inc(p_wT, 1)
            pe.wait_ge(v_wl, 9)
            pe.wait_ge(ld_w, 16 * 10)

            def transpose_tiles(bank, src, s):
                for k in range(KC):
                    for t in range(NT):
                        last = te.transpose(ps[:, bank, k * N + t * P:k * N + (t + 1) * P], src[:, t, k * P:(k + 1) * P], ident[:])
                last.then_inc(s, 1)

            def body(b, par, h):
                s, t_ = has_s(b), has_t(b)
                if s:
                    pe.wait_ge(v_xn[0], b + 2)
                    ge(pe, v_x1, b + 1)
                    transpose_tiles(0, xn1, p_xn[0])
                if has_prev(b):
                    pe.wait_ge(v_xn[2], b)
                    pe.wait_ge(a_o2T, b)
                    transpose_tiles(3, xn3, p_xn[2])
                if t_:
                    pe.wait_ge(ld_ctx[par], 16 * nth(h, par, 0))
                    ge(pe, a_xn[2], b)
                    ge(pe, a_o2T, b)
                    te.transpose(ps[:, 3, 0:J], ctxin[par][:, 0:P], ident[0:J, 0:J])
                    te.transpose(ps[:, 3, J:2 * J], ctxin[par][:, P:2 * P], ident[0:J, 0:J]).then_inc(p_cT, 1)
                if s:
                    pe.wait_ge(a_xn[0], b + 2)
                    ge(pe, a_oT, b + 1)
                    for m in range(KC):
                        for k in range(KC):
                            last = te.matmul(ps[:, 1, m * N:(m + 1) * N], wq1[:, k, m * P:(m + 1) * P], xn1T[:, k, :],
                                             start=(k == 0), stop=(k == KC - 1))
                    last.then_inc(p_q, 1)
                if t_:
                    pe.wait_ge(a_cT, b + 1)
                    ge(pe, v_x2, b)
                    for g in range(2):
                        for k in range(2):
                            te.matmul(ps[:, 4, g * J:(g + 1) * J], wk2[:, k, g * P:(g + 1) * P], ctxT[:, k, :],
                                      start=(k == 0), stop=(k == 1))
                    for k in range(2):
                        last = te.matmul(ps[0:J, 4, 256:512], ctxT[:, k, :], wv2[:, k, :], start=(k == 0), stop=(k == 1))
                    last.then_inc(p_ckv, 1)
                if s:
                    ge(pe, v_o, b + 1)
                    for t in range(NT):
                        for k in range(KC):
                            last = te.matmul(ps[:, 2 * t, :], xn1T[:, k, t * P:(t + 1) * P], wq1[:, k, D:3 * D],
                                             start=(k == 0), stop=(k == KC - 1))
                    last.then_inc(p_kv, 1)
                if t_:
                    pe.wait_ge(v_xn[1], b + 1)
                    transpose_tiles(3, xn2, p_xn[1])
                    pe.wait_ge(v_v, b + 1)
                    pe.wait_ge(a_xn[1], b + 1)
                    vg = vsb[:].rearrange("j (g c) -> j g c", g=2)
                    for c, (rows, h0, ns) in enumerate(SLOTS):
                        last = te.matmul(ps[:, 3, 2 * OFF[c] * HD:2 * OFF[c + 1] * HD], Sel[:, c * P:(c + 1) * P],
                                         vg[:, :, h0 * HD:(h0 + ns) * HD], start=True, stop=True)
                    last.then_inc(p_vr, 1)
                if s:
                    pe.wait_ge(a_kv, b + 2)
                    pe.wait_ge(v_kv, b + 2)
                    pe.wait_ge(a_q, b + 2)
                    for g in range(2):
                        for t in range(NT):
                            last = te.matmul(ps[:, 1, g * (P + 1):(g + 1) * (P + 1)], ktok[:, t, g * P:(g + 1) * P],
                                             vtok[:, t, g, :], start=(t == 0), stop=(t == NT - 1))
                    last.then_inc(p_agg, 1)
                if t_:
                    pe.wait_ge(v_kT, b + 1)
                    for m in range(KC):
                        for k in range(KC):
                            last = te.matmul(ps[:, 4, m * N:(m + 1) * N], wq2[:, k, m * P:(m + 1) * P], xn2T[:, k, :],
                                             start=(k == 0), stop=(k == KC - 1))
                    last.then_inc(p_q2, 1)

                def scores(t):
                    for bank, c0, g, h0, nh in ((5, 0, 0, 0, 6), (6, 0, 0, 6, 2), (6, 2 * J, 1, 0, 4), (7, 0, 1, 4, 4)):
                        o = ps[:, bank, c0:c0 + nh * J]
                        te.matmul(o, q2Tb[:, g, t * P:(t + 1) * P], KBDb[par][:, g, h0 * J:(h0 + nh) * J], start=True, stop=False)
                        last = te.matmul(o, maskrow1[:], aug[par][:, g, h0 * J:(h0 + nh) * J], start=False, stop=True)
                    last.then_inc(p_s, 1)

                if t_:
                    pe.wait_ge(v_q2b, b + 1)
                    pe.wait_ge(g_kbd, b + 1)
                    pe.wait_ge(ld_mrow[par], 32 * nth(h, par, 0))
                    ge(pe, v_o2, b)
                    scores(0)
                if s:
                    pe.wait_ge(v_bd, b + 2)
                    for t in range(NT):
                        for g in range(2):
                            last = te.matmul(ps[:, 2 * t, g * NG:(g + 1) * NG], qT[:, g, t * P:(t + 1) * P], kvbd[:, g, :],
                                             start=True, stop=True)
                    last.then_inc(p_num, 1)
                if t_:
                    pe.wait_ge(v_max, 2 * b + 1)
                    scores(1)
                if s:
                    pe.wait_ge(v_o, b + 2)
                    transpose_tiles(1, otok, p_oT)
                if t_:
                    pe.wait_ge(v_max, 2 * b + 2)
                    pe.wait_ge(v_vbd, b + 1)
                    for t in range(NT):
                        last = te.transpose(ps[:, 3, 0:N // 2].bitcast(BF16)[:, t * P:(t + 1) * P], mtile[:, t, :], identb[:])
                    last.then_inc(p_m, 1)
                    pe.wait_ge(a_m, b + 1)
                    for c, (rows, h0, ns) in enumerate(SLOTS):
                        bank = (5, 6, 7, 4, 5)[c]
                        if c == 3:
                            pe.wait_ge(a_q2, b + 1)
                        if c == 4:
                            pe.wait_ge(a_e, NC * b + 1)
                        for g in range(2):
                            o = ps[0:rows, bank, g * N:(g + 1) * N]
                            te.matmul(o, KBD[par][:, g, c * P:c * P + rows], q2T[:, g, :], start=True, stop=False)
                            last = te.matmul(o, aug[par][:, g, c * P:c * P + rows], mrow[:], start=False, stop=True)
                        last.then_inc(p_sT, 1)
                    pe.wait_ge(a_e, NC * (b + 1))
                    for t in range(NT):
                        for c, (rows, h0, ns) in enumerate(SLOTS):
                            for g in range(2):
                                c0 = (HG * g + h0) * (HD + 1)
                                v0 = 2 * OFF[c] + g * ns
                                last = te.matmul(ps[:, 6 + t, c0:c0 + ns * (HD + 1)], expT[0:rows, c, g, t * P:(t + 1) * P],
                                                 Vbd[0:rows, v0:v0 + ns, :].rearrange("p s i -> p (s i)"),
                                                 start=(c == 0 and g == 0), stop=(c == NC - 1), skip_group_check=True)
                    last.then_inc(p_av, 1)
                if s:
                    pe.wait_ge(a_oT, b + 2)
                    for t in range(NT):
                        for k in range(KC):
                            last = te.matmul(ps[:, 0, t * D:(t + 1) * D], oT[:, k, t * P:(t + 1) * P], wo1[:, k, :],
                                             start=(k == 0), stop=(k == KC - 1))
                    last.then_inc(p_att, 1)
                if t_:
                    pe.wait_ge(v_o2, b + 1)
                    transpose_tiles(3, o2, p_o2T)
                    pe.wait_ge(a_o2T, b + 1)
                    for t in range(NT):
                        for k in range(KC):
                            last = te.matmul(ps[:, 4, t * D:(t + 1) * D], o2T[:, k, t * P:(t + 1) * P], wo2[:, k, :],
                                             start=(k == 0), stop=(k == KC - 1))
                    last.then_inc(p_out, 1)

            bodies(pe, body)
            pe.wait_ge(v_xn[2], NB)
            transpose_tiles(3, xn3, p_xn[2])


def feed_forward_phases(nc, top, ps, wh, wl, wscale, xmax, x2_d, xn_d, g_d, p_d, out, NB, NCH, FT, sb_in, sem_in):
    KC = 2
    D = KC * P
    FC = FT * CH
    NP = FT // 2
    BT = CH // (2 * P)
    keep, ksem = sb_in(top), sem_in(top)
    R = keep("R", [P, NCH, KC, 2, CH], F16)
    sc = keep("sc", [P, 16], F32)
    gmax = keep("gmax", [P, NCH * NP], F32)
    umax = keep("umax", [P, NCH * NP], F32)
    smax = keep("smax", [P, 3 * NCH], F32)
    pmax = keep("pmax", [P, NP * NCH], F32)
    SX, KX, AG, AU, SG, KG, SU, KU, SS, CS, SO, KO, TD = range(13)

    def pair(n):
        return ps[:, 2 * (n % 4):2 * (n % 4) + 2, :]

    def chunks(eng, body):
        with eng.Fori(0, NCH // 2) as i:
            body(i * 2, 0)
            body(i * 2 + 1, 1)

    def at(ap, n):
        return ap[:, n:n + 1] if isinstance(n, int) else ap[:, bass.ds(n, 1)]

    def scale_of(dve, done, count, largest, factor, s, k):
        vec = nc.vector
        if factor is None:
            vec.tensor_scalar(sc[:, s:s + 1], largest, 1.0 / QMAX16, SMALLEST, ALU.mult, ALU.max).then_inc(done, 1)
        else:
            vec.tensor_scalar(sc[:, s:s + 1], largest, sc[:, factor:factor + 1], 1.0 / QMAX16, ALU.mult, ALU.mult).then_inc(done, 1)
            count += 1
            dve.wait_ge(done, count)
            vec.tensor_scalar(sc[:, s:s + 1], sc[:, s:s + 1], SMALLEST, None, ALU.max).then_inc(done, 1)
        count += 1
        dve.wait_ge(done, count)
        vec.reciprocal(sc[:, k:k + 1], sc[:, s:s + 1]).then_inc(done, 1)
        count += 1
        dve.wait_ge(done, count)
        return count

    def times(dve, done, count, dst, a, b, c=None):
        if c is None:
            nc.vector.tensor_scalar(sc[:, dst:dst + 1], a, b, None, ALU.mult).then_inc(done, 1)
        else:
            nc.vector.tensor_scalar(sc[:, dst:dst + 1], a, b, c, ALU.mult, ALU.mult).then_inc(done, 1)
        dve.wait_ge(done, count + 1)
        return count + 1

    with ExitStack() as stack:
        sb, sem = sb_in(stack), sem_in(stack)
        xf = [sb(f"xf{i}", [P, KC, CH], F32) for i in range(2)]
        gs = [sb(f"gs{i}", [P, 2, CH], F32) for i in range(NP)]
        pm = sb("pm", [P, 1], F32)
        pa = sb("pa", [P, 1], F32)
        done, g_all, v_pm = sem("b_done"), sem("b_all"), sem("b_pm")
        ld = [sem(f"b_ld{i}") for i in range(2)]
        a_r, v_hi, v_r = sem("b_round"), sem("b_hi"), sem("b_lo")
        p_g, a_g, v_g = sem("b_pg"), sem("b_ag"), sem("b_vg")
        st_g = [sem(f"b_stg{j}") for j in range(NP)]
        p_u, v_u = sem("b_pu"), sem("b_vu")
        block = stack.enter_context(nc.Block())

        @block.sync
        def _(sp):
            def body(n, par):
                if not (isinstance(n, int) and n < 2):
                    sp.wait_ge(v_r, n - 1)
                for i in range(BT):
                    sp.dma_start(xf[par][:, :, i * 2 * P:(i + 1) * 2 * P], xn_d[n * BT + i]).then_inc(ld[par], 16)

            body(0, 0)
            body(1, 1)
            with sp.Fori(1, NCH // 2) as i:
                body(i * 2, 0)
                body(i * 2 + 1, 1)

        @block.gpsimd
        def _(gp):
            gp.wait_ge(v_pm, 1)
            nc.gpsimd.partition_all_reduce(pa[:], pm[:], P, RMAX).then_inc(g_all, 1)

        @block.vector
        def _(dve):
            vec = nc.vector
            vec.tensor_reduce(pm[:], xmax[:], AX.X, ALU.max).then_inc(v_pm, 1)
            dve.wait_ge(g_all, 1)
            c = scale_of(dve, done, 0, pa[:], None, SX, KX)
            c = times(dve, done, c, AG, wscale[:, 0:1], sc[:, SX:SX + 1])
            c = times(dve, done, c, AU, wscale[:, 1:2], sc[:, SX:SX + 1])
            assert c == 4

            def split(n, par):
                dve.wait_ge(a_r, n + 1)
                r = R[:, n:n + 1] if isinstance(n, int) else R[:, bass.ds(n, 1)]
                r = r.rearrange("p n k s c -> p (n k) s c")
                vec.tensor_scalar(r[:, :, 0, :], xf[par][:], -ROUND, None, ALU.add).then_inc(v_hi, 1)
                dve.wait_ge(v_hi, n + 1)
                vec.scalar_tensor_tensor(out=r[:, :, 1, :], in0=xf[par][:], scalar=-ROUND, in1=r[:, :, 0, :],
                                         op0=ALU.add, op1=ALU.subtract).then_inc(v_r, 1)

            def body(n, par, last):
                if not last:
                    split(n + 1, 1 - par)
                for j in range(NP):
                    dve.wait_ge(a_g, n * NP + j + 1)
                    vec.tensor_reduce(at(gmax, n * NP + j), gs[j][:], AX.XY, ALU.max,
                                      apply_absolute_value=True).then_inc(v_g, 1)
                for j in range(NP):
                    dve.wait_ge(p_u, n * NP + j + 1)
                    vec.tensor_reduce(at(umax, n * NP + j), pair(NP + j + 2 * NP * par), AX.XY, ALU.max,
                                      apply_absolute_value=True).then_inc(v_u, 1)

            split(0, 0)
            with dve.Fori(0, NCH // 2 - 1) as i:
                body(i * 2, 0, False)
                body(i * 2 + 1, 1, False)
            body(NCH - 2, 0, False)
            body(NCH - 1, 1, True)

        @block.scalar
        def _(act):
            def scale_x(n, par, use):
                act.wait_ge(ld[par], 16 * BT * use)
                nc.scalar.activation(xf[par][:], xf[par][:], ACT.Copy, scale=sc[:, KX:KX + 1], bias=ROUND).then_inc(a_r, 1)

            def body(n, par, i, peeled, last=False):
                if not last:
                    scale_x(n + 1, 1 - par, i + par + 1)
                for j in range(NP):
                    act.wait_ge(p_g, n * NP + j + 1)
                    if not peeled:
                        act.wait_ge(v_g, (n - 1) * NP + j + 1)
                        act.wait_ge(st_g[j], 16 * n)
                    nc.scalar.activation(gs[j][:], pair(j + 2 * NP * par), ACT.Copy).then_inc(a_g, 1)
                    act.wait_ge(a_g, n * NP + j + 1)
                    act.dma_start((g_d[n])[:, 2 * CH * j:2 * CH * (j + 1)], gs[j][:].rearrange("p a c -> p (a c)")).then_inc(st_g[j], 16)

            act.wait_ge(done, 4)
            scale_x(0, 0, 1)
            body(0, 0, 0, True)
            body(1, 1, 0, False)
            with act.Fori(1, NCH // 2 - 1) as i:
                body(i * 2, 0, i, False)
                body(i * 2 + 1, 1, i, False)
            body(NCH - 2, 0, NCH // 2 - 1, False)
            body(NCH - 1, 1, NCH // 2 - 1, False, True)
            for j in range(NP):
                act.wait_ge(st_g[j], 16 * NCH)

        @block.tensor
        def _(pe):
            def body(n, par, first):
                pe.wait_ge(v_r, n + 1)
                for w, freed, s in ((0, a_g, p_g), (1, v_u, p_u)):
                    for j in range(NP):
                        back = 2 * NP * par + NP * w + j - 4
                        self_w, self_j, self_n = (back // NP) % 2, back % NP, back // (2 * NP)
                        if not (first and back < 0):
                            pe.wait_ge(v_u if self_w else a_g, (n - par + self_n) * NP + self_j + 1)
                        for m in range(2):
                            o = pair(2 * NP * par + NP * w + j)[:, m, :]
                            for k in range(KC):
                                col = k * FT * P + (2 * j + m) * P
                                r = R[:, n:n + 1, k] if isinstance(n, int) else R[:, bass.ds(n, 1), k]
                                r = r.rearrange("p n s c -> p (n s) c")
                                for q, (lhs, part) in enumerate(((wh, 0), (wl, 0), (wh, 1))):
                                    last = nc.tensor.matmul(o, lhs[:, w, col:col + P], r[:, part, :],
                                                            start=(k == 0 and q == 0), stop=(k == KC - 1 and q == 2))
                        last.then_inc(s, 1)

            body(0, 0, True)
            body(1, 1, False)
            with pe.Fori(1, NCH // 2) as i:
                body(i * 2, 0, False)
                body(i * 2 + 1, 1, False)

    with ExitStack() as stack:
        sb, sem = sb_in(stack), sem_in(stack)
        gf = [sb(f"gf{i}", [P, FC // 3], F32) for i in range(2)]
        gq = [sb(f"gq{i}", [P, FC // 3], I16) for i in range(2)]
        sg = [sb(f"sg{i}", [P, FC // 3], F32) for i in range(2)]
        sq = [sb(f"sq{i}", [P, FC // 3], U16) for i in range(2)]
        pm = sb("pm2", [P, 2], F32)
        pa = sb("pa2", [P, 2], F32)
        done, g_all, v_pm = sem("c_done"), sem("c_all"), sem("c_pm")
        ld = [sem(f"c_ld{i}") for i in range(2)]
        a_q, a_s, v_q, v_f, v_m = sem("c_q"), sem("c_s"), sem("c_vq"), sem("c_vf"), sem("c_vm")
        block = stack.enter_context(nc.Block())
        G3 = FC // 3
        NU = 3 * NCH

        def units(eng, body):
            body(0, 0, 0, True)
            body(1, 1, 0, True)
            with eng.Fori(1, NU // 2) as i:
                body(i * 2, 0, i, False)
                body(i * 2 + 1, 1, i, False)

        @block.sync
        def _(sp):
            def body(n, par):
                for j in range(3):
                    q = (3 * par + j)
                    if not (isinstance(n, int) and q < 2):
                        sp.wait_ge(a_q, 3 * n + j - 1)
                    sp.dma_start(gf[q % 2][:], (g_d[n])[:, j * G3:(j + 1) * G3]).then_inc(ld[q % 2], 16)

            body(0, 0)
            body(1, 1)
            with sp.Fori(1, NCH // 2) as i:
                body(i * 2, 0)
                body(i * 2 + 1, 1)

        @block.gpsimd
        def _(gp):
            gp.wait_ge(v_pm, 2)
            nc.gpsimd.partition_all_reduce(pa[:], pm[:], P, RMAX).then_inc(g_all, 1)

        @block.vector
        def _(dve):
            vec = nc.vector
            vec.tensor_reduce(pm[:, 0:1], gmax[:], AX.X, ALU.max).then_inc(v_pm, 1)
            vec.tensor_reduce(pm[:, 1:2], umax[:], AX.X, ALU.max).then_inc(v_pm, 1)
            dve.wait_ge(g_all, 1)
            c = scale_of(dve, done, 0, pa[:, 0:1], AG, SG, KG)
            c = scale_of(dve, done, c, pa[:, 1:2], AU, SU, KU)
            c = times(dve, done, c, KG, sc[:, KG:KG + 1], sc[:, AG:AG + 1])
            c = times(dve, done, c, KU, sc[:, KU:KU + 1], sc[:, AU:AU + 1])
            assert c == 8

            def body(n, par, i, first):
                dve.wait_ge(a_s, n + 1)
                vec.tensor_scalar(sq[par][:], sg[par][:], 65536.0, 65535.0, ALU.mult, ALU.min).then_inc(v_q, 1)
                dve.wait_ge(v_q, n + 1)
                if not (isinstance(n, int) and n < 1):
                    dve.wait_ge(v_m, n)
                vec.tensor_tensor(sg[par][:], sq[par][:], gq[par][:], ALU.mult).then_inc(v_f, 1)
                dve.wait_ge(v_f, n + 1)
                vec.tensor_reduce(at(smax, n), sg[par][:], AX.X, ALU.max, apply_absolute_value=True).then_inc(v_m, 1)

            units(dve, body)

        @block.scalar
        def _(act):
            act.wait_ge(done, 8)

            def body(n, par, i, first):
                act.wait_ge(ld[par], 16 * (i + 1))
                if not first:
                    act.wait_ge(v_m, n - 1)
                nc.scalar.activation(gq[par][:], gf[par][:], ACT.Copy, scale=sc[:, KG:KG + 1]).then_inc(a_q, 1)
                act.wait_ge(a_q, n + 1)
                nc.scalar.activation(sg[par][:], gq[par][:], ACT.Sigmoid, scale=sc[:, SG:SG + 1]).then_inc(a_s, 1)

            units(act, body)

    with ExitStack() as stack:
        sb, sem = sb_in(stack), sem_in(stack)
        G = 2 * CH
        gf = [sb(f"df{i}", [P, G], F32) for i in range(2)]
        gq = [sb(f"dq{i}", [P, G], I16) for i in range(2)]
        sg = [sb(f"dg{i}", [P, G], F32) for i in range(2)]
        sq = [sb(f"ds{i}", [P, G], U16) for i in range(2)]
        gz = [sb(f"dz{i}", [P, G], I16) for i in range(2)]
        uq = [sb(f"du{i}", [P, G], I16) for i in range(2)]
        pr = [sb(f"dp{i}", [P, G], F32) for i in range(2)]
        pm = sb("pm3", [P, 1], F32)
        pa = sb("pa3", [P, 1], F32)
        done, g_all, v_pm = sem("d_done"), sem("d_all"), sem("d_pm")
        ld, st = ([sem(f"d_{n}{i}") for i in range(2)] for n in ("ld", "st"))
        a_q, a_s, v_q, v_z = sem("d_q"), sem("d_s"), sem("d_vq"), sem("d_vz")
        p_u, a_u, v_p, v_m = sem("d_pu"), sem("d_au"), sem("d_vp"), sem("d_vm")
        block = stack.enter_context(nc.Block())

        def steps(eng, body):
            for n in range(2):
                for j in range(NP):
                    q = NP * n + j
                    body(n, j, q % 2, q, q, q // 2 + 1)
            with eng.Fori(1, NCH // 2) as i:
                for par in range(2):
                    for j in range(NP):
                        q = NP * par + j
                        body(i * 2 + par, j, q % 2, i * (2 * NP) + q, 99, i * NP + q // 2 + 1)

        @block.sync
        def _(sp):
            def store(u, par):
                sp.wait_ge(v_p, u + 1)
                sp.dma_start(p_d[u], pr[par][:]).then_inc(st[par], 16)

            def body(n, j, par, u, early, use):
                if early >= 2:
                    sp.wait_ge(a_q, u - 1)
                sp.dma_start(gf[par][:], (g_d[n])[:, j * G:(j + 1) * G]).then_inc(ld[par], 16)
                if early >= 1:
                    store(u - 1, 1 - par)

            steps(sp, body)
            store(NP * NCH - 1, 1)
            for i in range(2):
                sp.wait_ge(st[i], 16 * NCH * NP // 2)

        @block.gpsimd
        def _(gp):
            gp.wait_ge(v_pm, 1)
            nc.gpsimd.partition_all_reduce(pa[:], pm[:], P, RMAX).then_inc(g_all, 1)


        @block.vector
        def _(dve):
            vec = nc.vector
            vec.tensor_reduce(pm[:], smax[:], AX.X, ALU.max).then_inc(v_pm, 1)
            vec.tensor_scalar(sc[:, TD:TD + 1], sc[:, SG:SG + 1], 1.0 / 65536.0, None, ALU.mult).then_inc(done, 1)
            dve.wait_ge(done, 1)
            dve.wait_ge(g_all, 1)
            c = scale_of(dve, done, 1, pa[:], TD, SS, CS)
            c = times(dve, done, c, CS, sc[:, CS:CS + 1], sc[:, TD:TD + 1])

            def body(n, j, par, u, early, use):
                dve.wait_ge(a_s, u + 1)
                vec.tensor_scalar(sq[par][:], sg[par][:], 65536.0, 65535.0, ALU.mult, ALU.min).then_inc(v_q, 1)
                dve.wait_ge(v_q, u + 1)
                vec.scalar_tensor_tensor(out=gz[par][:], in0=sq[par][:], scalar=sc[:, CS:CS + 1], in1=gq[par][:],
                                         op0=ALU.mult, op1=ALU.mult).then_inc(v_z, 1)
                dve.wait_ge(v_z, u + 1)
                dve.wait_ge(a_u, u + 1)
                if early >= 2:
                    dve.wait_ge(st[par], 16 * (use - 1))
                vec.tensor_tensor(pr[par][:], gz[par][:], uq[par][:], ALU.mult).then_inc(v_p, 1)
                dve.wait_ge(v_p, u + 1)
                vec.tensor_reduce(at(pmax, u), pr[par][:], AX.X, ALU.max, apply_absolute_value=True).then_inc(v_m, 1)

            steps(dve, body)

        @block.scalar
        def _(act):
            def body(n, j, par, u, early, use):
                act.wait_ge(ld[par], 16 * use)
                if early >= 2:
                    act.wait_ge(v_z, u - 1)
                nc.scalar.activation(gq[par][:], gf[par][:], ACT.Copy, scale=sc[:, KG:KG + 1]).then_inc(a_q, 1)
                act.wait_ge(a_q, u + 1)
                nc.scalar.activation(sg[par][:], gq[par][:], ACT.Sigmoid, scale=sc[:, SG:SG + 1]).then_inc(a_s, 1)
                act.wait_ge(p_u, u + 1)
                if early >= 2:
                    act.wait_ge(v_p, u - 1)
                nc.scalar.activation(uq[par][:].rearrange("p (a c) -> p a c", a=2), pair(j), ACT.Copy,
                                     scale=sc[:, KU:KU + 1]).then_inc(a_u, 1)

            steps(act, body)

        @block.tensor
        def _(pe):
            def body(n, j, par, u, early, use):
                if early >= NP:
                    pe.wait_ge(a_u, u - NP + 1)
                for m in range(2):
                    o = pair(j)[:, m, :]
                    for k in range(KC):
                        col = k * FT * P + (2 * j + m) * P
                        r = R[:, n:n + 1, k] if isinstance(n, int) else R[:, bass.ds(n, 1), k]
                        r = r.rearrange("p n s c -> p (n s) c")
                        for q, (lhs, part) in enumerate(((wh, 0), (wl, 0), (wh, 1))):
                            last = nc.tensor.matmul(o, lhs[:, 1, col:col + P], r[:, part, :],
                                                    start=(k == 0 and q == 0), stop=(k == KC - 1 and q == 2))
                last.then_inc(p_u, 1)

            steps(pe, body)

    with ExitStack() as stack:
        sb, sem = sb_in(stack), sem_in(stack)
        G = FC // NP
        pf = [sb(f"ef{i}", [P, G], F32) for i in range(NP)]
        oq = sb("eq", [P, FC], I16)
        oh = sb("eh", [P, FC], F16)
        ol = sb("el", [P, FC], F16)
        xr = [sb(f"ex{i}", [P, BT * 2, D], F32) for i in range(2)]
        pm = sb("pm4", [P, 1], F32)
        pa = sb("pa4", [P, 1], F32)
        done, g_all, v_pm = sem("e_done"), sem("e_all"), sem("e_pm")
        ld = [sem(f"e_ld{i}") for i in range(NP)]
        ldx, st = ([sem(f"e_{n}{i}") for i in range(2)] for n in ("ldx", "st"))
        v_q, a_h, v_l, p_o, v_o = sem("e_vq"), sem("e_ah"), sem("e_vl"), sem("e_po"), sem("e_vo")
        block = stack.enter_context(nc.Block())

        def steps(eng, body):
            body(0, 0, 0, 0)
            body(1, 1, 1, 0)
            with eng.Fori(1, NCH // 2) as i:
                body(i * 2, 0, 99, i)
                body(i * 2 + 1, 1, 99, i)

        @block.sync
        def _(sp):
            def body(n, par, early, i):
                for h in range(NP):
                    if early >= 1:
                        sp.wait_ge(v_q, NP * (n - 1) + h + 1)
                    sp.dma_start(pf[h][:], p_d[NP * n + h]).then_inc(ld[h], 16)
                if early >= 2:
                    sp.wait_ge(st[par], 16 * BT * i)
                for k in range(BT):
                    sp.dma_start(xr[par][:, 2 * k:2 * k + 2, :], x2_d[BT * n + k].rearrange("p (t d) -> p t d", t=2)).then_inc(ldx[par], 16)

            steps(sp, body)

        @block.gpsimd
        def _(gp):
            gp.wait_ge(v_pm, 1)
            nc.gpsimd.partition_all_reduce(pa[:], pm[:], P, RMAX).then_inc(g_all, 1)

        @block.scalar
        def _(act):
            def body(n, par, early, i):
                for h in range(NP):
                    act.wait_ge(v_q, NP * n + h + 1)
                    if early >= 1:
                        act.wait_ge(p_o, n)
                    nc.scalar.activation(oh[:, h * G:(h + 1) * G], oq[:, h * G:(h + 1) * G], ACT.Copy).then_inc(a_h, 1)
                act.wait_ge(v_o, n + 1)
                for k in range(BT):
                    act.dma_start(out[BT * n + k].rearrange("(p t) d -> p t d", t=2), xr[par][:, 2 * k:2 * k + 2, :]).then_inc(st[par], 16)

            steps(act, body)
            for i in range(2):
                act.wait_ge(st[i], 16 * BT * NCH // 2)

        @block.vector
        def _(dve):
            vec = nc.vector
            vec.tensor_reduce(pm[:], pmax[:], AX.X, ALU.max).then_inc(v_pm, 1)
            vec.tensor_scalar(sc[:, TD:TD + 1], sc[:, SS:SS + 1], sc[:, SU:SU + 1], None, ALU.mult).then_inc(done, 1)
            dve.wait_ge(done, 1)
            dve.wait_ge(g_all, 1)
            c = scale_of(dve, done, 1, pa[:], TD, SO, KO)
            c = times(dve, done, c, KO, sc[:, KO:KO + 1], sc[:, TD:TD + 1])
            c = times(dve, done, c, TD, sc[:, SO:SO + 1], wscale[:, 2:3])

            def body(n, par, early, i):
                for h in range(NP):
                    dve.wait_ge(ld[h], 16 * (n + 1))
                    if early >= 1:
                        dve.wait_ge(a_h, NP * n)
                        dve.wait_ge(v_l, NP * n)
                    vec.tensor_scalar(oq[:, h * G:(h + 1) * G], pf[h][:], sc[:, KO:KO + 1], None, ALU.mult).then_inc(v_q, 1)
                for h in range(NP):
                    dve.wait_ge(a_h, NP * n + h + 1)
                    if early >= 1:
                        dve.wait_ge(p_o, n)
                    vec.tensor_tensor(ol[:, h * G:(h + 1) * G], oq[:, h * G:(h + 1) * G], oh[:, h * G:(h + 1) * G],
                                      ALU.subtract).then_inc(v_l, 1)
                dve.wait_ge(p_o, n + 1)
                dve.wait_ge(ldx[par], 16 * BT * (i + 1))
                o = ps[:, 2 * par:2 * par + 2, :].rearrange("p a c -> p (a c)")
                xf = xr[par][:].rearrange("p a c -> p (a c)")
                vec.scalar_tensor_tensor(out=xf, in0=o, scalar=sc[:, TD:TD + 1], in1=xf, op0=ALU.mult, op1=ALU.add).then_inc(v_o, 1)

            steps(dve, body)

        @block.tensor
        def _(pe):
            def body(n, par, early, i):
                pe.wait_ge(v_l, NP * (n + 1))
                if early >= 2:
                    pe.wait_ge(v_o, n - 1)
                for t in range(CH // P):
                    o = ps[:, 2 * par + t // 2, (t % 2) * D:(t % 2 + 1) * D]
                    for k in range(FT):
                        w0 = k * D
                        c0 = k * CH + t * P
                        for q, (lhs, rhs) in enumerate(((oh, wh), (oh, wl), (ol, wh))):
                            last = nc.tensor.matmul(o, lhs[:, c0:c0 + P], rhs[:, 2, w0:w0 + D],
                                                    start=(k == 0 and q == 0), stop=(k == FT - 1 and q == 2))
                last.then_inc(p_o, 1)

            steps(pe, body)


_INS = ["x", "ctx_768", "mask_BxS2_bf1", "L0_attn_Wqkv", "L0_attn_Wout", "L0_attn_bout", "L0_xattn_Wq", "L0_xattn_Wk",
        "L0_xattn_Wv", "L0_xattn_Wo", "L0_ffn_w_gate", "L0_ffn_w_up", "L0_ffn_w_down"]


def kernel(**inputs):
    import numpy as np
    import concourse.bacc as bacc
    from concourse.bass_utils import run_bass_kernel_spmd

    nc = bacc.Bacc("TRN2", target_bir_lowering=False, num_devices=1)
    arrays, args = {}, []
    for name in _INS:
        a = np.ascontiguousarray(inputs[name])
        if a.dtype == np.bool_:
            a = a.view(np.uint8)
        arrays[f"in_{name}"] = a
        args.append(nc.dram_tensor(f"in_{name}", a.shape, mybir.dt.from_np(a.dtype), kind="ExternalInput").ap())
    shape = tuple(inputs["x"].shape)
    args.append(nc.dram_tensor("out_x", shape, F32, kind="ExternalOutput").ap())
    decoder_layer(nc, *args)
    r = run_bass_kernel_spmd(nc, [arrays], core_ids=[0])
    return r.results[0]["out_x"]
```

```python
from contextlib import ExitStack

import concourse.bass as bass
from concourse import mybir

F32 = mybir.dt.float32
BF16 = mybir.dt.bfloat16
F16 = mybir.dt.float16
I16 = mybir.dt.int16
I32 = mybir.dt.int32
U16 = mybir.dt.uint16
U8 = mybir.dt.uint8
ALU = mybir.AluOpType
ACT = mybir.ActivationFunctionType
AX = mybir.AxisListType
RMAX = bass.bass_isa.ReduceOp.max

P = 128
H = 16
HG = 8
HD = 16
LN_EPS = 1e-5
ATT_EPS = 1e-6
BLOCK = 32
ROUND = 12582912.0
QMAX16 = 32767.0
SMALLEST = 1e-12
MASKED = -(2.0 ** 127)
WTOP = 4096.0
DIP = 0.3
CH = 512


def chunk_slots(J):
    out, at = [], 0
    while at < HG * J:
        rows = min(P, HG * J - at)
        first, last = at // J, (at + rows - 1) // J
        out.append((rows, first, last - first + 1))
        at += rows
    return out


def decoder_layer(nc, x, ctx, mask, wqkv, wout, bout, wq, wk, wv, wo, wgate, wup, wdown, out):
    NB, N, D = x.shape
    J, C = ctx.shape[1], ctx.shape[2]
    F = wgate.shape[0]
    T = NB * N
    NT = N // P
    KC = D // P
    FT = F // P
    NCH = T // CH
    HJ = HG * J
    SLOTS = chunk_slots(J)
    NC = len(SLOTS)
    NSLOT = sum(n for _, _, n in SLOTS)
    assert NT == 2 and KC == 2 and D == H * HD and J <= P and C <= 2 * P and NB % 2 == 0 and NB >= 8

    x2_d = nc.dram_tensor("x2_scratch", (NB, P, NT * D), F32).ap()
    xn_d = nc.dram_tensor("xn_scratch", (NB, P, KC, N), F32).ap()
    g_d = nc.dram_tensor("gate_scratch", (NCH, P, FT * CH), F32).ap()
    p_d = nc.dram_tensor("product_scratch", (NCH * FT // 2, P, 2 * CH), F32).ap()
    mrow_d = nc.dram_tensor("maskrow_scratch", (NB, HJ), BF16).ap()

    top = ExitStack()
    with top:
        def sb_in(stack):
            return lambda name, shape, dt: stack.enter_context(nc.sbuf_tensor(name, shape, dt))

        def sem_in(stack):
            return lambda name: stack.enter_context(nc.semaphore(name))

        keep = sb_in(top)
        ps = top.enter_context(nc.psum_tensor("ps", [P, 8, 512], F32))
        wh = keep("wh", [P, 3, FT * D], F16)
        wl = keep("wl", [P, 3, FT * D], F16)
        wscale = keep("wscale", [P, 3], F32)
        xmax = keep("xmax", [P, NB], F32)

        attention_phase(nc, ps, wh, wl, wscale, xmax, x2_d, xn_d, mrow_d, x, ctx, mask, wqkv, wout, bout,
                        wq, wk, wv, wo, wgate, wup, wdown, sb_in, sem_in)
        feed_forward_phases(nc, top, ps, wh, wl, wscale, xmax, x2_d, xn_d, g_d, p_d, out, NB, NCH, FT, sb_in, sem_in)


def attention_phase(nc, ps, wh, wl, wscale, xmax, x2_d, xn_d, mrow_d, x, ctx, mask, wqkv, wout, bout,
                    wq, wk, wv, wo, wgate, wup, wdown, sb_in, sem_in):
    NB, N, D = x.shape
    J, C = ctx.shape[1], ctx.shape[2]
    F = wgate.shape[0]
    NT, KC, FT = N // P, D // P, F // P
    HJ = HG * J
    SLOTS = chunk_slots(J)
    NC = len(SLOTS)
    OFF = [sum(n for _, _, n in SLOTS[:c]) for c in range(NC + 1)]
    NSLOT = OFF[NC]
    HJP = NC * P
    WB = FT * D // BLOCK
    NG = P + HG
    B1 = 6 if J * 6 <= 512 else 512 // J
    assert B1 == 6 and NC == 5
    stack = ExitStack()
    with stack:
        sb, sem = sb_in(stack), sem_in(stack)
        ident = sb("ident", [P, P], F32)
        identb = sb("identb", [P, P], BF16)
        HM = sb("HM", [P, HG], F32)
        BM = sb("BM", [P, P], F32)
        HRM = sb("HRM", [P, 2 * NSLOT], F32)
        Sel = sb("Sel", [J, HJP], F32)
        maskrow1 = sb("maskrow1", [P, P], BF16)
        wq1 = sb("wq1", [P, KC, 3 * D], F32)
        wo1 = sb("wo1", [P, KC, D], F32)
        wq2 = sb("wq2", [P, KC, D], F32)
        wk2 = sb("wk2", [P, 2, D], F32)
        wv2 = sb("wv2", [P, 2, D], F32)
        wo2 = sb("wo2", [P, KC, D], F32)
        bias = sb("bias", [P, D], F32)
        msk8 = sb("msk8", [P, NB, J], U8)
        mk = sb("mk", [NB, J], U8)
        mkf = sb("mkf", [NB, J], F32)
        mkr = sb("mkr", [NB, HG, J], BF16)
        W3 = sb("W3", [P, 3, FT * D], F32)
        am = sb("am", [P, 3 * WB], F32)
        s3 = sb("s3", [P, 3 * WB], F32)
        rs3 = sb("rs3", [P, 3 * WB], F32)
        sm = sb("sm", [P, 3], F32)
        smx = sb("smx", [P, 3], F32)
        rsm = sb("rsm", [P, 3], F32)
        mhalf = sb("mhalf", [P, NT], F32)
        epst = sb("epst", [P, NT], F32)
        fence = sb("fence", [P, 3], F32)

        xin = [sb(f"xin{i}", [P, NT, D], F32) for i in range(2)]
        ctxin = [sb(f"ctxin{i}", [J, 2 * P], F32) for i in range(2)]
        aug = [sb(f"aug{i}", [P, 2, HJ], BF16) for i in range(2)]
        st = [sb(f"st{i}", [P, NT, 6], F32) for i in range(3)]
        mv = [sb(f"mv{i}", [P, NT, 2], F32) for i in range(3)]
        ve = [sb(f"ve{i}", [P, NT], F32) for i in range(3)]
        rstd = [sb(f"rstd{i}", [P, NT], F32) for i in range(3)]
        xn1 = sb("xn1", [P, NT, D], F32)
        xn2 = sb("xn2", [P, NT, D], F32)
        xn3 = sb("xn3", [P, NT, D], F32)
        xn1T = sb("xn1T", [P, KC, N], F32)
        xn2T = sb("xn2T", [P, KC, N], F32)
        xn3T = sb("xn3T", [P, KC, N], F32)
        qT = sb("qT", [P, KC, N], F32)
        ktok = sb("ktok", [P, NT, D], F32)
        vtok = sb("vtok", [P, NT, 2, P + 1], F32)
        kvbd = sb("kvbd", [P, 2, NG], F32)
        dz = sb("dz", [P, NT, H], F32)
        zz = sb("zz", [P, NT, H], F32)
        otok = sb("otok", [P, NT, D], F32)
        oT = sb("oT", [P, KC, N], F32)
        xb = sb("xb", [P, NT, D], F32)
        x1 = [sb(f"x1_{i}", [P, NT, D], F32) for i in range(2)]
        ctxT = sb("ctxT", [P, 2, J], F32)
        kTm = sb("kTm", [P, 2, J], F32)
        vsb = sb("vsb", [J, D], F32)
        KBD = [sb(f"KBD{i}", [P, 2, HJ], F32) for i in range(2)]
        KBDb = [sb(f"KBDb{i}", [P, 2, HJ], BF16) for i in range(2)]
        Vbd = [sb(f"Vbd{i}", [P, NC, 2, HG, HD + 1], F32) for i in range(2)]
        q2T = sb("q2T", [P, KC, N], F32)
        q2Tb = sb("q2Tb", [P, KC, N], BF16)
        mtile = sb("mtile", [P, NT, P], BF16)
        mrow = sb("mrow", [P, N], BF16)
        expT = sb("expT", [P, NC, 2, N], F32)
        rden = sb("rden", [P, NT, H], F32)
        o2 = sb("o2", [P, NT, D], F32)
        o2T = sb("o2T", [P, KC, N], F32)
        x2 = [sb(f"x2_{i}", [P, NT, D], F32) for i in range(2)]

        ld_w = sem("ld_w")
        ld_w3 = sem("ld_w3")
        ld_m = sem("ld_m")
        g_c = sem("g_c")
        v_c = sem("v_c")
        g_smx = sem("g_smx")
        p_wT = sem("p_wT")
        a_wh = sem("a_wh")
        v_wl = sem("v_wl")
        st_m = sem("st_m")
        ld_x, ld_ctx, ld_mrow = ([sem(f"{n}{i}") for i in range(2)] for n in ("ld_x", "ld_ctx", "ld_mrow"))
        st_x2, st_xn = [sem(f"st_x2{i}") for i in range(2)], sem("st_xn")
        v_st = [sem(f"v_st{i}") for i in range(3)]
        v_ag = [sem(f"v_ag{i}") for i in range(3)]
        g_ve = [sem(f"g_ve{i}") for i in range(3)]
        g_rs = [sem(f"g_rs{i}") for i in range(3)]
        v_xn = [sem(f"v_xn{i}") for i in range(3)]
        p_xn = [sem(f"p_xn{i}") for i in range(3)]
        a_xn = [sem(f"a_xn{i}") for i in range(3)]
        p_q, a_q = sem("p_q"), sem("a_q")
        p_kv, a_kv, v_kv = sem("p_kv"), sem("a_kv"), sem("v_kv")
        p_agg, v_bd = sem("p_agg"), sem("v_bd")
        p_num, v_dz, v_z, v_o = sem("p_num"), sem("v_dz"), sem("v_z"), sem("v_o")
        p_oT, a_oT = sem("p_oT"), sem("a_oT")
        p_att, g_xb, v_x1 = sem("p_att"), sem("g_xb"), sem("v_x1")
        p_cT, a_cT = sem("p_cT"), sem("a_cT")
        p_ckv, v_kT, v_v, g_kbd = sem("p_ckv"), sem("v_kT"), sem("v_v"), sem("g_kbd")
        p_vr, v_vbd = sem("p_vr"), sem("v_vbd")
        p_q2, a_q2, v_q2b = sem("p_q2"), sem("a_q2"), sem("v_q2b")
        p_s, v_max = sem("p_s"), sem("v_max")
        p_m, a_m = sem("p_m"), sem("a_m")
        p_sT, a_e = sem("p_sT"), sem("a_e")
        p_av, v_rd, v_o2 = sem("p_av"), sem("v_rd"), sem("v_o2")
        p_o2T, a_o2T = sem("p_o2T"), sem("a_o2T")
        p_out, v_x2 = sem("p_out"), sem("v_x2")
        v_xm = sem("v_xm")

        block = stack.enter_context(nc.Block())

        def ge(eng, s, value):
            if isinstance(value, int) and value <= 0:
                return
            eng.wait_ge(s, value)

        def bodies(eng, body):
            body(-1, 1, -1)
            body(0, 0, 0)
            body(1, 1, 0)
            with eng.Fori(1, NB // 2 - 1) as i:
                body(i * 2, 0, i)
                body(i * 2 + 1, 1, i)
            body(NB - 2, 0, NB // 2 - 1)
            body(NB - 1, 1, NB // 2 - 1)
            body(NB, 0, NB // 2)

        def vbd_heads(i, c):
            rows, h0, ns = SLOTS[c]
            return Vbd[i][:, c, :, h0:h0 + ns, 0:HD]

        def nth(h, par, ahead):
            return h + (par + ahead) // 2 + 1

        def there(b):
            return not isinstance(b, int) or 0 <= b < NB

        @block.sync
        def _(sp):
            sp.dma_start(mk[:], mask).then_inc(ld_m, 16)
            sp.dma_start(msk8[:], bass.AP(tensor=mask.tensor, offset=mask.offset, ap=[[0, P], [J, NB], [1, J]])).then_inc(ld_m, 16)

            def load_x(b, par):
                ge(sp, g_xb, b - 1)
                ge(sp, v_xn[0], b - 1)
                sp.dma_start(xin[par][:], x[b].rearrange("(p t) d -> p t d", t=NT)).then_inc(ld_x[par], 16)

            def load_ctx(b, par):
                ge(sp, p_cT, b - 1)
                sp.dma_start(ctxin[par][:, 0:C], ctx[b]).then_inc(ld_ctx[par], 16)
                ge(sp, p_sT, NC * (b - 1))
                for g in range(2):
                    sp.dma_start(aug[par][32:33, g, :], mrow_d[b:b + 1, :] if isinstance(b, int) else mrow_d[bass.ds(b, 1), :]).then_inc(ld_mrow[par], 16)

            load_x(0, 0)
            load_x(1, 1)
            for k in range(KC):
                sp.dma_start(wq1[:, k, :], wqkv[k * P:(k + 1) * P, :]).then_inc(ld_w, 16)
            sp.dma_start(wo1[:], wout.rearrange("(k p) n -> p k n", p=P)).then_inc(ld_w, 16)
            sp.dma_start(wq2[:], wq.rearrange("(k p) n -> p k n", p=P)).then_inc(ld_w, 16)
            sp.dma_start(wo2[:], wo.rearrange("(k p) n -> p k n", p=P)).then_inc(ld_w, 16)
            sp.wait_ge(g_c, 1)
            for w2, w in ((wk2, wk), (wv2, wv)):
                sp.dma_start(w2[:, 0, :], w[0:P, :]).then_inc(ld_w, 16)
                sp.dma_start(w2[0:C - P, 1, :], w[P:C, :]).then_inc(ld_w, 16)
            sp.dma_start(bias[:], bass.AP(tensor=bout.tensor, offset=bout.offset, ap=[[0, P], [1, D]])).then_inc(ld_w, 16)
            sp.dma_start(W3[:, 0, :].rearrange("p (m i) -> p m i", m=FT), wgate.rearrange("(m p) i -> p m i", p=P)).then_inc(ld_w3, 16)
            sp.dma_start(W3[:, 1, :].rearrange("p (m i) -> p m i", m=FT), wup.rearrange("(m p) i -> p m i", p=P)).then_inc(ld_w3, 16)
            sp.dma_start(W3[:, 2, :].rearrange("p (m i) -> p m i", m=KC), wdown.rearrange("(m p) i -> p m i", p=P)).then_inc(ld_w3, 16)
            sp.wait_ge(v_c, 2)
            sp.dma_start(mrow_d, mkr[:]).then_inc(st_m, 16)
            sp.wait_ge(st_m, 16)
            sp.wait_ge(g_c, 11)
            load_ctx(0, 0)
            load_ctx(1, 1)

            def store_xn(b, par):
                sp.wait_ge(a_xn[2], b + 1)
                for k in range(KC):
                    sp.dma_start(xn_d[b][:, k, :], xn3T[:, k, :]).then_inc(st_xn, 16)

            def body(b, par, h):
                if there(b + 2) and not (isinstance(b, int) and b < 0):
                    load_x(b + 2, par)
                if there(b - 1):
                    sp.wait_ge(v_x2, b)
                    sp.dma_start(x2_d[b - 1], x2[1 - par][:].rearrange("p t d -> p (t d)")).then_inc(st_x2[1 - par], 16)
                    store_xn(b - 1, 1 - par)
                if there(b + 2) and not (isinstance(b, int) and b < 0):
                    load_ctx(b + 2, par)

            bodies(sp, body)
            for i in range(2):
                sp.wait_ge(st_x2[i], 16 * NB // 2)
            sp.wait_ge(st_xn, 16 * KC * NB)

        @block.gpsimd
        def _(gp):
            pool = nc.gpsimd
            pool.memset(wk2[:, 1, :], 0.0)
            pool.memset(wv2[:, 1, :], 0.0).then_inc(g_c, 1)
            pool.memset(ident[:], 0.0)
            pool.memset(identb[:], 0.0)
            pool.memset(HM[:], 1.0)
            pool.memset(HRM[:], 1.0)
            pool.memset(Sel[:], 0.0)
            pool.memset(aug[0][:], 0.0)
            pool.memset(aug[1][:], 0.0)
            pool.memset(maskrow1[:], 0.0)
            pool.memset(mtile[:], 0.0)
            pool.memset(mhalf[:], -0.5)
            pool.memset(epst[:], LN_EPS)
            pool.memset(vtok[:, :, :, P:P + 1], 1.0)
            for i in range(2):
                pool.memset(ctxin[i][:], 0.0)
            pool.memset(Vbd[0][:], 0.0)
            pool.memset(Vbd[1][:], 0.0).then_inc(g_c, 1)
            gp.wait_ge(g_c, 2)
            pool.affine_select(out=ident[:], in_=ident[:], compare_op=ALU.not_equal, fill=1.0, base=0,
                               pattern=[[-1, P]], channel_multiplier=1)
            pool.affine_select(out=identb[:], in_=identb[:], compare_op=ALU.not_equal, fill=1.0, base=0,
                               pattern=[[-1, P]], channel_multiplier=1)
            pool.affine_select(out=maskrow1[:], in_=maskrow1[:], compare_op=ALU.not_equal, fill=1.0, base=-32,
                               pattern=[[0, P]], channel_multiplier=1)
            pool.memset(mtile[:, :, 32:33], 1.0)
            for i in range(2):
                v = aug[i][:].rearrange("p g (h j) -> p g h j", h=HG)
                for g in range(2):
                    pool.affine_select(out=v[:, g], in_=v[:, g], compare_op=ALU.not_equal, fill=-1.0, base=-HG * g,
                                       pattern=[[-1, HG], [0, J]], channel_multiplier=1)
            pool.affine_select(out=HM[:], in_=HM[:], compare_op=ALU.is_ge, fill=0.0, base=0,
                               pattern=[[-HD, HG]], channel_multiplier=1).then_inc(g_c, 1)
            gp.wait_ge(g_c, 3)
            pool.affine_select(out=HM[:], in_=HM[:], compare_op=ALU.is_ge, fill=0.0, base=HD - 1,
                               pattern=[[HD, HG]], channel_multiplier=-1)
            for step in range(2):
                for c, (rows, h0, ns) in enumerate(SLOTS):
                    for g in range(2):
                        v = HRM[:, 2 * OFF[c] + g * ns:2 * OFF[c] + (g + 1) * ns]
                        if step == 0:
                            last = pool.affine_select(out=v, in_=v, compare_op=ALU.is_ge, fill=0.0, base=c * P - J * h0,
                                                      pattern=[[-J, ns]], channel_multiplier=1)
                        else:
                            last = pool.affine_select(out=v, in_=v, compare_op=ALU.is_ge, fill=0.0,
                                                      base=J * h0 + J - 1 - c * P, pattern=[[J, ns]],
                                                      channel_multiplier=-1)
                last.then_inc(g_c, 1)
                gp.wait_ge(g_c, 4 + step)
            for i in range(2):
                for c, (rows, h0, ns) in enumerate(SLOTS):
                    nh = min(ns, HG - h0)
                    pool.tensor_copy(Vbd[i][:, c, :, h0:h0 + nh, HD],
                                     HRM[:, 2 * OFF[c]:2 * OFF[c + 1]].rearrange("p (g s) -> p g s", g=2)[:, :, 0:nh])
            pool.tensor_copy(BM[:].rearrange("p (h i) -> p h i", h=HG), HM[:, :, None].broadcast_to([P, HG, HD])).then_inc(g_c, 1)
            gp.wait_ge(g_c, 6)
            for h in range(HG):
                v = Sel[:, h * J:(h + 1) * J]
                last = pool.affine_select(out=v, in_=v, compare_op=ALU.not_equal, fill=1.0, base=0,
                                          pattern=[[-1, J]], channel_multiplier=1)
            last.then_inc(g_c, 5)
            gp.wait_ge(v_c, 5)
            pool.partition_all_reduce(smx[:], sm[:], P, RMAX).then_inc(g_smx, 1)

            def ln_scale(i, b):
                gp.wait_ge(v_ag[i], b + 1)
                pool.tensor_tensor(ve[i][:], mv[i][:, :, 1], epst[:], ALU.add).then_inc(g_ve[i], 1)
                gp.wait_ge(g_ve[i], b + 1)
                ge(gp, v_xn[i], b)
                pool.tensor_tensor(rstd[i][:], ve[i][:], mhalf[:], ALU.pow).then_inc(g_rs[i], 1)

            def add_bias(b, par, use):
                gp.wait_ge(ld_x[par], 16 * use)
                ge(gp, v_x1, b)
                pool.tensor_tensor(xb[:], xin[par][:], bias[:, None, :].broadcast_to([P, NT, D]), ALU.add).then_inc(g_xb, 1)

            def keys(b, par):
                gp.wait_ge(v_kT, b + 1)
                ge(gp, p_sT, NC * (b - 1))
                kb = kTm[:, :, None, :].broadcast_to([P, 2, HG, J])
                hb = HM[:, None, :, None].broadcast_to([P, 2, HG, J])
                pool.tensor_tensor(KBD[par][:].rearrange("p g (h j) -> p g h j", h=HG), kb, hb, ALU.mult)
                pool.tensor_tensor(KBDb[par][:].rearrange("p g (h j) -> p g h j", h=HG), kb, hb, ALU.mult).then_inc(g_kbd, 1)

            ln_scale(0, 0)
            gp.wait_ge(ld_w, 16 * 10)

            def body(b, par, h):
                if there(b - 1):
                    ln_scale(2, b - 1)
                if there(b + 1):
                    add_bias(b + 1, 1 - par, nth(h, par, 1))
                    keys(b + 1, 1 - par)
                if there(b + 2):
                    ln_scale(0, b + 2)
                if there(b + 1):
                    ln_scale(1, b + 1)

            bodies(gp, body)

        @block.vector
        def _(dve):
            vec = nc.vector
            dve.wait_ge(ld_m, 32)
            vec.tensor_scalar(mkf[:], mk[:], -1.0, -MASKED, ALU.add, ALU.mult).then_inc(v_c, 1)
            dve.wait_ge(v_c, 1)
            vec.tensor_copy(mkr[:], mkf[:, None, :].broadcast_to([NB, HG, J])).then_inc(v_c, 1)

            def stats(i, b, src):
                ge(dve, v_xn[i], b)
                for t in range(NT):
                    last = vec.bn_stats(st[i][:, t, :], src[:, t, :])
                last.then_inc(v_st[i], 1)

            def aggregate(i, b):
                dve.wait_ge(v_st[i], b + 1)
                vec.tensor_copy(fence[:, i:i + 1], mhalf[:, 0:1])
                for t in range(NT):
                    last = vec.bn_aggr(mv[i][:, t, :], st[i][:, t, :])
                last.then_inc(v_ag[i], 1)

            def normalise(i, b, src, dst):
                dve.wait_ge(g_rs[i], b + 1)
                ge(dve, p_xn[i], b)
                for t in range(NT):
                    last = vec.tensor_scalar(dst[:, t, :], src[:, t, :], mv[i][:, t, 0:1], rstd[i][:, t:t + 1],
                                             ALU.subtract, ALU.mult)
                last.then_inc(v_xn[i], 1)

            dve.wait_ge(g_c, 2)
            dve.wait_ge(ld_x[0], 16)
            stats(0, 0, xin[0])
            aggregate(0, 0)
            dve.wait_ge(ld_w3, 48)
            vec.tensor_reduce(am[:], W3[:].rearrange("p w (n k) -> p (w n) k", k=BLOCK), AX.X, ALU.max,
                              apply_absolute_value=True).then_inc(v_c, 1)
            dve.wait_ge(v_c, 3)
            vec.tensor_scalar(s3[:], am[:], 1.0 / 7.0, SMALLEST, ALU.mult, ALU.max).then_inc(v_c, 1)
            dve.wait_ge(v_c, 4)
            vec.tensor_reduce(sm[:], s3[:].rearrange("p (w n) -> p w n", w=3), AX.X, ALU.max).then_inc(v_c, 1)
            normalise(0, 0, xin[0], xn1)
            vec.reciprocal(rs3[:], s3[:]).then_inc(v_c, 1)
            dve.wait_ge(v_c, 6)
            w3 = W3[:].rearrange("p w (n k) -> p (w n) k", k=BLOCK)
            rb = rs3[:, :, None].broadcast_to([P, 3 * WB, BLOCK])
            vec.tensor_tensor(w3, w3, rb, ALU.mult).then_inc(v_c, 1)
            dve.wait_ge(v_c, 7)
            vec.tensor_scalar(W3[:], W3[:], ROUND, -ROUND, ALU.add, ALU.add).then_inc(v_c, 1)
            dve.wait_ge(v_c, 8)
            vec.tensor_scalar(W3[:], W3[:], 7.0, -8.0, ALU.min, ALU.max).then_inc(v_c, 1)
            dve.wait_ge(g_smx, 1)
            vec.reciprocal(rsm[:], smx[:]).then_inc(v_c, 1)
            dve.wait_ge(v_c, 10)
            vec.tensor_scalar(wscale[:], smx[:], 1.0 / WTOP, None, ALU.mult)
            for w in range(3):
                last = vec.tensor_scalar(s3[:, w * WB:(w + 1) * WB], s3[:, w * WB:(w + 1) * WB], rsm[:, w:w + 1], WTOP,
                                         ALU.mult, ALU.mult)
            last.then_inc(v_c, 1)
            dve.wait_ge(v_c, 11)
            vec.tensor_tensor(w3, w3, s3[:, :, None].broadcast_to([P, 3 * WB, BLOCK]), ALU.mult).then_inc(v_c, 1)
            for n in range(3 * 3):
                w, f = n // 3, n % 3
                dve.wait_ge(a_wh, n + 1)
                vec.tensor_tensor(wl[:, w, f * 512:(f + 1) * 512], ps[:, n % 8, :], wh[:, w, f * 512:(f + 1) * 512],
                                  ALU.subtract).then_inc(v_wl, 1)

            dve.wait_ge(g_c, 11)

            def at_batch(ap, b):
                return ap[:, b:b + 1] if isinstance(b, int) else ap[:, bass.ds(b, 1)]

            def maxima(b, t):
                dve.wait_ge(p_s, 2 * b + t + 1)
                ge(dve, p_m, b)
                vec.tensor_reduce(mtile[:, t, 0:2 * B1].rearrange("p (k h) -> p k h", k=2),
                                  ps[:, 5:7, 0:B1 * J].rearrange("p k (h j) -> p k h j", j=J), AX.X, ALU.max)
                vec.tensor_reduce(mtile[:, t, 2 * B1:H], ps[:, 7, 0:(H - 2 * B1) * J].rearrange("p (h j) -> p h j", j=J),
                                  AX.X, ALU.max).then_inc(v_max, 1)

            def body(b, par, h):
                s, t_ = there(b + 1), there(b)
                if there(b - 1):
                    dve.wait_ge(p_out, b)
                    ge(dve, st_x2[1 - par], 16 * (nth(h, par, -1) - 1))
                    vec.tensor_tensor(x2[1 - par][:], ps[:, 4, :].rearrange("p (t d) -> p t d", t=NT), x1[1 - par][:], ALU.add).then_inc(v_x2, 1)
                    dve.wait_ge(v_x2, b)
                    stats(2, b - 1, x2[1 - par])
                    aggregate(2, b - 1)
                if t_:
                    dve.wait_ge(a_q2, b + 1)
                    ge(dve, p_s, 2 * b)
                    vec.tensor_copy(q2Tb[:], q2T[:]).then_inc(v_q2b, 1)
                if there(b - 1):
                    normalise(2, b - 1, x2[1 - par], xn3)
                if t_:
                    maxima(b, 0)
                if there(b - 1):
                    dve.wait_ge(v_xn[2], b)
                    vec.tensor_reduce(at_batch(xmax, b - 1), xn3[:], AX.XY, ALU.max, apply_absolute_value=True).then_inc(v_xm, 1)
                if s:
                    dve.wait_ge(p_kv, b + 2)
                    ge(dve, p_agg, b + 1)
                    vec.tensor_scalar(ktok[:, 1, :], ps[:, 2, 0:D], 0.0, None, ALU.max)
                    vec.tensor_copy(vtok[:, 1, :, 0:P], ps[:, 2, D:2 * D].rearrange("p (g c) -> p g c", g=2)).then_inc(v_kv, 1)
                if t_:
                    maxima(b, 1)
                if s:
                    dve.wait_ge(p_ckv, b + 2)
                    ge(dve, g_kbd, b + 1)
                    vec.tensor_tensor(kTm[:], ps[:, 4, 0:2 * J].rearrange("p (g j) -> p g j", g=2),
                                      (msk8[:, b + 1:b + 2, :] if isinstance(b, int) else msk8[:, bass.ds(b + 1, 1), :]).broadcast_to([P, 2, J]),
                                      ALU.mult).then_inc(v_kT, 1)
                    ge(dve, p_vr, b + 1)
                    vec.tensor_copy(vsb[:], ps[0:J, 4, 256:512]).then_inc(v_v, 1)
                    dve.wait_ge(p_agg, b + 2)
                    ge(dve, p_num, b + 1)
                    a = ps[:, 1, 0:2 * (P + 1)].rearrange("p (g c) -> p g c", g=2)
                    vec.tensor_tensor(kvbd[:, :, 0:P], a[:, :, 0:P], BM[:, None, :].broadcast_to([P, 2, P]), ALU.mult)
                    vec.scalar_tensor_tensor(out=kvbd[:, :, P:NG], in0=a[:, :, P:P + 1].broadcast_to([P, 2, HG]),
                                             scalar=ATT_EPS, in1=HM[:, None, :].broadcast_to([P, 2, HG]),
                                             op0=ALU.add, op1=ALU.mult).then_inc(v_bd, 1)
                if there(b + 2):
                    dve.wait_ge(ld_x[par], 16 * nth(h, par, 2))
                    stats(0, b + 2, xin[par])
                if s:
                    dve.wait_ge(p_num, b + 2)
                    ge(dve, v_o, b + 1)
                    vec.tensor_scalar(dz[:].rearrange("p t (g h) -> p t g h", g=2),
                                      ps[:, 0:3:2, 0:2 * NG].rearrange("p t (g c) -> p t g c", g=2)[:, :, :, P:NG],
                                      ATT_EPS, None, ALU.add).then_inc(v_dz, 1)
                    dve.wait_ge(v_dz, b + 2)
                    vec.reciprocal(zz[:], dz[:]).then_inc(v_z, 1)
                    dve.wait_ge(v_z, b + 2)
                    ge(dve, p_oT, b + 1)
                    for t in range(NT):
                        last = vec.tensor_tensor(
                            otok[:, t, :].rearrange("p (g h i) -> p g h i", g=2, h=HG),
                            ps[:, 2 * t, 0:2 * NG].rearrange("p (g c) -> p g c", g=2)[:, :, 0:P].rearrange("p g (h i) -> p g h i", h=HG),
                            zz[:, t, :].rearrange("p (g h) -> p g h", g=2)[:, :, :, None].broadcast_to([P, 2, HG, HD]), ALU.mult)
                    last.then_inc(v_o, 1)
                if there(b + 2):
                    aggregate(0, b + 2)
                if s:
                    dve.wait_ge(p_att, b + 2)
                    dve.wait_ge(g_xb, b + 2)
                    vec.tensor_tensor(x1[1 - par][:], ps[:, 0, :].rearrange("p (t d) -> p t d", t=NT), xb[:], ALU.add).then_inc(v_x1, 1)
                    dve.wait_ge(v_x1, b + 2)
                    stats(1, b + 1, x1[1 - par])
                    aggregate(1, b + 1)
                if there(b + 2):
                    normalise(0, b + 2, xin[par], xn1)
                if s:
                    normalise(1, b + 1, x1[1 - par], xn2)
                if t_:
                    dve.wait_ge(p_av, b + 1)
                    av = ps[:, 6:8, 0:2 * NG].rearrange("p t (h i) -> p t h i", i=HD + 1)
                    ge(dve, v_o2, b)
                    vec.reciprocal(rden[:], av[:, :, :, HD]).then_inc(v_rd, 1)
                    dve.wait_ge(v_rd, b + 1)
                    ge(dve, p_o2T, b)
                    vec.tensor_tensor(o2[:].rearrange("p t (h i) -> p t h i", h=H), av[:, :, :, 0:HD],
                                      rden[:, :, :, None].broadcast_to([P, NT, H, HD]), ALU.mult).then_inc(v_o2, 1)
                if s:
                    dve.wait_ge(p_vr, b + 2)
                    for c, (rows, h0, ns) in enumerate(SLOTS):
                        lo, hi = 2 * OFF[c], 2 * OFF[c + 1]
                        last = vec.tensor_tensor(
                            vbd_heads(1 - par, c),
                            ps[:, 4, lo * HD:hi * HD].rearrange("p (g s i) -> p g s i", g=2, i=HD),
                            HRM[:, lo:hi].rearrange("p (g s) -> p g s", g=2)[:, :, :, None].broadcast_to([P, 2, ns, HD]), ALU.mult)
                    last.then_inc(v_vbd, 1)

            bodies(dve, body)

        @block.scalar
        def _(act):
            sc = nc.scalar
            for n in range(3 * 3):
                w, f = n // 3, n % 3
                act.wait_ge(p_wT, n + 1)
                sc.activation(wh[:, w, f * 512:(f + 1) * 512], ps[:, n % 8, :], ACT.Copy).then_inc(a_wh, 1)

            def copy_xn(i, b, bank, dst):
                act.wait_ge(p_xn[i], b + 1)
                sc.activation(dst[:].rearrange("p k n -> p (k n)"), ps[:, bank, :], ACT.Copy).then_inc(a_xn[i], 1)

            def exponentials(b, c):
                rows = SLOTS[c][0]
                act.wait_ge(p_sT, NC * b + c + 1)
                sc.activation(expT[0:rows, c, :, :], ps[0:rows, (5, 6, 7, 4, 5)[c], :].rearrange("p (g n) -> p g n", g=2),
                              ACT.Exp).then_inc(a_e, 1)

            def body(b, par, h):
                s, t_ = there(b + 1), there(b)
                if t_:
                    ge(act, p_q2, b)
                    copy_xn(1, b, 3, xn2T)
                if s:
                    ge(act, p_kv, b + 1)
                    copy_xn(0, b + 1, 0, xn1T)
                if t_:
                    act.wait_ge(p_q2, b + 1)
                    ge(act, p_sT, NC * b)
                    ge(act, v_q2b, b)
                    sc.activation(q2T[:].rearrange("p k n -> p (k n)"), ps[:, 5, :], ACT.Copy, scale=float(HD) ** -0.5).then_inc(a_q2, 1)
                if s:
                    act.wait_ge(p_cT, b + 2)
                    ge(act, p_ckv, b + 1)
                    sc.activation(ctxT[:].rearrange("p k j -> p (k j)"), ps[:, 3, 0:2 * J], ACT.Copy).then_inc(a_cT, 1)
                    act.wait_ge(p_q, b + 2)
                    ge(act, p_num, b + 1)
                    sc.activation(qT[:].rearrange("p k n -> p (k n)"), ps[:, 1, :], ACT.Relu).then_inc(a_q, 1)
                    act.wait_ge(p_kv, b + 2)
                    ge(act, p_agg, b + 1)
                    sc.activation(ktok[:, 0, :], ps[:, 0, 0:D], ACT.Relu)
                    sc.activation(vtok[:, 0, :, 0:P], ps[:, 0, D:2 * D].rearrange("p (g c) -> p g c", g=2), ACT.Copy).then_inc(a_kv, 1)
                if there(b - 1):
                    ge(act, st_xn, 16 * KC * (b - 1))
                    copy_xn(2, b - 1, 3, xn3T)
                if t_:
                    act.wait_ge(p_m, b + 1)
                    sc.activation(mrow[:], ps[:, 3, 0:N // 2].bitcast(BF16), ACT.Copy).then_inc(a_m, 1)
                    ge(act, p_av, b)
                    for c in range(3):
                        exponentials(b, c)
                if s:
                    act.wait_ge(p_oT, b + 2)
                    ge(act, p_att, b + 1)
                    sc.activation(oT[:].rearrange("p k n -> p (k n)"), ps[:, 1, :], ACT.Copy).then_inc(a_oT, 1)
                if t_:
                    for c in range(3, NC):
                        exponentials(b, c)
                    act.wait_ge(p_o2T, b + 1)
                    ge(act, p_out, b)
                    sc.activation(o2T[:].rearrange("p k n -> p (k n)"), ps[:, 3, :], ACT.Copy).then_inc(a_o2T, 1)

            bodies(act, body)

        @block.tensor
        def _(pe):
            te = nc.tensor
            pe.wait_ge(g_c, 11)
            pe.wait_ge(v_c, 12)
            for n in range(3 * 3):
                w, f = n // 3, n % 3
                ge(pe, v_wl, n - 7)
                for q in range(4):
                    at = 4 * f + q
                    if w < 2:
                        k, m = at // FT, at % FT
                        src = W3[:, w, m * D + k * P:m * D + (k + 1) * P]
                    else:
                        k, m = at // KC, at % KC
                        src = W3[:, w, m * F + k * P:m * F + (k + 1) * P]
                    last = te.transpose(ps[:, n % 8, q * P:(q + 1) * P], src, ident[:])
                last.then_inc(p_wT, 1)
            pe.wait_ge(v_wl, 9)
            pe.wait_ge(ld_w, 16 * 10)

            def transpose_tiles(bank, src, s):
                for k in range(KC):
                    for t in range(NT):
                        last = te.transpose(ps[:, bank, k * N + t * P:k * N + (t + 1) * P], src[:, t, k * P:(k + 1) * P], ident[:])
                last.then_inc(s, 1)

            def scores(b, par, t):
                for bank, c0, g, h0, nh in ((5, 0, 0, 0, 6), (6, 0, 0, 6, 2), (6, 2 * J, 1, 0, 4), (7, 0, 1, 4, 4)):
                    o = ps[:, bank, c0:c0 + nh * J]
                    te.matmul(o, q2Tb[:, g, t * P:(t + 1) * P], KBDb[par][:, g, h0 * J:(h0 + nh) * J], start=True, stop=False)
                    last = te.matmul(o, maskrow1[:], aug[par][:, g, h0 * J:(h0 + nh) * J], start=False, stop=True)
                last.then_inc(p_s, 1)

            def shifted(b, par, c):
                rows, bank = SLOTS[c][0], (5, 6, 7, 4, 5)[c]
                for g in range(2):
                    o = ps[0:rows, bank, g * N:(g + 1) * N]
                    te.matmul(o, KBD[par][:, g, c * P:c * P + rows], q2T[:, g, :], start=True, stop=False)
                    last = te.matmul(o, aug[par][:, g, c * P:c * P + rows], mrow[:], start=False, stop=True)
                last.then_inc(p_sT, 1)

            def project(bank, src, w, s):
                for t in range(NT):
                    for k in range(KC):
                        last = te.matmul(ps[:, bank, t * D:(t + 1) * D], src[:, k, t * P:(t + 1) * P], w[:, k, :],
                                         start=(k == 0), stop=(k == KC - 1))
                last.then_inc(s, 1)

            def queries(bank, w, src, s):
                for m in range(KC):
                    for k in range(KC):
                        last = te.matmul(ps[:, bank, m * N:(m + 1) * N], w[:, k, m * P:(m + 1) * P], src[:, k, :],
                                         start=(k == 0), stop=(k == KC - 1))
                last.then_inc(s, 1)

            def body(b, par, h):
                s, t_ = there(b + 1), there(b)
                if t_:
                    pe.wait_ge(v_xn[1], b + 1)
                    ge(pe, a_o2T, b)
                    transpose_tiles(3, xn2, p_xn[1])
                if there(b - 1):
                    pe.wait_ge(a_o2T, b)
                    pe.wait_ge(v_vbd, b + 1) if t_ else None
                    project(4, o2T, wo2, p_out)
                if s:
                    pe.wait_ge(v_xn[0], b + 2)
                    ge(pe, v_x1, b + 1)
                    transpose_tiles(0, xn1, p_xn[0])
                if t_:
                    pe.wait_ge(a_xn[1], b + 1)
                    ge(pe, a_e, NC * b)
                    queries(5, wq2, xn2T, p_q2)
                if s:
                    pe.wait_ge(ld_ctx[1 - par], 16 * nth(h, par, 1))
                    te.transpose(ps[:, 3, 0:J], ctxin[1 - par][:, 0:P], ident[0:J, 0:J])
                    te.transpose(ps[:, 3, J:2 * J], ctxin[1 - par][:, P:2 * P], ident[0:J, 0:J]).then_inc(p_cT, 1)
                    pe.wait_ge(a_xn[0], b + 2)
                    ge(pe, a_oT, b + 1)
                    queries(1, wq1, xn1T, p_q)
                if t_:
                    pe.wait_ge(v_q2b, b + 1)
                    pe.wait_ge(g_kbd, b + 1)
                    pe.wait_ge(ld_mrow[par], 32 * nth(h, par, 0))
                    ge(pe, v_o2, b)
                    scores(b, par, 0)
                if s:
                    ge(pe, v_o, b + 1)
                    for t in range(NT):
                        for k in range(KC):
                            last = te.matmul(ps[:, 2 * t, :], xn1T[:, k, t * P:(t + 1) * P], wq1[:, k, D:3 * D],
                                             start=(k == 0), stop=(k == KC - 1))
                    last.then_inc(p_kv, 1)
                if there(b - 1):
                    pe.wait_ge(v_xn[2], b)
                    if s:
                        pe.wait_ge(a_cT, b + 2)
                    transpose_tiles(3, xn3, p_xn[2])
                if t_:
                    pe.wait_ge(v_max, 2 * b + 1)
                    scores(b, par, 1)
                if s:
                    pe.wait_ge(a_cT, b + 2)
                    ge(pe, v_x2, b)
                    for g in range(2):
                        for k in range(2):
                            te.matmul(ps[:, 4, g * J:(g + 1) * J], wk2[:, k, g * P:(g + 1) * P], ctxT[:, k, :],
                                      start=(k == 0), stop=(k == 1))
                    for k in range(2):
                        last = te.matmul(ps[0:J, 4, 256:512], ctxT[:, k, :], wv2[:, k, :], start=(k == 0), stop=(k == 1))
                    last.then_inc(p_ckv, 1)
                    pe.wait_ge(a_kv, b + 2)
                    pe.wait_ge(v_kv, b + 2)
                    for g in range(2):
                        for t in range(NT):
                            last = te.matmul(ps[:, 1, g * (P + 1):(g + 1) * (P + 1)], ktok[:, t, g * P:(g + 1) * P],
                                             vtok[:, t, g, :], start=(t == 0), stop=(t == NT - 1))
                    last.then_inc(p_agg, 1)
                if t_:
                    pe.wait_ge(v_max, 2 * b + 2)
                    ge(pe, a_xn[2], b)
                    for t in range(NT):
                        last = te.transpose(ps[:, 3, 0:N // 2].bitcast(BF16)[:, t * P:(t + 1) * P], mtile[:, t, :], identb[:])
                    last.then_inc(p_m, 1)
                if s:
                    pe.wait_ge(v_bd, b + 2)
                    for t in range(NT):
                        for g in range(2):
                            last = te.matmul(ps[:, 2 * t, g * NG:(g + 1) * NG], qT[:, g, t * P:(t + 1) * P], kvbd[:, g, :],
                                             start=True, stop=True)
                    last.then_inc(p_num, 1)
                if t_:
                    pe.wait_ge(a_m, b + 1)
                    for c in range(3):
                        shifted(b, par, c)
                if s:
                    pe.wait_ge(v_o, b + 2)
                    transpose_tiles(1, otok, p_oT)
                if t_:
                    if s:
                        pe.wait_ge(v_v, b + 2)
                    shifted(b, par, 3)
                    pe.wait_ge(a_e, NC * b + 1)
                    shifted(b, par, 4)
                if s:
                    pe.wait_ge(a_oT, b + 2)
                    project(0, oT, wo1, p_att)
                if t_:
                    pe.wait_ge(a_e, NC * (b + 1))
                    pe.wait_ge(v_vbd, b + 1)
                    for t in range(NT):
                        for g in range(2):
                            for c, (rows, h0, ns) in enumerate(SLOTS):
                                last = te.matmul(ps[:, 6 + t, g * NG:(g + 1) * NG], expT[0:rows, c, g, t * P:(t + 1) * P],
                                                 Vbd[par][0:rows, c, g].rearrange("p h i -> p (h i)"),
                                                 start=(c == 0), stop=(c == NC - 1))
                    last.then_inc(p_av, 1)
                if s:
                    pe.wait_ge(v_v, b + 2)
                    vg = vsb[:].rearrange("j (g c) -> j g c", g=2)
                    for c, (rows, h0, ns) in enumerate(SLOTS):
                        last = te.matmul(ps[:, 4, 2 * OFF[c] * HD:2 * OFF[c + 1] * HD], Sel[:, c * P:(c + 1) * P],
                                         vg[:, :, h0 * HD:(h0 + ns) * HD], start=True, stop=True)
                    last.then_inc(p_vr, 1)
                if t_:
                    pe.wait_ge(v_o2, b + 1)
                    transpose_tiles(3, o2, p_o2T)

            bodies(pe, body)


def feed_forward_phases(nc, top, ps, wh, wl, wscale, xmax, x2_d, xn_d, g_d, p_d, out, NB, NCH, FT, sb_in, sem_in):
    KC = 2
    D = KC * P
    FC = FT * CH
    NP = FT // 2
    BT = CH // (2 * P)
    keep, ksem = sb_in(top), sem_in(top)
    sc = keep("sc", [P, 16], F32)
    gmax = keep("gmax", [P, NCH * NP], F32)
    gtop = keep("gtop", [P, NCH * NP], F32)
    umax = keep("umax", [P, NCH * NP], F32)
    smax = keep("smax", [P, 3 * NCH], F32)
    pmax = keep("pmax", [P, NP * NCH], F32)
    xstack = ExitStack()
    R = sb_in(xstack)("R", [P, NCH, KC, 2, CH], F16)
    SX, KX, AG, AU, SG, KG, SU, KU, SS, CS, SO, KO, TD = range(13)

    def pair(n):
        return ps[:, 2 * (n % 4):2 * (n % 4) + 2, :]

    def chunks(eng, body):
        with eng.Fori(0, NCH // 2) as i:
            body(i * 2, 0)
            body(i * 2 + 1, 1)

    def tokens(n, k):
        r = R[:, n:n + 1, k] if isinstance(n, int) else R[:, bass.ds(n, 1), k]
        return r.rearrange("p n s c -> p (n s) c")

    def at(ap, n):
        return ap[:, n:n + 1] if isinstance(n, int) else ap[:, bass.ds(n, 1)]

    def scale_of(dve, done, count, largest, factor, s, k):
        vec = nc.vector
        if factor is None:
            vec.tensor_scalar(sc[:, s:s + 1], largest, 1.0 / QMAX16, SMALLEST, ALU.mult, ALU.max).then_inc(done, 1)
        else:
            vec.tensor_scalar(sc[:, s:s + 1], largest, sc[:, factor:factor + 1], 1.0 / QMAX16, ALU.mult, ALU.mult).then_inc(done, 1)
            count += 1
            dve.wait_ge(done, count)
            vec.tensor_scalar(sc[:, s:s + 1], sc[:, s:s + 1], SMALLEST, None, ALU.max).then_inc(done, 1)
        count += 1
        dve.wait_ge(done, count)
        vec.reciprocal(sc[:, k:k + 1], sc[:, s:s + 1]).then_inc(done, 1)
        count += 1
        dve.wait_ge(done, count)
        return count

    def times(dve, done, count, dst, a, b, c=None):
        if c is None:
            nc.vector.tensor_scalar(sc[:, dst:dst + 1], a, b, None, ALU.mult).then_inc(done, 1)
        else:
            nc.vector.tensor_scalar(sc[:, dst:dst + 1], a, b, c, ALU.mult, ALU.mult).then_inc(done, 1)
        dve.wait_ge(done, count + 1)
        return count + 1

    with ExitStack() as stack:
        sb, sem = sb_in(stack), sem_in(stack)
        xf = [sb(f"xf{i}", [P, KC, CH], F32) for i in range(2)]
        gs = [sb(f"gs{i}", [P, 2, CH], F32) for i in range(NP)]
        pm = sb("pm", [P, 1], F32)
        pa = sb("pa", [P, 1], F32)
        done, g_all, v_pm = sem("b_done"), sem("b_all"), sem("b_pm")
        ld = [sem(f"b_ld{i}") for i in range(2)]
        a_r, v_hi, v_r = sem("b_round"), sem("b_hi"), sem("b_lo")
        p_g, a_g, v_g = sem("b_pg"), sem("b_ag"), sem("b_vg")
        st_g = [sem(f"b_stg{j}") for j in range(NP)]
        p_u, v_u = sem("b_pu"), sem("b_vu")
        block = stack.enter_context(nc.Block())

        @block.sync
        def _(sp):
            def body(n, par):
                if not (isinstance(n, int) and n < 2):
                    sp.wait_ge(v_r, n - 1)
                for i in range(BT):
                    sp.dma_start(xf[par][:, :, i * 2 * P:(i + 1) * 2 * P], xn_d[n * BT + i]).then_inc(ld[par], 16)

            body(0, 0)
            body(1, 1)
            with sp.Fori(1, NCH // 2) as i:
                body(i * 2, 0)
                body(i * 2 + 1, 1)

        @block.gpsimd
        def _(gp):
            gp.wait_ge(v_pm, 1)
            nc.gpsimd.partition_all_reduce(pa[:], pm[:], P, RMAX).then_inc(g_all, 1)

        @block.vector
        def _(dve):
            vec = nc.vector
            vec.tensor_reduce(pm[:], xmax[:], AX.X, ALU.max).then_inc(v_pm, 1)
            dve.wait_ge(g_all, 1)
            c = scale_of(dve, done, 0, pa[:], None, SX, KX)
            c = times(dve, done, c, AG, wscale[:, 0:1], sc[:, SX:SX + 1])
            c = times(dve, done, c, AU, wscale[:, 1:2], sc[:, SX:SX + 1])
            assert c == 4

            def split(n, par):
                dve.wait_ge(a_r, n + 1)
                r = R[:, n:n + 1] if isinstance(n, int) else R[:, bass.ds(n, 1)]
                r = r.rearrange("p n k s c -> p (n k) s c")
                vec.tensor_scalar(r[:, :, 0, :], xf[par][:], -ROUND, None, ALU.add).then_inc(v_hi, 1)
                dve.wait_ge(v_hi, n + 1)
                vec.scalar_tensor_tensor(out=r[:, :, 1, :], in0=xf[par][:], scalar=-ROUND, in1=r[:, :, 0, :],
                                         op0=ALU.add, op1=ALU.subtract).then_inc(v_r, 1)

            def body(n, par, last):
                if not last:
                    split(n + 1, 1 - par)
                for j in range(NP):
                    dve.wait_ge(a_g, n * NP + j + 1)
                    vec.tensor_reduce(at(gtop, n * NP + j), gs[j][:], AX.XY, ALU.max)
                    vec.tensor_reduce(at(gmax, n * NP + j), gs[j][:], AX.XY, ALU.max,
                                      apply_absolute_value=True).then_inc(v_g, 1)
                for j in range(NP):
                    dve.wait_ge(p_u, n * NP + j + 1)
                    vec.tensor_reduce(at(umax, n * NP + j), pair(NP + j + 2 * NP * par), AX.XY, ALU.max,
                                      apply_absolute_value=True).then_inc(v_u, 1)

            split(0, 0)
            with dve.Fori(0, NCH // 2 - 1) as i:
                body(i * 2, 0, False)
                body(i * 2 + 1, 1, False)
            body(NCH - 2, 0, False)
            body(NCH - 1, 1, True)

        @block.scalar
        def _(act):
            def scale_x(n, par, use):
                act.wait_ge(ld[par], 16 * BT * use)
                nc.scalar.activation(xf[par][:], xf[par][:], ACT.Copy, scale=sc[:, KX:KX + 1], bias=ROUND).then_inc(a_r, 1)

            def body(n, par, i, peeled, last=False):
                if not last:
                    scale_x(n + 1, 1 - par, i + par + 1)
                for j in range(NP):
                    act.wait_ge(p_g, n * NP + j + 1)
                    if not peeled:
                        act.wait_ge(v_g, (n - 1) * NP + j + 1)
                        act.wait_ge(st_g[j], 16 * n)
                    nc.scalar.activation(gs[j][:], pair(j + 2 * NP * par), ACT.Copy).then_inc(a_g, 1)
                    act.wait_ge(a_g, n * NP + j + 1)
                    act.dma_start((g_d[n])[:, 2 * CH * j:2 * CH * (j + 1)], gs[j][:].rearrange("p a c -> p (a c)")).then_inc(st_g[j], 16)

            act.wait_ge(done, 4)
            scale_x(0, 0, 1)
            body(0, 0, 0, True)
            body(1, 1, 0, False)
            with act.Fori(1, NCH // 2 - 1) as i:
                body(i * 2, 0, i, False)
                body(i * 2 + 1, 1, i, False)
            body(NCH - 2, 0, NCH // 2 - 1, False)
            body(NCH - 1, 1, NCH // 2 - 1, False, True)
            for j in range(NP):
                act.wait_ge(st_g[j], 16 * NCH)

        @block.tensor
        def _(pe):
            def body(n, par, first):
                pe.wait_ge(v_r, n + 1)
                for w, freed, s in ((0, a_g, p_g), (1, v_u, p_u)):
                    for j in range(NP):
                        back = 2 * NP * par + NP * w + j - 4
                        self_w, self_j, self_n = (back // NP) % 2, back % NP, back // (2 * NP)
                        if not (first and back < 0):
                            pe.wait_ge(v_u if self_w else a_g, (n - par + self_n) * NP + self_j + 1)
                        for m in range(2):
                            o = pair(2 * NP * par + NP * w + j)[:, m, :]
                            for k in range(KC):
                                col = k * FT * P + (2 * j + m) * P
                                r = R[:, n:n + 1, k] if isinstance(n, int) else R[:, bass.ds(n, 1), k]
                                r = r.rearrange("p n s c -> p (n s) c")
                                for q, (lhs, part) in enumerate(((wh, 0), (wl, 0), (wh, 1))):
                                    last = nc.tensor.matmul(o, lhs[:, w, col:col + P], r[:, part, :],
                                                            start=(k == 0 and q == 0), stop=(k == KC - 1 and q == 2))
                        last.then_inc(s, 1)

            body(0, 0, True)
            body(1, 1, False)
            with pe.Fori(1, NCH // 2) as i:
                body(i * 2, 0, False)
                body(i * 2 + 1, 1, False)

    with ExitStack() as stack:
        sb, sem = sb_in(stack), sem_in(stack)
        gf = [sb(f"gf{i}", [P, FC // 3], F32) for i in range(2)]
        gq = [sb(f"gq{i}", [P, FC // 3], I16) for i in range(2)]
        sg = [sb(f"sg{i}", [P, FC // 3], F32) for i in range(2)]
        sq = [sb(f"sq{i}", [P, FC // 3], U16) for i in range(2)]
        pm = sb("pm2", [P, 3], F32)
        pa = sb("pa2", [P, 3], F32)
        tq = sb("tq", [P, 1], I16)
        ts = sb("ts", [P, 1], F32)
        tu = sb("tu", [P, 1], U16)
        tp = sb("tp", [P, 1], F32)
        below = sb("below", [P, 1], F32)
        flag = sb("flag", [P, 1], I32)
        top_s = sem("c_top")
        done, g_all, v_pm = sem("c_done"), sem("c_all"), sem("c_pm")
        ld = [sem(f"c_ld{i}") for i in range(2)]
        a_q, a_s, v_q, v_f, v_m = sem("c_q"), sem("c_s"), sem("c_vq"), sem("c_vf"), sem("c_vm")
        block = stack.enter_context(nc.Block())
        G3 = FC // 3
        NU = 3 * NCH

        def units(eng, body):
            body(0, 0, 0, True)
            body(1, 1, 0, True)
            with eng.Fori(1, NU // 2) as i:
                body(i * 2, 0, i, False)
                body(i * 2 + 1, 1, i, False)

        @block.sync
        def _(sp):
            def body(n, par):
                for j in range(3):
                    q = (3 * par + j)
                    if not (isinstance(n, int) and q < 2):
                        sp.wait_ge(a_q, 3 * n + j - 1)
                    sp.dma_start(gf[q % 2][:], (g_d[n])[:, j * G3:(j + 1) * G3]).then_inc(ld[q % 2], 16)

            sp.wait_ge(top_s, 7)
            with sp.If(sp.value_load(flag[0:1, 0:1]) > 0):
                body(0, 0)
                body(1, 1)
                with sp.Fori(1, NCH // 2) as i:
                    body(i * 2, 0)
                    body(i * 2 + 1, 1)

        @block.gpsimd
        def _(gp):
            gp.wait_ge(v_pm, 3)
            nc.gpsimd.partition_all_reduce(pa[:], pm[:], P, RMAX).then_inc(g_all, 1)

        @block.vector
        def _(dve):
            vec = nc.vector
            vec.tensor_reduce(pm[:, 0:1], gmax[:], AX.X, ALU.max).then_inc(v_pm, 1)
            vec.tensor_reduce(pm[:, 1:2], umax[:], AX.X, ALU.max).then_inc(v_pm, 1)
            vec.tensor_reduce(pm[:, 2:3], gtop[:], AX.X, ALU.max).then_inc(v_pm, 1)
            dve.wait_ge(g_all, 1)
            c = scale_of(dve, done, 0, pa[:, 0:1], AG, SG, KG)
            c = scale_of(dve, done, c, pa[:, 1:2], AU, SU, KU)
            c = times(dve, done, c, KG, sc[:, KG:KG + 1], sc[:, AG:AG + 1])
            c = times(dve, done, c, KU, sc[:, KU:KU + 1], sc[:, AU:AU + 1])
            assert c == 8
            dve.wait_ge(top_s, 2)
            vec.tensor_scalar(tu[:], ts[:], 65536.0, 65535.0, ALU.mult, ALU.min).then_inc(top_s, 1)
            dve.wait_ge(top_s, 3)
            vec.tensor_tensor(tp[:], tu[:], tq[:], ALU.mult).then_inc(top_s, 1)
            dve.wait_ge(top_s, 4)
            vec.tensor_scalar(below[:], tp[:], sc[:, SG:SG + 1], 1.0 / 65536.0, ALU.mult, ALU.mult).then_inc(top_s, 1)
            vec.tensor_scalar(smax[:], tp[:].broadcast_to([P, 3 * NCH]), 0.0, None, ALU.max).then_inc(top_s, 1)
            dve.wait_ge(top_s, 5)
            vec.tensor_scalar(flag[:], below[:], DIP, None, ALU.is_lt).then_inc(top_s, 1)

            def body(n, par, i, first):
                dve.wait_ge(a_s, n + 1)
                vec.tensor_scalar(sq[par][:], sg[par][:], 65536.0, 65535.0, ALU.mult, ALU.min).then_inc(v_q, 1)
                dve.wait_ge(v_q, n + 1)
                if not (isinstance(n, int) and n < 1):
                    dve.wait_ge(v_m, n)
                vec.tensor_tensor(sg[par][:], sq[par][:], gq[par][:], ALU.mult).then_inc(v_f, 1)
                dve.wait_ge(v_f, n + 1)
                vec.tensor_reduce(at(smax, n), sg[par][:], AX.X, ALU.max, apply_absolute_value=True).then_inc(v_m, 1)

            dve.wait_ge(top_s, 7)
            with dve.If(dve.value_load(flag[0:1, 0:1]) > 0):
                units(dve, body)

        @block.scalar
        def _(act):
            act.wait_ge(done, 8)
            nc.scalar.activation(tq[:], pa[:, 2:3], ACT.Copy, scale=sc[:, KG:KG + 1]).then_inc(top_s, 1)
            act.wait_ge(top_s, 1)
            nc.scalar.activation(ts[:], tq[:], ACT.Sigmoid, scale=sc[:, SG:SG + 1]).then_inc(top_s, 1)

            def body(n, par, i, first):
                act.wait_ge(ld[par], 16 * (i + 1))
                if not first:
                    act.wait_ge(v_m, n - 1)
                nc.scalar.activation(gq[par][:], gf[par][:], ACT.Copy, scale=sc[:, KG:KG + 1]).then_inc(a_q, 1)
                act.wait_ge(a_q, n + 1)
                nc.scalar.activation(sg[par][:], gq[par][:], ACT.Sigmoid, scale=sc[:, SG:SG + 1]).then_inc(a_s, 1)

            act.wait_ge(top_s, 7)
            with act.If(act.value_load(flag[0:1, 0:1]) > 0):
                units(act, body)

    with ExitStack() as stack:
        sb, sem = sb_in(stack), sem_in(stack)
        G = 2 * CH
        gf = [sb(f"df{i}", [P, G], F32) for i in range(3)]
        gq = [sb(f"dq{i}", [P, G], I16) for i in range(3)]
        sq = [sb(f"ds{i}", [P, G], U16) for i in range(2)]
        gz = [sb(f"dz{i}", [P, G], I16) for i in range(2)]
        uq = [sb(f"du{i}", [P, G], I16) for i in range(2)]
        pr = [sb(f"dp{i}", [P, G], F32) for i in range(3)]
        pm = sb("pm3", [P, 1], F32)
        pa = sb("pa3", [P, 1], F32)
        done, g_all, v_pm = sem("d_done"), sem("d_all"), sem("d_pm")
        ld, st = ([sem(f"d_{n}{i}") for i in range(3)] for n in ("ld", "st"))
        a_q, a_s, v_q, v_z = sem("d_q"), sem("d_s"), sem("d_vq"), sem("d_vz")
        p_u, a_u, v_p, v_m = sem("d_pu"), sem("d_au"), sem("d_vp"), sem("d_vm")
        block = stack.enter_context(nc.Block())
        NQ = 2 * NP
        NU = NP * NCH

        def steps(eng, body):
            for q in range(NQ):
                body(q, q, 0)
            with eng.Fori(1, NCH // 2 - 1) as i:
                for q in range(NQ):
                    body(i * NQ + q, q, i)
            for q in range(NQ):
                body(NU - NQ + q, q, NCH // 2 - 1)

        def before(u, n):
            return isinstance(u, int) and u < n

        @block.sync
        def _(sp):
            def store(u, q):
                sp.wait_ge(v_p, u + 1)
                sp.dma_start(p_d[u], pr[q % 3][:]).then_inc(st[q % 3], 16)

            def body(u, q, i):
                if not before(u, 3):
                    sp.wait_ge(v_q, u - 2)
                sp.dma_start(gf[q % 3][:], (g_d[i * 2 + q // NP])[:, (q % NP) * G:(q % NP + 1) * G]).then_inc(ld[q % 3], 16)
                if not before(u, 3):
                    store(u - 3, q)

            steps(sp, body)
            for q in range(3):
                store(NU - 3 + q, q)
            for i in range(3):
                sp.wait_ge(st[i], 16 * NU // 3)

        @block.gpsimd
        def _(gp):
            gp.wait_ge(v_pm, 1)
            nc.gpsimd.partition_all_reduce(pa[:], pm[:], P, RMAX).then_inc(g_all, 1)

        @block.vector
        def _(dve):
            vec = nc.vector
            vec.tensor_reduce(pm[:], smax[:], AX.X, ALU.max).then_inc(v_pm, 1)
            vec.tensor_scalar(sc[:, TD:TD + 1], sc[:, SG:SG + 1], 1.0 / 65536.0, None, ALU.mult).then_inc(done, 1)
            dve.wait_ge(done, 1)
            dve.wait_ge(g_all, 1)
            c = scale_of(dve, done, 1, pa[:], TD, SS, CS)
            c = times(dve, done, c, CS, sc[:, CS:CS + 1], sc[:, TD:TD + 1])

            def quantise_sigmoid(u, q):
                dve.wait_ge(a_s, u + 1)
                vec.tensor_scalar(sq[q % 2][:], gf[q % 3][:], 65536.0, 65535.0, ALU.mult, ALU.min).then_inc(v_q, 1)

            def reduce_product(u, q):
                dve.wait_ge(v_p, u + 1)
                vec.tensor_reduce(at(pmax, u), pr[q % 3][:], AX.X, ALU.max, apply_absolute_value=True).then_inc(v_m, 1)

            def body(u, q, i):
                par = q % 2
                if not (isinstance(u, int) and u == NU - 1):
                    quantise_sigmoid(u + 1, q + 1)
                dve.wait_ge(v_q, u + 1)
                vec.scalar_tensor_tensor(out=gz[par][:], in0=sq[par][:], scalar=sc[:, CS:CS + 1], in1=gq[q % 3][:],
                                         op0=ALU.mult, op1=ALU.mult).then_inc(v_z, 1)
                if not before(u, 1):
                    reduce_product(u - 1, q - 1)
                dve.wait_ge(v_z, u + 1)
                dve.wait_ge(a_u, u + 1)
                if not before(u, 3):
                    dve.wait_ge(st[q % 3], 16 * (i * 2 + q // 3))
                    dve.wait_ge(v_m, u - 2)
                vec.tensor_tensor(pr[q % 3][:], gz[par][:], uq[par][:], ALU.mult).then_inc(v_p, 1)

            quantise_sigmoid(0, 0)
            steps(dve, body)
            reduce_product(NU - 1, NQ - 1)

        @block.scalar
        def _(act):
            def body(u, q, i):
                par = q % 2
                act.wait_ge(ld[q % 3], 16 * (i * 2 + q // 3 + 1))
                if not before(u, 3):
                    act.wait_ge(v_z, u - 2)
                nc.scalar.activation(gq[q % 3][:], gf[q % 3][:], ACT.Copy, scale=sc[:, KG:KG + 1]).then_inc(a_q, 1)
                act.wait_ge(a_q, u + 1)
                nc.scalar.activation(gf[q % 3][:], gq[q % 3][:], ACT.Sigmoid, scale=sc[:, SG:SG + 1]).then_inc(a_s, 1)
                act.wait_ge(p_u, u + 1)
                if not before(u, 2):
                    act.wait_ge(v_p, u - 1)
                nc.scalar.activation(uq[par][:].rearrange("p (a c) -> p a c", a=2), pair(q % NP), ACT.Copy,
                                     scale=sc[:, KU:KU + 1]).then_inc(a_u, 1)

            steps(act, body)

        @block.tensor
        def _(pe):
            def body(u, q, i):
                if not before(u, NP):
                    pe.wait_ge(a_u, u - NP + 1)
                j = q % NP
                for m in range(2):
                    o = pair(j)[:, m, :]
                    for k in range(KC):
                        col = k * FT * P + (2 * j + m) * P
                        x3 = tokens(i * 2 + q // NP, k)
                        for pas, (lhs, part) in enumerate(((wh, 0), (wl, 0), (wh, 1))):
                            last = nc.tensor.matmul(o, lhs[:, 1, col:col + P], x3[:, part, :],
                                                    start=(k == 0 and pas == 0), stop=(k == KC - 1 and pas == 2))
                last.then_inc(p_u, 1)

            steps(pe, body)

    xstack.close()

    with ExitStack() as stack:
        sb, sem = sb_in(stack), sem_in(stack)
        G = FC // NP
        pf = [[sb(f"ef{i}_{h}", [P, G], F32) for h in range(NP)] for i in range(2)]
        oq = [sb(f"eq{i}", [P, FC], I16) for i in range(2)]
        oh = [sb(f"eh{i}", [P, FC], F16) for i in range(2)]
        ol = [sb(f"el{i}", [P, FC], F16) for i in range(2)]
        xr = [sb(f"ex{i}", [P, BT * 2, D], F32) for i in range(2)]
        xo = [sb(f"eo{i}", [P, BT * 2, D], F32) for i in range(2)]
        pm = sb("pm4", [P, 1], F32)
        pa = sb("pa4", [P, 1], F32)
        done, g_all, v_pm = sem("e_done"), sem("e_all"), sem("e_pm")
        ld = [[sem(f"e_ld{i}_{h}") for h in range(NP)] for i in range(2)]
        ldx, st = ([sem(f"e_{n}{i}") for i in range(2)] for n in ("ldx", "st"))
        v_q, a_h, v_l, p_o, v_o = sem("e_vq"), sem("e_ah"), sem("e_vl"), sem("e_po"), sem("e_vo")
        block = stack.enter_context(nc.Block())

        def before(n, m):
            return isinstance(n, int) and n < m

        def steps(eng, body):
            body(0, 0, 0)
            body(1, 1, 0)
            with eng.Fori(1, NCH // 2 - 1) as i:
                body(i * 2, 0, i)
                body(i * 2 + 1, 1, i)
            body(NCH - 2, 0, NCH // 2 - 1)
            body(NCH - 1, 1, NCH // 2 - 1)

        @block.sync
        def _(sp):
            def body(n, par, i):
                for h in range(NP):
                    if not before(n, 2):
                        sp.wait_ge(v_q, NP * (n - 2) + h + 1)
                    sp.dma_start(pf[par][h][:], p_d[NP * n + h]).then_inc(ld[par][h], 16)
                if not before(n, 1):
                    load_x(n - 1, 1 - par)

            def load_x(n, par):
                if not before(n, 2):
                    sp.wait_ge(v_o, n - 1)
                for k in range(BT):
                    sp.dma_start(xr[par][:, 2 * k:2 * k + 2, :], x2_d[BT * n + k].rearrange("p (t d) -> p t d", t=2)).then_inc(ldx[par], 16)

            steps(sp, body)
            load_x(NCH - 1, 1)

        @block.gpsimd
        def _(gp):
            gp.wait_ge(v_pm, 1)
            nc.gpsimd.partition_all_reduce(pa[:], pm[:], P, RMAX).then_inc(g_all, 1)

        @block.scalar
        def _(act):
            def high(n, par):
                for h in range(NP):
                    act.wait_ge(v_q, NP * n + h + 1)
                    if h == 0 and not before(n, 2):
                        act.wait_ge(p_o, n - 1)
                    nc.scalar.activation(oh[par][:, h * G:(h + 1) * G], oq[par][:, h * G:(h + 1) * G], ACT.Copy).then_inc(a_h, 1)

            def store(n, par):
                act.wait_ge(v_o, n + 1)
                for k in range(BT):
                    act.dma_start(out[BT * n + k].rearrange("(p t) d -> p t d", t=2), xo[par][:, 2 * k:2 * k + 2, :]).then_inc(st[par], 16)

            def body(n, par, i):
                high(n, par)
                if not before(n, 2):
                    store(n - 2, par)

            steps(act, body)
            store(NCH - 2, 0)
            store(NCH - 1, 1)
            for i in range(2):
                act.wait_ge(st[i], 16 * BT * NCH // 2)

        @block.vector
        def _(dve):
            vec = nc.vector
            vec.tensor_reduce(pm[:], pmax[:], AX.X, ALU.max).then_inc(v_pm, 1)
            vec.tensor_scalar(sc[:, TD:TD + 1], sc[:, SS:SS + 1], sc[:, SU:SU + 1], None, ALU.mult).then_inc(done, 1)
            dve.wait_ge(done, 1)
            dve.wait_ge(g_all, 1)
            c = scale_of(dve, done, 1, pa[:], TD, SO, KO)
            c = times(dve, done, c, KO, sc[:, KO:KO + 1], sc[:, TD:TD + 1])
            c = times(dve, done, c, TD, sc[:, SO:SO + 1], wscale[:, 2:3])

            def finish(n, par, use):
                dve.wait_ge(p_o, n + 1)
                dve.wait_ge(ldx[par], 16 * BT * use)
                o = ps[:, 2 * par:2 * par + 2, :].rearrange("p a c -> p (a c)")
                xf = xr[par][:].rearrange("p a c -> p (a c)")
                if not before(n, 2):
                    dve.wait_ge(st[par], 16 * BT * (use - 1))
                vec.scalar_tensor_tensor(out=xo[par][:].rearrange("p a c -> p (a c)"), in0=o, scalar=sc[:, TD:TD + 1], in1=xf, op0=ALU.mult, op1=ALU.add).then_inc(v_o, 1)

            def body(n, par, i):
                for h in range(NP):
                    dve.wait_ge(ld[par][h], 16 * (i + 1))
                    if h == 0 and not before(n, 2):
                        dve.wait_ge(a_h, NP * (n - 1))
                        dve.wait_ge(v_l, NP * (n - 1))
                    vec.tensor_scalar(oq[par][:, h * G:(h + 1) * G], pf[par][h][:], sc[:, KO:KO + 1], None, ALU.mult).then_inc(v_q, 1)
                if not before(n, 2):
                    finish(n - 2, par, i)
                for h in range(NP):
                    dve.wait_ge(a_h, NP * n + h + 1)
                    if h == 0 and not before(n, 2):
                        dve.wait_ge(p_o, n - 1)
                    vec.tensor_tensor(ol[par][:, h * G:(h + 1) * G], oq[par][:, h * G:(h + 1) * G], oh[par][:, h * G:(h + 1) * G],
                                      ALU.subtract).then_inc(v_l, 1)

            steps(dve, body)
            finish(NCH - 2, 0, NCH // 2)
            finish(NCH - 1, 1, NCH // 2)

        @block.tensor
        def _(pe):
            def body(n, par, i):
                pe.wait_ge(v_l, NP * (n + 1))
                if not before(n, 2):
                    pe.wait_ge(v_o, n - 1)
                for t in range(CH // P):
                    o = ps[:, 2 * par + t // 2, (t % 2) * D:(t % 2 + 1) * D]
                    for k in range(FT):
                        w0 = k * D
                        c0 = k * CH + t * P
                        for q, (lhs, rhs) in enumerate(((oh, wh), (oh, wl), (ol, wh))):
                            last = nc.tensor.matmul(o, lhs[par][:, c0:c0 + P], rhs[:, 2, w0:w0 + D],
                                                    start=(k == 0 and q == 0), stop=(k == FT - 1 and q == 2))
                last.then_inc(p_o, 1)

            steps(pe, body)


_INS = ["x", "ctx_768", "mask_BxS2_bf1", "L0_attn_Wqkv", "L0_attn_Wout", "L0_attn_bout", "L0_xattn_Wq", "L0_xattn_Wk",
        "L0_xattn_Wv", "L0_xattn_Wo", "L0_ffn_w_gate", "L0_ffn_w_up", "L0_ffn_w_down"]


def kernel(**inputs):
    import numpy as np
    import concourse.bacc as bacc
    from concourse.bass_utils import run_bass_kernel_spmd

    nc = bacc.Bacc("TRN2", target_bir_lowering=False, num_devices=1)
    arrays, args = {}, []
    for name in _INS:
        a = np.ascontiguousarray(inputs[name])
        if a.dtype == np.bool_:
            a = a.view(np.uint8)
        arrays[f"in_{name}"] = a
        args.append(nc.dram_tensor(f"in_{name}", a.shape, mybir.dt.from_np(a.dtype), kind="ExternalInput").ap())
    shape = tuple(inputs["x"].shape)
    args.append(nc.dram_tensor("out_x", shape, F32, kind="ExternalOutput").ap())
    decoder_layer(nc, *args)
    r = run_bass_kernel_spmd(nc, [arrays], core_ids=[0])
    return r.results[0]["out_x"]
```

```python
from contextlib import ExitStack

import concourse.bass as bass
from concourse import mybir

F32 = mybir.dt.float32
BF16 = mybir.dt.bfloat16
F16 = mybir.dt.float16
I16 = mybir.dt.int16
I32 = mybir.dt.int32
U16 = mybir.dt.uint16
U8 = mybir.dt.uint8
ALU = mybir.AluOpType
ACT = mybir.ActivationFunctionType
AX = mybir.AxisListType
RMAX = bass.bass_isa.ReduceOp.max

P = 128
H = 16
HG = 8
HD = 16
LN_EPS = 1e-5
ATT_EPS = 1e-6
BLOCK = 32
ROUND = 12582912.0
QMAX16 = 32767.0
SMALLEST = 1e-12
MASKED = -(2.0 ** 127)
WTOP = 4096.0
WUP = 64.0
NUP = 1024.0
VUP = 64.0
PASSES = ((0, 0), (0, 1), (1, 0))
DIP = 0.3
CH = 512


def chunk_slots(J):
    out, at = [], 0
    while at < HG * J:
        rows = min(P, HG * J - at)
        first, last = at // J, (at + rows - 1) // J
        out.append((rows, first, last - first + 1))
        at += rows
    return out


def decoder_layer(nc, x, ctx, mask, wqkv, wout, bout, wq, wk, wv, wo, wgate, wup, wdown, out):
    NB, N, D = x.shape
    J, C = ctx.shape[1], ctx.shape[2]
    F = wgate.shape[0]
    T = NB * N
    NT = N // P
    KC = D // P
    FT = F // P
    NCH = T // CH
    HJ = HG * J
    SLOTS = chunk_slots(J)
    NC = len(SLOTS)
    assert NT == 2 and KC == 2 and D == H * HD and J <= P and C <= 2 * P and NB % 4 == 0 and NB >= 12

    x2_d = nc.dram_tensor("x2_scratch", (NB, P, NT * D), F32).ap()
    xn_d = nc.dram_tensor("xn_scratch", (NB, P, KC, N), F32).ap()
    g_d = nc.dram_tensor("gate_scratch", (NCH, P, FT * CH), F32).ap()
    p_d = nc.dram_tensor("product_scratch", (NCH * FT // 2, P, 2 * CH), F32).ap()
    mrow_d = nc.dram_tensor("maskrow_scratch", (NB, HJ), BF16).ap()

    top = ExitStack()
    with top:
        def sb_in(stack):
            return lambda name, shape, dt: stack.enter_context(nc.sbuf_tensor(name, shape, dt))

        def sem_in(stack):
            return lambda name: stack.enter_context(nc.semaphore(name))

        keep = sb_in(top)
        ps = top.enter_context(nc.psum_tensor("ps", [P, 8, 512], F32))
        wh = keep("wh", [P, 3, FT * D], F16)
        wl = keep("wl", [P, 3, FT * D], F16)
        wscale = keep("wscale", [P, 3], F32)
        xmax = keep("xmax", [P, NB], F32)

        attention_phase(nc, ps, wh, wl, wscale, xmax, x2_d, xn_d, mrow_d, x, ctx, mask, wqkv, wout, bout,
                        wq, wk, wv, wo, wgate, wup, wdown, sb_in, sem_in)
        feed_forward_phases(nc, top, ps, wh, wl, wscale, xmax, x2_d, xn_d, g_d, p_d, out, NB, NCH, FT, sb_in, sem_in)


def attention_phase(nc, ps, wh, wl, wscale, xmax, x2_d, xn_d, mrow_d, x, ctx, mask, wqkv, wout, bout,
                    wq, wk, wv, wo, wgate, wup, wdown, sb_in, sem_in):
    NB, N, D = x.shape
    J, C = ctx.shape[1], ctx.shape[2]
    F = wgate.shape[0]
    NT, KC, FT = N // P, D // P, F // P
    HJ = HG * J
    SLOTS = chunk_slots(J)
    NC = len(SLOTS)
    OFF = [sum(n for _, _, n in SLOTS[:c]) for c in range(NC + 1)]
    NSLOT = OFF[NC]
    HJP = NC * P
    WB = FT * D // BLOCK
    NG = P + HG
    B1 = 6 if J * 6 <= 512 else 512 // J
    assert B1 == 6 and NC == 5
    QSCALE = VUP * float(HD) ** -0.5 / (WUP * NUP)
    stack = ExitStack()
    with stack:
        sb, sem = sb_in(stack), sem_in(stack)
        ident = sb("ident", [P, P], F32)
        identb = sb("identb", [P, P], BF16)
        HM = sb("HM", [P, HG], F32)
        BM = sb("BM", [P, P], F32)
        HRM = sb("HRM", [P, 2 * NSLOT], F32)
        Sel = sb("Sel", [J, HJP], F32)
        maskrow1 = sb("maskrow1", [P, P], BF16)
        WA = 6 * KC * D
        wa = sb("wa", [P, WA], F32)
        wah = sb("wah", [P, WA], F16)
        wal = sb("wal", [P, WA], F16)
        wk2 = sb("wk2", [P, 2, D], F32)
        wv2 = sb("wv2", [P, 2, D], F32)
        bias = sb("bias", [P, D], F32)
        msk8 = sb("msk8", [P, NB, J], U8)
        mk = sb("mk", [NB, J], U8)
        mkf = sb("mkf", [NB, J], F32)
        mkr = sb("mkr", [NB, HG, J], BF16)
        W3 = sb("W3", [P, 3, FT * D], F32)
        am = sb("am", [P, 3 * WB], F32)
        s3 = sb("s3", [P, 3 * WB], F32)
        rs3 = sb("rs3", [P, 3 * WB], F32)
        sm = sb("sm", [P, 3], F32)
        smx = sb("smx", [P, 3], F32)
        rsm = sb("rsm", [P, 3], F32)
        mhalf = sb("mhalf", [P, NT], F32)
        epst = sb("epst", [P, NT], F32)
        fence = sb("fence", [P, 3], F32)
        one = sb("one", [P, 2], F32)

        xin = [sb(f"xin{i}", [P, NT, D], F32) for i in range(2)]
        ctxin = [sb(f"ctxin{i}", [J, 2 * P], F32) for i in range(2)]
        aug = [sb(f"aug{i}", [P, 2, HJ], BF16) for i in range(2)]
        st = [sb(f"st{i}", [P, NT, 6], F32) for i in range(3)]
        mv = [sb(f"mv{i}", [P, NT, 2], F32) for i in range(3)]
        ve = [sb(f"ve{i}", [P, NT], F32) for i in range(3)]
        rstd = [sb(f"rstd{i}", [P, NT], F32) for i in range(3)]
        xn1 = sb("xn1", [P, NT, D], F32)
        xn2 = sb("xn2", [P, NT, D], F32)
        xn3 = sb("xn3", [P, NT, D], F32)
        xn1T = [sb(f"xn1T{i}", [P, KC, N], F16) for i in range(2)]
        xn2T = [sb(f"xn2T{i}", [P, KC, N], F16) for i in range(2)]
        xn3T = sb("xn3T", [P, KC, N], F32)
        qT = sb("qT", [P, KC, N], F32)
        ktok = sb("ktok", [P, NT, D], F32)
        vtok = sb("vtok", [P, NT, 2, P + 1], F32)
        kvbd = sb("kvbd", [P, 2, NG], F32)
        dz = sb("dz", [P, NT, H], F32)
        zz = sb("zz", [P, NT, H], F32)
        otok = sb("otok", [P, NT, D], F32)
        oT = [sb(f"oT{i}", [P, KC, N], F16) for i in range(2)]
        xb = sb("xb", [P, NT, D], F32)
        x1 = [sb(f"x1_{i}", [P, NT, D], F32) for i in range(2)]
        ctxT = sb("ctxT", [P, 2, J], F32)
        kTm = sb("kTm", [P, 2, J], F32)
        vsb = sb("vsb", [J, D], F32)
        kh = sb("kh", [P, 2, J], F16)
        kl = sb("kl", [P, 2, J], F16)
        KBD = [[sb(f"KBD{i}_{part}", [P, 2, HJ], F16) for part in range(2)] for i in range(2)]
        Vbd = [sb(f"Vbd{i}", [P, NC, 2, HG, HD + 1], F32) for i in range(2)]
        q2T = [sb(f"q2T{i}", [P, KC, N], F16) for i in range(2)]
        mtile = sb("mtile", [P, NT, P], BF16)
        mrow = sb("mrow", [P, N], BF16)
        expT = sb("expT", [P, NC, 2, N], F32)
        rden = sb("rden", [P, NT, H], F32)
        o2 = sb("o2", [P, NT, D], F32)
        o2T = [sb(f"o2T{i}", [P, KC, N], F16) for i in range(2)]
        x2 = [sb(f"x2_{i}", [P, NT, D], F32) for i in range(2)]

        ld_w = sem("ld_w")
        ld_w3 = [sem(f"ld_w3{w}") for w in range(3)]
        ld_m = sem("ld_m")
        g_c = sem("g_c")
        v_c = sem("v_c")
        v_w = sem("v_w")
        v_sm = sem("v_sm")
        v_w3 = sem("v_w3")
        g_smx = sem("g_smx")
        p_wT = sem("p_wT")
        a_wh = sem("a_wh")
        v_wl = sem("v_wl")
        st_m = sem("st_m")
        ld_x, ld_ctx, ld_mrow = ([sem(f"{n}{i}") for i in range(2)] for n in ("ld_x", "ld_ctx", "ld_mrow"))
        st_x2, st_xn = [sem(f"st_x2{i}") for i in range(2)], sem("st_xn")
        v_st = [sem(f"v_st{i}") for i in range(3)]
        v_ag = [sem(f"v_ag{i}") for i in range(3)]
        g_ve = [sem(f"g_ve{i}") for i in range(3)]
        g_rs = [sem(f"g_rs{i}") for i in range(3)]
        v_xn = [sem(f"v_xn{i}") for i in range(3)]
        p_xn = [sem(f"p_xn{i}") for i in range(3)]
        a_xn = [sem(f"a_xn{i}") for i in range(3)]
        p_q, a_q = sem("p_q"), sem("a_q")
        p_kv, a_kv, v_kv = sem("p_kv"), sem("a_kv"), sem("v_kv")
        p_agg, v_bd = sem("p_agg"), sem("v_bd")
        p_num, v_dz, v_z, v_o = sem("p_num"), sem("v_dz"), sem("v_z"), sem("v_o")
        p_oT, a_oT = sem("p_oT"), sem("a_oT")
        p_att, g_xb, v_x1 = sem("p_att"), sem("g_xb"), sem("v_x1")
        p_cT, a_cT = sem("p_cT"), sem("a_cT")
        p_ckv, v_kT, v_v, g_kbd = sem("p_ckv"), sem("v_kT"), sem("v_v"), sem("g_kbd")
        p_vr, v_vbd = sem("p_vr"), sem("v_vbd")
        p_q2, a_q2, v_q2l = sem("p_q2"), sem("a_q2"), sem("v_q2l")
        a_wa, v_wa = sem("a_wa"), sem("v_wa")
        v_xl = [sem(f"v_xl{i}") for i in range(2)]
        v_oTl, v_o2Tl = sem("v_oTl"), sem("v_o2Tl")
        g_k = sem("g_k")
        p_s, v_max = sem("p_s"), sem("v_max")
        p_m, a_m = sem("p_m"), sem("a_m")
        p_sT, a_e = sem("p_sT"), sem("a_e")
        p_av, v_rd, v_o2 = sem("p_av"), sem("v_rd"), sem("v_o2")
        p_o2T, a_o2T = sem("p_o2T"), sem("a_o2T")
        p_out, v_x2 = sem("p_out"), sem("v_x2")

        block = stack.enter_context(nc.Block())

        def ge(eng, s, value):
            if isinstance(value, int) and value <= 0:
                return
            eng.wait_ge(s, value)

        def bodies(eng, body):
            body(-1, 1, -1)
            body(0, 0, 0)
            body(1, 1, 0)
            with eng.Fori(1, NB // 2 - 1) as i:
                body(i * 2, 0, i)
                body(i * 2 + 1, 1, i)
            body(NB - 2, 0, NB // 2 - 1)
            body(NB - 1, 1, NB // 2 - 1)
            body(NB, 0, NB // 2)

        def vbd_heads(i, c):
            rows, h0, ns = SLOTS[c]
            return Vbd[i][:, c, :, h0:h0 + ns, 0:HD]

        def nth(h, par, ahead):
            return h + (par + ahead) // 2 + 1

        def there(b):
            return not isinstance(b, int) or 0 <= b < NB

        @block.sync
        def _(sp):
            sp.dma_start(mk[:], mask).then_inc(ld_m, 16)
            sp.dma_start(msk8[:], bass.AP(tensor=mask.tensor, offset=mask.offset, ap=[[0, P], [J, NB], [1, J]])).then_inc(ld_m, 16)

            def load_x(b, par):
                ge(sp, g_xb, b - 1)
                ge(sp, v_xn[0], b - 1)
                sp.dma_start(xin[par][:], x[b].rearrange("(p t) d -> p t d", t=NT)).then_inc(ld_x[par], 16)

            def load_ctx(b, par):
                ge(sp, p_cT, b - 1)
                sp.dma_start(ctxin[par][:, 0:C], ctx[b]).then_inc(ld_ctx[par], 16)
                ge(sp, p_sT, NC * (b - 1))
                for g in range(2):
                    sp.dma_start(aug[par][32:33, g, :], mrow_d[b:b + 1, :] if isinstance(b, int) else mrow_d[bass.ds(b, 1), :]).then_inc(ld_mrow[par], 16)

            load_x(0, 0)
            for n, (w, tiles) in enumerate(((wgate, FT), (wup, FT), (wdown, KC))):
                sp.dma_start(W3[:, n, :].rearrange("p (m i) -> p m i", m=tiles), w.rearrange("(m p) i -> p m i", p=P)).then_inc(ld_w3[n], 16)
            for k in range(KC):
                sp.dma_start(wa[:, k * 3 * D:(k + 1) * 3 * D], wqkv[k * P:(k + 1) * P, :]).then_inc(ld_w, 16)
            for n, w in enumerate((wout, wq, wo)):
                sp.dma_start(wa[:, (3 + n) * KC * D:(4 + n) * KC * D].rearrange("p (k n) -> p k n", k=KC),
                             w.rearrange("(k p) n -> p k n", p=P)).then_inc(ld_w, 16)
            sp.wait_ge(g_c, 1)
            for w2, w in ((wk2, wk), (wv2, wv)):
                sp.dma_start(w2[:, 0, :], w[0:P, :]).then_inc(ld_w, 16)
                sp.dma_start(w2[0:C - P, 1, :], w[P:C, :]).then_inc(ld_w, 16)
            sp.dma_start(bias[:], bass.AP(tensor=bout.tensor, offset=bout.offset, ap=[[0, P], [1, D]])).then_inc(ld_w, 16)
            load_x(1, 1)
            sp.wait_ge(v_c, 2)
            sp.dma_start(mrow_d, mkr[:]).then_inc(st_m, 16)
            sp.wait_ge(st_m, 16)
            sp.wait_ge(g_c, 11)
            load_ctx(0, 0)
            load_ctx(1, 1)

            def store_xn(b, par):
                sp.wait_ge(a_xn[2], b + 1)
                for k in range(KC):
                    sp.dma_start(xn_d[b][:, k, :], xn3T[:, k, :]).then_inc(st_xn, 16)

            def body(b, par, h):
                if there(b + 2) and not (isinstance(b, int) and b < 0):
                    load_x(b + 2, par)
                if there(b - 1):
                    sp.wait_ge(v_x2, b)
                    sp.dma_start(x2_d[b - 1], x2[1 - par][:].rearrange("p t d -> p (t d)")).then_inc(st_x2[1 - par], 16)
                    store_xn(b - 1, 1 - par)
                if there(b + 2) and not (isinstance(b, int) and b < 0):
                    load_ctx(b + 2, par)

            bodies(sp, body)
            for i in range(2):
                sp.wait_ge(st_x2[i], 16 * (NB // 2 + 1))
            sp.wait_ge(st_xn, 16 * KC * NB)

        @block.gpsimd
        def _(gp):
            pool = nc.gpsimd
            pool.memset(wk2[:, 1, :], 0.0)
            pool.memset(wv2[:, 1, :], 0.0).then_inc(g_c, 1)
            pool.memset(ident[:], 0.0)
            pool.memset(identb[:], 0.0)
            pool.memset(HM[:], 1.0)
            pool.memset(HRM[:], 1.0)
            pool.memset(Sel[:], 0.0)
            pool.memset(aug[0][:], 0.0)
            pool.memset(aug[1][:], 0.0)
            pool.memset(maskrow1[:], 0.0)
            pool.memset(mtile[:], 0.0)
            pool.memset(mhalf[:], -0.5).then_inc(st_x2[0], 16)
            pool.memset(epst[:], LN_EPS).then_inc(st_x2[1], 16)
            pool.memset(one[:], 1.0)
            pool.memset(vtok[:, :, :, P:P + 1], 1.0)
            for i in range(2):
                pool.memset(ctxin[i][:], 0.0)
            pool.memset(Vbd[0][:], 0.0)
            pool.memset(Vbd[1][:], 0.0).then_inc(g_c, 1)
            gp.wait_ge(g_c, 2)
            pool.affine_select(out=ident[:], in_=ident[:], compare_op=ALU.not_equal, fill=1.0, base=0,
                               pattern=[[-1, P]], channel_multiplier=1)
            pool.affine_select(out=identb[:], in_=identb[:], compare_op=ALU.not_equal, fill=1.0, base=0,
                               pattern=[[-1, P]], channel_multiplier=1)
            pool.affine_select(out=maskrow1[:], in_=maskrow1[:], compare_op=ALU.not_equal, fill=1.0, base=-32,
                               pattern=[[0, P]], channel_multiplier=1)
            pool.memset(mtile[:, :, 32:33], 1.0)
            for i in range(2):
                v = aug[i][:].rearrange("p g (h j) -> p g h j", h=HG)
                for g in range(2):
                    pool.affine_select(out=v[:, g], in_=v[:, g], compare_op=ALU.not_equal, fill=-1.0, base=-HG * g,
                                       pattern=[[-1, HG], [0, J]], channel_multiplier=1)
            pool.affine_select(out=HM[:], in_=HM[:], compare_op=ALU.is_ge, fill=0.0, base=0,
                               pattern=[[-HD, HG]], channel_multiplier=1).then_inc(g_c, 1)
            gp.wait_ge(g_c, 3)
            pool.affine_select(out=HM[:], in_=HM[:], compare_op=ALU.is_ge, fill=0.0, base=HD - 1,
                               pattern=[[HD, HG]], channel_multiplier=-1)
            for step in range(2):
                for c, (rows, h0, ns) in enumerate(SLOTS):
                    for g in range(2):
                        v = HRM[:, 2 * OFF[c] + g * ns:2 * OFF[c] + (g + 1) * ns]
                        if step == 0:
                            last = pool.affine_select(out=v, in_=v, compare_op=ALU.is_ge, fill=0.0, base=c * P - J * h0,
                                                      pattern=[[-J, ns]], channel_multiplier=1)
                        else:
                            last = pool.affine_select(out=v, in_=v, compare_op=ALU.is_ge, fill=0.0,
                                                      base=J * h0 + J - 1 - c * P, pattern=[[J, ns]],
                                                      channel_multiplier=-1)
                last.then_inc(g_c, 1)
                gp.wait_ge(g_c, 4 + step)
            for i in range(2):
                for c, (rows, h0, ns) in enumerate(SLOTS):
                    nh = min(ns, HG - h0)
                    pool.tensor_copy(Vbd[i][:, c, :, h0:h0 + nh, HD],
                                     HRM[:, 2 * OFF[c]:2 * OFF[c + 1]].rearrange("p (g s) -> p g s", g=2)[:, :, 0:nh])
            pool.tensor_copy(BM[:].rearrange("p (h i) -> p h i", h=HG), HM[:, :, None].broadcast_to([P, HG, HD])).then_inc(g_c, 1)
            gp.wait_ge(g_c, 6)
            for h in range(HG):
                v = Sel[:, h * J:(h + 1) * J]
                last = pool.affine_select(out=v, in_=v, compare_op=ALU.not_equal, fill=1.0, base=0,
                                          pattern=[[-1, J]], channel_multiplier=1)
            last.then_inc(g_c, 5)
            gp.wait_ge(v_sm, 3)
            pool.partition_all_reduce(smx[:], sm[:], P, RMAX).then_inc(g_smx, 1)

            def ln_scale(i, b):
                gp.wait_ge(v_ag[i], b + 1)
                pool.tensor_tensor(ve[i][:], mv[i][:, :, 1], epst[:], ALU.add).then_inc(g_ve[i], 1)
                gp.wait_ge(g_ve[i], b + 1)
                ge(gp, v_xn[i], b)
                pool.tensor_tensor(rstd[i][:], ve[i][:], mhalf[:], ALU.pow).then_inc(g_rs[i], 1)

            def add_bias(b, par, use):
                gp.wait_ge(ld_x[par], 16 * use)
                ge(gp, v_x1, b)
                pool.tensor_tensor(xb[:], xin[par][:], bias[:, None, :].broadcast_to([P, NT, D]), ALU.add).then_inc(g_xb, 1)

            def keys(b, par):
                gp.wait_ge(v_kT, b + 1)
                ge(gp, p_sT, NC * (b - 1))
                pool.tensor_tensor(kh[:], kTm[:], one[:, :, None].broadcast_to([P, 2, J]), ALU.mult).then_inc(g_k, 1)
                gp.wait_ge(g_k, 2 * b + 1)
                pool.tensor_tensor(kl[:], kTm[:], kh[:], ALU.subtract).then_inc(g_k, 1)
                gp.wait_ge(g_k, 2 * b + 2)
                for part, k in enumerate((kh, kl)):
                    last = pool.tensor_tensor(KBD[par][part][:].rearrange("p g (h j) -> p g h j", h=HG),
                                              k[:, :, None, :].broadcast_to([P, 2, HG, J]),
                                              HM[:, None, :, None].broadcast_to([P, 2, HG, J]), ALU.mult)
                last.then_inc(g_kbd, 1)

            ln_scale(0, 0)
            gp.wait_ge(ld_w, 16 * 10)

            def body(b, par, h):
                if there(b - 1):
                    ln_scale(2, b - 1)
                if there(b + 1):
                    add_bias(b + 1, 1 - par, nth(h, par, 1))
                    keys(b + 1, 1 - par)
                if there(b + 2):
                    ln_scale(0, b + 2)
                if there(b + 1):
                    ln_scale(1, b + 1)

            bodies(gp, body)

        @block.vector
        def _(dve):
            vec = nc.vector
            dve.wait_ge(ld_m, 32)
            vec.tensor_scalar(mkf[:], mk[:], -1.0, -MASKED, ALU.add, ALU.mult).then_inc(v_c, 1)
            dve.wait_ge(v_c, 1)
            vec.tensor_copy(mkr[:], mkf[:, None, :].broadcast_to([NB, HG, J])).then_inc(v_c, 1)

            def stats(i, b, src):
                ge(dve, v_xn[i], b)
                for t in range(NT):
                    last = vec.bn_stats(st[i][:, t, :], src[:, t, :])
                last.then_inc(v_st[i], 1)

            def aggregate(i, b):
                dve.wait_ge(v_st[i], b + 1)
                vec.tensor_copy(fence[:, i:i + 1], mhalf[:, 0:1])
                for t in range(NT):
                    last = vec.bn_aggr(mv[i][:, t, :], st[i][:, t, :])
                last.then_inc(v_ag[i], 1)

            def normalise(i, b, src, dst):
                dve.wait_ge(g_rs[i], b + 1)
                ge(dve, p_xn[i], b)
                for t in range(NT):
                    last = vec.tensor_scalar(dst[:, t, :], src[:, t, :], mv[i][:, t, 0:1], rstd[i][:, t:t + 1],
                                             ALU.subtract, ALU.mult)
                last.then_inc(v_xn[i], 1)

            dve.wait_ge(g_c, 2)
            dve.wait_ge(ld_x[0], 16)
            stats(0, 0, xin[0])
            aggregate(0, 0)
            done = 0
            blocks = [slice(w * WB, (w + 1) * WB) for w in range(3)]

            def step(instruction):
                nonlocal done
                done += 1
                instruction.then_inc(v_w, 1)
                dve.wait_ge(v_w, done)

            w3 = [W3[:, w].rearrange("p (n k) -> p n k", k=BLOCK) for w in range(3)]
            for w in range(3):
                dve.wait_ge(ld_w3[w], 16)
                step(vec.tensor_reduce(am[:, blocks[w]], w3[w], AX.X, ALU.max, apply_absolute_value=True))
                step(vec.tensor_scalar(s3[:, blocks[w]], am[:, blocks[w]], 1.0 / 7.0, SMALLEST, ALU.mult, ALU.max))
                vec.tensor_reduce(sm[:, w:w + 1], s3[:, blocks[w]], AX.X, ALU.max).then_inc(v_sm, 1)
            step(vec.reciprocal(rs3[:], s3[:]))

            def low_weights(w):
                for n in range(3 * w, 3 * w + 3):
                    f = n % 3
                    dve.wait_ge(a_wh, n + 1)
                    vec.tensor_tensor(wl[:, w, f * 512:(f + 1) * 512], ps[:, n % 8, :], wh[:, w, f * 512:(f + 1) * 512],
                                      ALU.subtract).then_inc(v_wl, 1)

            for w in range(3):
                step(vec.tensor_tensor(w3[w], w3[w], rs3[:, blocks[w], None].broadcast_to([P, WB, BLOCK]), ALU.mult))
                step(vec.tensor_scalar(W3[:, w], W3[:, w], ROUND, -ROUND, ALU.add, ALU.add))
                step(vec.tensor_scalar(W3[:, w], W3[:, w], 7.0, -8.0, ALU.min, ALU.max))
                if w == 0:
                    dve.wait_ge(g_smx, 1)
                    vec.tensor_scalar(wscale[:], smx[:], 1.0 / WTOP, None, ALU.mult)
                    step(vec.reciprocal(rsm[:], smx[:]))
                step(vec.tensor_scalar(s3[:, blocks[w]], s3[:, blocks[w]], rsm[:, w:w + 1], WTOP, ALU.mult, ALU.mult))
                vec.tensor_tensor(w3[w], w3[w], s3[:, blocks[w], None].broadcast_to([P, WB, BLOCK]), ALU.mult).then_inc(v_w3, 1)
                if w == 0:
                    normalise(0, 0, xin[0], xn1)
                    dve.wait_ge(a_wa, 1)
                    vec.scalar_tensor_tensor(out=wal[:], in0=wa[:], scalar=WUP, in1=wah[:], op0=ALU.mult, op1=ALU.subtract).then_inc(v_wa, 1)
                else:
                    low_weights(w - 1)
            low_weights(2)
            dve.wait_ge(g_c, 11)

            def low(bank, parts, scale, s):
                vec.scalar_tensor_tensor(out=parts[1][:].rearrange("p k n -> p (k n)"), in0=ps[:, bank, :], scalar=scale,
                                         in1=parts[0][:].rearrange("p k n -> p (k n)"), op0=ALU.mult,
                                         op1=ALU.subtract).then_inc(s, 1)

            def at_batch(ap, b):
                return ap[:, b:b + 1] if isinstance(b, int) else ap[:, bass.ds(b, 1)]

            def maxima(b, t):
                dve.wait_ge(p_s, 2 * b + t + 1)
                ge(dve, p_m, b)
                vec.tensor_reduce(mtile[:, t, 0:2 * B1].rearrange("p (k h) -> p k h", k=2),
                                  ps[:, 5:7, 0:B1 * J].rearrange("p k (h j) -> p k h j", j=J), AX.X, ALU.max)
                vec.tensor_reduce(mtile[:, t, 2 * B1:H], ps[:, 7, 0:(H - 2 * B1) * J].rearrange("p (h j) -> p h j", j=J),
                                  AX.X, ALU.max).then_inc(v_max, 1)

            def body(b, par, h):
                s, t_ = there(b + 1), there(b)
                if t_:
                    dve.wait_ge(a_xn[1], b + 1)
                    low(3, xn2T, NUP, v_xl[1])
                if there(b - 1):
                    dve.wait_ge(p_out, b)
                    dve.wait_ge(st_x2[1 - par], 16 * nth(h, par, -1))
                    vec.scalar_tensor_tensor(out=x2[1 - par][:], in0=ps[:, 4, :].rearrange("p (t d) -> p t d", t=NT),
                                             scalar=1.0 / (WUP * VUP), in1=x1[1 - par][:], op0=ALU.mult, op1=ALU.add).then_inc(v_x2, 1)
                    dve.wait_ge(v_x2, b)
                    stats(2, b - 1, x2[1 - par])
                    aggregate(2, b - 1)
                if t_:
                    dve.wait_ge(a_q2, b + 1)
                    ge(dve, p_s, 2 * b)
                    vec.scalar_tensor_tensor(out=q2T[1][:].rearrange("p k n -> p (k n)"), in0=ps[:, 5, :],
                                             scalar=QSCALE, in1=q2T[0][:].rearrange("p k n -> p (k n)"),
                                             op0=ALU.mult, op1=ALU.subtract).then_inc(v_q2l, 1)
                if there(b - 1):
                    normalise(2, b - 1, x2[1 - par], xn3)
                if s:
                    dve.wait_ge(p_kv, b + 2)
                    ge(dve, p_agg, b + 1)
                    vec.tensor_scalar(ktok[:, 1, :], ps[:, 2, 0:D], 1.0 / (WUP * NUP), 0.0, ALU.mult, ALU.max)
                    vec.tensor_scalar(vtok[:, 1, :, 0:P], ps[:, 2, D:2 * D].rearrange("p (g c) -> p g c", g=2), 1.0 / (WUP * NUP), None,
                                      ALU.mult).then_inc(v_kv, 1)
                if t_:
                    maxima(b, 0)
                if there(b - 1):
                    dve.wait_ge(v_xn[2], b)
                    vec.tensor_reduce(at_batch(xmax, b - 1), xn3[:], AX.XY, ALU.max, apply_absolute_value=True)
                if s:
                    dve.wait_ge(p_agg, b + 2)
                    ge(dve, p_num, b + 1)
                    a = ps[:, 1, 0:2 * (P + 1)].rearrange("p (g c) -> p g c", g=2)
                    vec.tensor_tensor(kvbd[:, :, 0:P], a[:, :, 0:P], BM[:, None, :].broadcast_to([P, 2, P]), ALU.mult)
                    vec.scalar_tensor_tensor(out=kvbd[:, :, P:NG], in0=a[:, :, P:P + 1].broadcast_to([P, 2, HG]),
                                             scalar=ATT_EPS, in1=HM[:, None, :].broadcast_to([P, 2, HG]),
                                             op0=ALU.add, op1=ALU.mult).then_inc(v_bd, 1)
                if t_:
                    maxima(b, 1)
                if s:
                    dve.wait_ge(p_num, b + 2)
                    ge(dve, v_o, b + 1)
                    vec.tensor_scalar(dz[:].rearrange("p t (g h) -> p t g h", g=2),
                                      ps[:, 0:3:2, 0:2 * NG].rearrange("p t (g c) -> p t g c", g=2)[:, :, :, P:NG],
                                      ATT_EPS, None, ALU.add).then_inc(v_dz, 1)
                    dve.wait_ge(v_dz, b + 2)
                    vec.reciprocal(zz[:], dz[:]).then_inc(v_z, 1)
                    dve.wait_ge(v_z, b + 2)
                    ge(dve, p_oT, b + 1)
                    for t in range(NT):
                        last = vec.tensor_tensor(
                            otok[:, t, :].rearrange("p (g h i) -> p g h i", g=2, h=HG),
                            ps[:, 2 * t, 0:2 * NG].rearrange("p (g c) -> p g c", g=2)[:, :, 0:P].rearrange("p g (h i) -> p g h i", h=HG),
                            zz[:, t, :].rearrange("p (g h) -> p g h", g=2)[:, :, :, None].broadcast_to([P, 2, HG, HD]), ALU.mult)
                    last.then_inc(v_o, 1)
                if s:
                    dve.wait_ge(p_ckv, b + 2)
                    ge(dve, g_kbd, b + 1)
                    vec.scalar_tensor_tensor(out=kTm[:], in0=ps[:, 4, 0:2 * J].rearrange("p (g j) -> p g j", g=2), scalar=VUP,
                                      in1=(msk8[:, b + 1:b + 2, :] if isinstance(b, int) else msk8[:, bass.ds(b + 1, 1), :]).broadcast_to([P, 2, J]),
                                      op0=ALU.mult, op1=ALU.mult).then_inc(v_kT, 1)
                    ge(dve, p_vr, b + 1)
                    vec.tensor_copy(vsb[:], ps[0:J, 4, 256:512]).then_inc(v_v, 1)
                if there(b + 2):
                    dve.wait_ge(ld_x[par], 16 * nth(h, par, 2))
                    stats(0, b + 2, xin[par])
                if there(b + 2):
                    aggregate(0, b + 2)
                if s:
                    dve.wait_ge(a_oT, b + 2)
                    low(1, oT, VUP, v_oTl)
                    dve.wait_ge(p_att, b + 2)
                    dve.wait_ge(g_xb, b + 2)
                    vec.scalar_tensor_tensor(out=x1[1 - par][:], in0=ps[:, 0, :].rearrange("p (t d) -> p t d", t=NT),
                                             scalar=1.0 / (WUP * VUP), in1=xb[:], op0=ALU.mult, op1=ALU.add).then_inc(v_x1, 1)
                    dve.wait_ge(v_x1, b + 2)
                    stats(1, b + 1, x1[1 - par])
                    aggregate(1, b + 1)
                if there(b + 2):
                    normalise(0, b + 2, xin[par], xn1)
                if s:
                    normalise(1, b + 1, x1[1 - par], xn2)
                if t_:
                    dve.wait_ge(p_av, b + 1)
                    av = ps[:, 6:8, 0:2 * NG].rearrange("p t (h i) -> p t h i", i=HD + 1)
                    ge(dve, v_o2, b)
                    vec.reciprocal(rden[:], av[:, :, :, HD]).then_inc(v_rd, 1)
                    dve.wait_ge(v_rd, b + 1)
                    ge(dve, p_o2T, b)
                    vec.tensor_tensor(o2[:].rearrange("p t (h i) -> p t h i", h=H), av[:, :, :, 0:HD],
                                      rden[:, :, :, None].broadcast_to([P, NT, H, HD]), ALU.mult).then_inc(v_o2, 1)
                if there(b + 2):
                    dve.wait_ge(a_xn[0], b + 3)
                    low(0, xn1T, NUP, v_xl[0])
                if s:
                    dve.wait_ge(p_vr, b + 2)
                    for c, (rows, h0, ns) in enumerate(SLOTS):
                        lo, hi = 2 * OFF[c], 2 * OFF[c + 1]
                        last = vec.tensor_tensor(
                            vbd_heads(1 - par, c),
                            ps[:, 4, lo * HD:hi * HD].rearrange("p (g s i) -> p g s i", g=2, i=HD),
                            HRM[:, lo:hi].rearrange("p (g s) -> p g s", g=2)[:, :, :, None].broadcast_to([P, 2, ns, HD]), ALU.mult)
                    last.then_inc(v_vbd, 1)
                if t_:
                    dve.wait_ge(a_o2T, b + 1)
                    low(3, o2T, VUP, v_o2Tl)

            dve.wait_ge(a_xn[0], 1)
            low(0, xn1T, NUP, v_xl[0])
            bodies(dve, body)

        @block.scalar
        def _(act):
            sc = nc.scalar
            act.wait_ge(ld_w, 16 * 10)
            sc.activation(wah[:], wa[:], ACT.Copy, scale=WUP).then_inc(a_wa, 1)
            for n in range(3 * 3):
                w, f = n // 3, n % 3
                act.wait_ge(p_wT, n + 1)
                sc.activation(wh[:, w, f * 512:(f + 1) * 512], ps[:, n % 8, :], ACT.Copy).then_inc(a_wh, 1)

            def copy_xn(i, b, bank, dst, scale):
                act.wait_ge(p_xn[i], b + 1)
                sc.activation(dst[:].rearrange("p k n -> p (k n)"), ps[:, bank, :], ACT.Copy, scale=scale).then_inc(a_xn[i], 1)

            def exponentials(b, c):
                rows = SLOTS[c][0]
                act.wait_ge(p_sT, NC * b + c + 1)
                sc.activation(expT[0:rows, c, :, :], ps[0:rows, (5, 6, 7, 4, 5)[c], :].rearrange("p (g n) -> p g n", g=2),
                              ACT.Exp, scale=1.0 / (VUP * VUP)).then_inc(a_e, 1)

            def body(b, par, h):
                s, t_ = there(b + 1), there(b)
                if s:
                    act.wait_ge(p_q, b + 2)
                    ge(act, p_num, b + 1)
                    sc.activation(qT[:].rearrange("p k n -> p (k n)"), ps[:, 1, :], ACT.Relu, scale=1.0 / (WUP * NUP)).then_inc(a_q, 1)
                if t_:
                    ge(act, p_q2, b)
                    copy_xn(1, b, 3, xn2T[0], NUP)
                    act.wait_ge(p_q2, b + 1)
                    ge(act, p_sT, NC * b)
                    sc.activation(q2T[0][:].rearrange("p k n -> p (k n)"), ps[:, 5, :], ACT.Copy, scale=QSCALE).then_inc(a_q2, 1)
                if s:
                    act.wait_ge(p_cT, b + 2)
                    ge(act, p_ckv, b + 1)
                    sc.activation(ctxT[:].rearrange("p k j -> p (k j)"), ps[:, 3, 0:2 * J], ACT.Copy).then_inc(a_cT, 1)
                    act.wait_ge(p_kv, b + 2)
                    ge(act, p_agg, b + 1)
                    sc.activation(ktok[:, 0, :], ps[:, 0, 0:D], ACT.Relu, scale=1.0 / (WUP * NUP))
                    sc.activation(vtok[:, 0, :, 0:P], ps[:, 0, D:2 * D].rearrange("p (g c) -> p g c", g=2), ACT.Copy,
                                  scale=1.0 / (WUP * NUP)).then_inc(a_kv, 1)
                if there(b - 1):
                    ge(act, st_xn, 16 * KC * (b - 1))
                    copy_xn(2, b - 1, 3, xn3T, 1.0)
                if t_:
                    act.wait_ge(p_m, b + 1)
                    sc.activation(mrow[:], ps[:, 3, 0:N // 2].bitcast(BF16), ACT.Copy).then_inc(a_m, 1)
                    ge(act, p_av, b)
                    for c in range(3):
                        exponentials(b, c)
                if s:
                    act.wait_ge(p_oT, b + 2)
                    ge(act, p_att, b + 1)
                    sc.activation(oT[0][:].rearrange("p k n -> p (k n)"), ps[:, 1, :], ACT.Copy, scale=VUP).then_inc(a_oT, 1)
                if t_:
                    for c in range(3, NC):
                        exponentials(b, c)
                if there(b + 2):
                    ge(act, p_kv, b + 2)
                    copy_xn(0, b + 2, 0, xn1T[0], NUP)
                if t_:
                    act.wait_ge(p_o2T, b + 1)
                    ge(act, p_out, b)
                    sc.activation(o2T[0][:].rearrange("p k n -> p (k n)"), ps[:, 3, :], ACT.Copy, scale=VUP).then_inc(a_o2T, 1)

            copy_xn(0, 0, 0, xn1T[0], NUP)
            bodies(act, body)

        @block.tensor
        def _(pe):
            te = nc.tensor
            pe.wait_ge(g_c, 11)
            for n in range(3 * 3):
                w, f = n // 3, n % 3
                pe.wait_ge(v_w3, w + 1)
                ge(pe, v_wl, n - 7)
                for q in range(4):
                    at = 4 * f + q
                    if w < 2:
                        k, m = at // FT, at % FT
                        src = W3[:, w, m * D + k * P:m * D + (k + 1) * P]
                    else:
                        k, m = at // KC, at % KC
                        src = W3[:, w, m * F + k * P:m * F + (k + 1) * P]
                    last = te.transpose(ps[:, n % 8, q * P:(q + 1) * P], src, ident[:])
                last.then_inc(p_wT, 1)
            pe.wait_ge(v_wl, 9)
            pe.wait_ge(v_wa, 1)

            def transpose_tiles(bank, src, s):
                for k in range(KC):
                    for t in range(NT):
                        last = te.transpose(ps[:, bank, k * N + t * P:k * N + (t + 1) * P], src[:, t, k * P:(k + 1) * P], ident[:])
                last.then_inc(s, 1)

            def scores(b, par, t):
                for bank, c0, g, h0, nh in ((5, 0, 0, 0, 6), (6, 0, 0, 6, 2), (6, 2 * J, 1, 0, 4), (7, 0, 1, 4, 4)):
                    o = ps[:, bank, c0:c0 + nh * J]
                    te.matmul(o, q2T[0][:, g, t * P:(t + 1) * P], KBD[par][0][:, g, h0 * J:(h0 + nh) * J], start=True, stop=False)
                    last = te.matmul(o, maskrow1[:], aug[par][:, g, h0 * J:(h0 + nh) * J], start=False, stop=True)
                last.then_inc(p_s, 1)

            def shifted(b, par, c):
                rows, bank = SLOTS[c][0], (5, 6, 7, 4, 5)[c]
                for g in range(2):
                    o = ps[0:rows, bank, g * N:(g + 1) * N]
                    for i, j in PASSES:
                        te.matmul(o, KBD[par][i][:, g, c * P:c * P + rows], q2T[j][:, g, :], start=(i == 0 and j == 0), stop=False)
                    last = te.matmul(o, aug[par][:, g, c * P:c * P + rows], mrow[:], start=False, stop=True)
                last.then_inc(p_sT, 1)

            def weight(part, n, m):
                w = (wah, wal)[part]
                return w[:, m * 3 * D + n * D:m * 3 * D + (n + 1) * D] if n < 3 else w[:, n * KC * D + m * D:n * KC * D + (m + 1) * D]

            def project(bank, src, n, low_ready, count, s):
                for t in range(NT):
                    for i, j in PASSES:
                        if t == 0 and i == 1:
                            pe.wait_ge(low_ready, count)
                        for k in range(KC):
                            last = te.matmul(ps[:, bank, t * D:(t + 1) * D], src[i][:, k, t * P:(t + 1) * P], weight(j, n, k),
                                             start=(i == 0 and j == 0 and k == 0), stop=(i == 1 and k == KC - 1))
                last.then_inc(s, 1)

            def queries(bank, n, src, low_ready, count, s):
                for m in range(KC):
                    for i, j in PASSES:
                        if m == 0 and i == 1:
                            pe.wait_ge(low_ready, count)
                        for k in range(KC):
                            last = te.matmul(ps[:, bank, m * N:(m + 1) * N], weight(j, n, k)[:, m * P:(m + 1) * P], src[i][:, k, :],
                                             start=(i == 0 and j == 0 and k == 0), stop=(i == 1 and k == KC - 1))
                last.then_inc(s, 1)

            def body(b, par, h):
                s, t_ = there(b + 1), there(b)
                if s:
                    pe.wait_ge(a_xn[0], b + 2)
                    ge(pe, v_oTl, b + 1)
                    queries(1, 0, xn1T, v_xl[0], b + 2, p_q)
                if t_:
                    pe.wait_ge(v_xn[1], b + 1)
                    ge(pe, v_o2Tl, b)
                    transpose_tiles(3, xn2, p_xn[1])
                if there(b - 1):
                    pe.wait_ge(a_o2T, b)
                    if t_:
                        pe.wait_ge(v_vbd, b + 1)
                    project(4, o2T, 5, v_o2Tl, b, p_out)
                if t_:
                    pe.wait_ge(a_xn[1], b + 1)
                    ge(pe, a_e, NC * b)
                    queries(5, 4, xn2T, v_xl[1], b + 1, p_q2)
                if s:
                    pe.wait_ge(ld_ctx[1 - par], 16 * nth(h, par, 1))
                    te.transpose(ps[:, 3, 0:J], ctxin[1 - par][:, 0:P], ident[0:J, 0:J])
                    te.transpose(ps[:, 3, J:2 * J], ctxin[1 - par][:, P:2 * P], ident[0:J, 0:J]).then_inc(p_cT, 1)
                if s:
                    ge(pe, v_o, b + 1)
                    for t in range(NT):
                        for i, j in PASSES:
                            for k in range(KC):
                                last = te.matmul(ps[:, 2 * t, :], xn1T[i][:, k, t * P:(t + 1) * P],
                                                 (wah, wal)[j][:, k * 3 * D + D:(k + 1) * 3 * D],
                                                 start=(i == 0 and j == 0 and k == 0), stop=(i == 1 and k == KC - 1))
                    last.then_inc(p_kv, 1)
                if t_:
                    pe.wait_ge(v_q2l, b + 1)
                    pe.wait_ge(g_kbd, b + 1)
                    pe.wait_ge(ld_mrow[par], 32 * nth(h, par, 0))
                    ge(pe, v_o2, b)
                    scores(b, par, 0)
                if there(b - 1):
                    pe.wait_ge(v_xn[2], b)
                    if s:
                        pe.wait_ge(a_cT, b + 2)
                    transpose_tiles(3, xn3, p_xn[2])
                if s:
                    pe.wait_ge(a_kv, b + 2)
                    pe.wait_ge(v_kv, b + 2)
                    for g in range(2):
                        for t in range(NT):
                            last = te.matmul(ps[:, 1, g * (P + 1):(g + 1) * (P + 1)], ktok[:, t, g * P:(g + 1) * P],
                                             vtok[:, t, g, :], start=(t == 0), stop=(t == NT - 1))
                    last.then_inc(p_agg, 1)
                if t_:
                    pe.wait_ge(v_max, 2 * b + 1)
                    scores(b, par, 1)
                if s:
                    pe.wait_ge(v_bd, b + 2)
                    for t in range(NT):
                        for g in range(2):
                            last = te.matmul(ps[:, 2 * t, g * NG:(g + 1) * NG], qT[:, g, t * P:(t + 1) * P], kvbd[:, g, :],
                                             start=True, stop=True)
                    last.then_inc(p_num, 1)
                if s:
                    pe.wait_ge(a_cT, b + 2)
                    ge(pe, v_x2, b)
                    for g in range(2):
                        for k in range(2):
                            te.matmul(ps[:, 4, g * J:(g + 1) * J], wk2[:, k, g * P:(g + 1) * P], ctxT[:, k, :],
                                      start=(k == 0), stop=(k == 1))
                if t_:
                    pe.wait_ge(v_max, 2 * b + 2)
                    ge(pe, a_xn[2], b)
                    for t in range(NT):
                        last = te.transpose(ps[:, 3, 0:N // 2].bitcast(BF16)[:, t * P:(t + 1) * P], mtile[:, t, :], identb[:])
                    last.then_inc(p_m, 1)
                if s:
                    for k in range(2):
                        last = te.matmul(ps[0:J, 4, 256:512], ctxT[:, k, :], wv2[:, k, :], start=(k == 0), stop=(k == 1))
                    last.then_inc(p_ckv, 1)
                if t_:
                    pe.wait_ge(a_m, b + 1)
                    for c in range(3):
                        shifted(b, par, c)
                if s:
                    pe.wait_ge(v_o, b + 2)
                    transpose_tiles(1, otok, p_oT)
                if t_:
                    if s:
                        pe.wait_ge(v_v, b + 2)
                    shifted(b, par, 3)
                    pe.wait_ge(a_e, NC * b + 1)
                    shifted(b, par, 4)
                if s:
                    pe.wait_ge(a_oT, b + 2)
                    project(0, oT, 3, v_oTl, b + 2, p_att)
                if t_:
                    pe.wait_ge(a_e, NC * (b + 1))
                    pe.wait_ge(v_vbd, b + 1)
                    for t in range(NT):
                        for g in range(2):
                            for c, (rows, h0, ns) in enumerate(SLOTS):
                                last = te.matmul(ps[:, 6 + t, g * NG:(g + 1) * NG], expT[0:rows, c, g, t * P:(t + 1) * P],
                                                 Vbd[par][0:rows, c, g].rearrange("p h i -> p (h i)"),
                                                 start=(c == 0), stop=(c == NC - 1))
                    last.then_inc(p_av, 1)
                if there(b + 2):
                    pe.wait_ge(v_xn[0], b + 3)
                    ge(pe, v_x1, b + 2)
                    transpose_tiles(0, xn1, p_xn[0])
                if s:
                    pe.wait_ge(v_v, b + 2)
                    vg = vsb[:].rearrange("j (g c) -> j g c", g=2)
                    for c, (rows, h0, ns) in enumerate(SLOTS):
                        last = te.matmul(ps[:, 4, 2 * OFF[c] * HD:2 * OFF[c + 1] * HD], Sel[:, c * P:(c + 1) * P],
                                         vg[:, :, h0 * HD:(h0 + ns) * HD], start=True, stop=True)
                    last.then_inc(p_vr, 1)
                if t_:
                    pe.wait_ge(v_o2, b + 1)
                    transpose_tiles(3, o2, p_o2T)

            pe.wait_ge(v_xn[0], 1)
            transpose_tiles(0, xn1, p_xn[0])
            bodies(pe, body)


def feed_forward_phases(nc, top, ps, wh, wl, wscale, xmax, x2_d, xn_d, g_d, p_d, out, NB, NCH, FT, sb_in, sem_in):
    KC = 2
    D = KC * P
    FC = FT * CH
    NP = FT // 2
    BT = CH // (2 * P)
    keep, ksem = sb_in(top), sem_in(top)
    sc = keep("sc", [P, 16], F32)
    gmax = keep("gmax", [P, NCH * NP], F32)
    gtop = keep("gtop", [P, NCH * NP], F32)
    umax = keep("umax", [P, NCH * NP], F32)
    smax = keep("smax", [P, 3 * NCH], F32)
    pmax = keep("pmax", [P, NP * NCH], F32)
    xstack = ExitStack()
    R = sb_in(xstack)("R", [P, NCH, KC, 2, CH], F16)
    SX, KX, AG, AU, SG, KG, SU, KU, SS, CS, SO, KO, TD = range(13)

    def pair(n):
        return ps[:, 2 * (n % 4):2 * (n % 4) + 2, :]

    def tokens(n, k):
        r = R[:, n:n + 1, k] if isinstance(n, int) else R[:, bass.ds(n, 1), k]
        return r.rearrange("p n s c -> p (n s) c")

    def at(ap, n):
        return ap[:, n:n + 1] if isinstance(n, int) else ap[:, bass.ds(n, 1)]

    def scale_of(dve, done, count, largest, factor, s, k):
        vec = nc.vector
        if factor is None:
            vec.tensor_scalar(sc[:, s:s + 1], largest, 1.0 / QMAX16, SMALLEST, ALU.mult, ALU.max).then_inc(done, 1)
        else:
            vec.tensor_scalar(sc[:, s:s + 1], largest, sc[:, factor:factor + 1], 1.0 / QMAX16, ALU.mult, ALU.mult).then_inc(done, 1)
            count += 1
            dve.wait_ge(done, count)
            vec.tensor_scalar(sc[:, s:s + 1], sc[:, s:s + 1], SMALLEST, None, ALU.max).then_inc(done, 1)
        count += 1
        dve.wait_ge(done, count)
        vec.reciprocal(sc[:, k:k + 1], sc[:, s:s + 1]).then_inc(done, 1)
        count += 1
        dve.wait_ge(done, count)
        return count

    def times(dve, done, count, dst, a, b, c=None):
        if c is None:
            nc.vector.tensor_scalar(sc[:, dst:dst + 1], a, b, None, ALU.mult).then_inc(done, 1)
        else:
            nc.vector.tensor_scalar(sc[:, dst:dst + 1], a, b, c, ALU.mult, ALU.mult).then_inc(done, 1)
        dve.wait_ge(done, count + 1)
        return count + 1

    with ExitStack() as stack:
        sb, sem = sb_in(stack), sem_in(stack)
        xf = [sb(f"xf{i}", [P, KC, CH], F32) for i in range(2)]
        gs = [sb(f"gs{i}", [P, 2, CH], F32) for i in range(NP)]
        pm = sb("pm", [P, 1], F32)
        pa = sb("pa", [P, 1], F32)
        done, g_all, v_pm = sem("b_done"), sem("b_all"), sem("b_pm")
        ld = [sem(f"b_ld{i}") for i in range(2)]
        a_r, v_hi, v_r = sem("b_round"), sem("b_hi"), sem("b_lo")
        p_g, a_g, v_g = sem("b_pg"), sem("b_ag"), sem("b_vg")
        st_g = [sem(f"b_stg{j}") for j in range(NP)]
        p_u, v_u = sem("b_pu"), sem("b_vu")
        block = stack.enter_context(nc.Block())

        @block.sync
        def _(sp):
            def body(n, par):
                if not (isinstance(n, int) and n < 2):
                    sp.wait_ge(v_r, n - 1)
                for i in range(BT):
                    sp.dma_start(xf[par][:, :, i * 2 * P:(i + 1) * 2 * P], xn_d[n * BT + i]).then_inc(ld[par], 16)

            body(0, 0)
            body(1, 1)
            with sp.Fori(1, NCH // 2) as i:
                body(i * 2, 0)
                body(i * 2 + 1, 1)

        @block.gpsimd
        def _(gp):
            gp.wait_ge(v_pm, 1)
            nc.gpsimd.partition_all_reduce(pa[:], pm[:], P, RMAX).then_inc(g_all, 1)

        @block.vector
        def _(dve):
            vec = nc.vector
            vec.tensor_reduce(pm[:], xmax[:], AX.X, ALU.max).then_inc(v_pm, 1)
            dve.wait_ge(g_all, 1)
            c = scale_of(dve, done, 0, pa[:], None, SX, KX)
            c = times(dve, done, c, AG, wscale[:, 0:1], sc[:, SX:SX + 1])
            c = times(dve, done, c, AU, wscale[:, 1:2], sc[:, SX:SX + 1])
            assert c == 4

            def split(n, par):
                dve.wait_ge(a_r, n + 1)
                r = R[:, n:n + 1] if isinstance(n, int) else R[:, bass.ds(n, 1)]
                r = r.rearrange("p n k s c -> p (n k) s c")
                vec.tensor_scalar(r[:, :, 0, :], xf[par][:], -ROUND, None, ALU.add).then_inc(v_hi, 1)
                dve.wait_ge(v_hi, n + 1)
                vec.scalar_tensor_tensor(out=r[:, :, 1, :], in0=xf[par][:], scalar=-ROUND, in1=r[:, :, 0, :],
                                         op0=ALU.add, op1=ALU.subtract).then_inc(v_r, 1)

            def body(n, par, last):
                if not last:
                    split(n + 1, 1 - par)
                for j in range(NP):
                    dve.wait_ge(a_g, n * NP + j + 1)
                    vec.tensor_reduce(at(gtop, n * NP + j), gs[j][:], AX.XY, ALU.max)
                    vec.tensor_reduce(at(gmax, n * NP + j), gs[j][:], AX.XY, ALU.max,
                                      apply_absolute_value=True).then_inc(v_g, 1)
                for j in range(NP):
                    dve.wait_ge(p_u, n * NP + j + 1)
                    vec.tensor_reduce(at(umax, n * NP + j), pair(NP + j + 2 * NP * par), AX.XY, ALU.max,
                                      apply_absolute_value=True).then_inc(v_u, 1)

            split(0, 0)
            with dve.Fori(0, NCH // 2 - 1) as i:
                body(i * 2, 0, False)
                body(i * 2 + 1, 1, False)
            body(NCH - 2, 0, False)
            body(NCH - 1, 1, True)

        @block.scalar
        def _(act):
            def scale_x(n, par, use):
                act.wait_ge(ld[par], 16 * BT * use)
                nc.scalar.activation(xf[par][:], xf[par][:], ACT.Copy, scale=sc[:, KX:KX + 1], bias=ROUND).then_inc(a_r, 1)

            def body(n, par, i, peeled, last=False):
                if not last:
                    scale_x(n + 1, 1 - par, i + par + 1)
                for j in range(NP):
                    act.wait_ge(p_g, n * NP + j + 1)
                    if not peeled:
                        act.wait_ge(v_g, (n - 1) * NP + j + 1)
                        act.wait_ge(st_g[j], 16 * n)
                    nc.scalar.activation(gs[j][:], pair(j + 2 * NP * par), ACT.Copy).then_inc(a_g, 1)
                    act.wait_ge(a_g, n * NP + j + 1)
                    act.dma_start((g_d[n])[:, 2 * CH * j:2 * CH * (j + 1)], gs[j][:].rearrange("p a c -> p (a c)")).then_inc(st_g[j], 16)

            act.wait_ge(done, 4)
            scale_x(0, 0, 1)
            body(0, 0, 0, True)
            body(1, 1, 0, False)
            with act.Fori(1, NCH // 2 - 1) as i:
                body(i * 2, 0, i, False)
                body(i * 2 + 1, 1, i, False)
            body(NCH - 2, 0, NCH // 2 - 1, False)
            body(NCH - 1, 1, NCH // 2 - 1, False, True)
            for j in range(NP):
                act.wait_ge(st_g[j], 16 * NCH)

        @block.tensor
        def _(pe):
            def body(n, par, first):
                pe.wait_ge(v_r, n + 1)
                for w, s in ((0, p_g), (1, p_u)):
                    for j in range(NP):
                        back = 2 * NP * par + NP * w + j - 4
                        w_back, j_back, n_back = (back // NP) % 2, back % NP, back // (2 * NP)
                        if not (first and back < 0):
                            pe.wait_ge(v_u if w_back else a_g, (n - par + n_back) * NP + j_back + 1)
                        for m in range(2):
                            o = pair(2 * NP * par + NP * w + j)[:, m, :]
                            for k in range(KC):
                                col = k * FT * P + (2 * j + m) * P
                                r = tokens(n, k)
                                for q, (lhs, part) in enumerate(((wh, 0), (wl, 0), (wh, 1))):
                                    last = nc.tensor.matmul(o, lhs[:, w, col:col + P], r[:, part, :],
                                                            start=(k == 0 and q == 0), stop=(k == KC - 1 and q == 2))
                        last.then_inc(s, 1)

            body(0, 0, True)
            body(1, 1, False)
            with pe.Fori(1, NCH // 2) as i:
                body(i * 2, 0, False)
                body(i * 2 + 1, 1, False)

    with ExitStack() as stack:
        sb, sem = sb_in(stack), sem_in(stack)
        gf = [sb(f"gf{i}", [P, FC // 3], F32) for i in range(2)]
        gq = [sb(f"gq{i}", [P, FC // 3], I16) for i in range(2)]
        sg = [sb(f"sg{i}", [P, FC // 3], F32) for i in range(2)]
        sq = [sb(f"sq{i}", [P, FC // 3], U16) for i in range(2)]
        pm = sb("pm2", [P, 3], F32)
        pa = sb("pa2", [P, 3], F32)
        tq = sb("tq", [P, 1], I16)
        ts = sb("ts", [P, 1], F32)
        tu = sb("tu", [P, 1], U16)
        tp = sb("tp", [P, 1], F32)
        below = sb("below", [P, 1], F32)
        flag = sb("flag", [P, 1], I32)
        top_s = sem("c_top")
        done, g_all, v_pm = sem("c_done"), sem("c_all"), sem("c_pm")
        ld = [sem(f"c_ld{i}") for i in range(2)]
        a_q, a_s, v_q, v_f, v_m = sem("c_q"), sem("c_s"), sem("c_vq"), sem("c_vf"), sem("c_vm")
        block = stack.enter_context(nc.Block())
        G3 = FC // 3
        NU = 3 * NCH

        def units(eng, body):
            body(0, 0, 0, True)
            body(1, 1, 0, True)
            with eng.Fori(1, NU // 2) as i:
                body(i * 2, 0, i, False)
                body(i * 2 + 1, 1, i, False)

        @block.sync
        def _(sp):
            def body(n, par):
                for j in range(3):
                    q = (3 * par + j)
                    if not (isinstance(n, int) and q < 2):
                        sp.wait_ge(a_q, 3 * n + j - 1)
                    sp.dma_start(gf[q % 2][:], (g_d[n])[:, j * G3:(j + 1) * G3]).then_inc(ld[q % 2], 16)

            sp.wait_ge(top_s, 7)
            with sp.If(sp.value_load(flag[0:1, 0:1]) > 0):
                body(0, 0)
                body(1, 1)
                with sp.Fori(1, NCH // 2) as i:
                    body(i * 2, 0)
                    body(i * 2 + 1, 1)

        @block.gpsimd
        def _(gp):
            gp.wait_ge(v_pm, 3)
            nc.gpsimd.partition_all_reduce(pa[:], pm[:], P, RMAX).then_inc(g_all, 1)

        @block.vector
        def _(dve):
            vec = nc.vector
            vec.tensor_reduce(pm[:, 0:1], gmax[:], AX.X, ALU.max).then_inc(v_pm, 1)
            vec.tensor_reduce(pm[:, 1:2], umax[:], AX.X, ALU.max).then_inc(v_pm, 1)
            vec.tensor_reduce(pm[:, 2:3], gtop[:], AX.X, ALU.max).then_inc(v_pm, 1)
            dve.wait_ge(g_all, 1)
            c = scale_of(dve, done, 0, pa[:, 0:1], AG, SG, KG)
            c = scale_of(dve, done, c, pa[:, 1:2], AU, SU, KU)
            c = times(dve, done, c, KG, sc[:, KG:KG + 1], sc[:, AG:AG + 1])
            c = times(dve, done, c, KU, sc[:, KU:KU + 1], sc[:, AU:AU + 1])
            assert c == 8
            dve.wait_ge(top_s, 2)
            vec.tensor_scalar(tu[:], ts[:], 65536.0, 65535.0, ALU.mult, ALU.min).then_inc(top_s, 1)
            dve.wait_ge(top_s, 3)
            vec.tensor_tensor(tp[:], tu[:], tq[:], ALU.mult).then_inc(top_s, 1)
            dve.wait_ge(top_s, 4)
            vec.tensor_scalar(below[:], tp[:], sc[:, SG:SG + 1], 1.0 / 65536.0, ALU.mult, ALU.mult).then_inc(top_s, 1)
            vec.tensor_scalar(smax[:], tp[:].broadcast_to([P, 3 * NCH]), 0.0, None, ALU.max).then_inc(top_s, 1)
            dve.wait_ge(top_s, 5)
            vec.tensor_scalar(flag[:], below[:], DIP, None, ALU.is_lt).then_inc(top_s, 1)

            def body(n, par, i, first):
                dve.wait_ge(a_s, n + 1)
                vec.tensor_scalar(sq[par][:], sg[par][:], 65536.0, 65535.0, ALU.mult, ALU.min).then_inc(v_q, 1)
                dve.wait_ge(v_q, n + 1)
                if not (isinstance(n, int) and n < 1):
                    dve.wait_ge(v_m, n)
                vec.tensor_tensor(sg[par][:], sq[par][:], gq[par][:], ALU.mult).then_inc(v_f, 1)
                dve.wait_ge(v_f, n + 1)
                vec.tensor_reduce(at(smax, n), sg[par][:], AX.X, ALU.max, apply_absolute_value=True).then_inc(v_m, 1)

            dve.wait_ge(top_s, 7)
            with dve.If(dve.value_load(flag[0:1, 0:1]) > 0):
                units(dve, body)

        @block.scalar
        def _(act):
            act.wait_ge(done, 8)
            nc.scalar.activation(tq[:], pa[:, 2:3], ACT.Copy, scale=sc[:, KG:KG + 1]).then_inc(top_s, 1)
            act.wait_ge(top_s, 1)
            nc.scalar.activation(ts[:], tq[:], ACT.Sigmoid, scale=sc[:, SG:SG + 1]).then_inc(top_s, 1)

            def body(n, par, i, first):
                act.wait_ge(ld[par], 16 * (i + 1))
                if not first:
                    act.wait_ge(v_m, n - 1)
                nc.scalar.activation(gq[par][:], gf[par][:], ACT.Copy, scale=sc[:, KG:KG + 1]).then_inc(a_q, 1)
                act.wait_ge(a_q, n + 1)
                nc.scalar.activation(sg[par][:], gq[par][:], ACT.Sigmoid, scale=sc[:, SG:SG + 1]).then_inc(a_s, 1)

            act.wait_ge(top_s, 7)
            with act.If(act.value_load(flag[0:1, 0:1]) > 0):
                units(act, body)

    with ExitStack() as stack:
        sb, sem = sb_in(stack), sem_in(stack)
        G = 2 * CH
        gf = [sb(f"df{i}", [P, G], F32) for i in range(3)]
        gq = [sb(f"dq{i}", [P, G], I16) for i in range(3)]
        sq = [sb(f"ds{i}", [P, G], U16) for i in range(2)]
        gz = [sb(f"dz{i}", [P, G], I16) for i in range(2)]
        uq = [sb(f"du{i}", [P, G], I16) for i in range(2)]
        pr = [sb(f"dp{i}", [P, G], F32) for i in range(3)]
        pm = sb("pm3", [P, 1], F32)
        pa = sb("pa3", [P, 1], F32)
        done, g_all, v_pm = sem("d_done"), sem("d_all"), sem("d_pm")
        ld, st = ([sem(f"d_{n}{i}") for i in range(3)] for n in ("ld", "st"))
        a_q, a_s, v_q, v_z = sem("d_q"), sem("d_s"), sem("d_vq"), sem("d_vz")
        p_u, a_u, v_p, v_m = sem("d_pu"), sem("d_au"), sem("d_vp"), sem("d_vm")
        block = stack.enter_context(nc.Block())
        NQ = 2 * NP
        NU = NP * NCH

        def steps(eng, body):
            for q in range(NQ):
                body(q, q, 0)
            with eng.Fori(1, NCH // 2 - 1) as i:
                for q in range(NQ):
                    body(i * NQ + q, q, i)
            for q in range(NQ):
                body(NU - NQ + q, q, NCH // 2 - 1)

        def before(u, n):
            return isinstance(u, int) and u < n

        @block.sync
        def _(sp):
            def store(u, q):
                sp.wait_ge(v_p, u + 1)
                sp.dma_start(p_d[u], pr[q % 3][:]).then_inc(st[q % 3], 16)

            def body(u, q, i):
                if not before(u, 3):
                    sp.wait_ge(v_q, u - 2)
                sp.dma_start(gf[q % 3][:], (g_d[i * 2 + q // NP])[:, (q % NP) * G:(q % NP + 1) * G]).then_inc(ld[q % 3], 16)
                if not before(u, 3):
                    store(u - 3, q)

            steps(sp, body)
            for q in range(3):
                store(NU - 3 + q, q)
            for i in range(3):
                sp.wait_ge(st[i], 16 * NU // 3)

        @block.gpsimd
        def _(gp):
            gp.wait_ge(v_pm, 1)
            nc.gpsimd.partition_all_reduce(pa[:], pm[:], P, RMAX).then_inc(g_all, 1)

        @block.vector
        def _(dve):
            vec = nc.vector
            vec.tensor_reduce(pm[:], smax[:], AX.X, ALU.max).then_inc(v_pm, 1)
            vec.tensor_scalar(sc[:, TD:TD + 1], sc[:, SG:SG + 1], 1.0 / 65536.0, None, ALU.mult).then_inc(done, 1)
            dve.wait_ge(done, 1)
            dve.wait_ge(g_all, 1)
            c = scale_of(dve, done, 1, pa[:], TD, SS, CS)
            c = times(dve, done, c, CS, sc[:, CS:CS + 1], sc[:, TD:TD + 1])

            def quantise_sigmoid(u, q):
                dve.wait_ge(a_s, u + 1)
                vec.tensor_scalar(sq[q % 2][:], gf[q % 3][:], 65536.0, 65535.0, ALU.mult, ALU.min).then_inc(v_q, 1)

            def reduce_product(u, q):
                dve.wait_ge(v_p, u + 1)
                vec.tensor_reduce(at(pmax, u), pr[q % 3][:], AX.X, ALU.max, apply_absolute_value=True).then_inc(v_m, 1)

            def body(u, q, i):
                par = q % 2
                if not (isinstance(u, int) and u == NU - 1):
                    quantise_sigmoid(u + 1, q + 1)
                dve.wait_ge(v_q, u + 1)
                vec.scalar_tensor_tensor(out=gz[par][:], in0=sq[par][:], scalar=sc[:, CS:CS + 1], in1=gq[q % 3][:],
                                         op0=ALU.mult, op1=ALU.mult).then_inc(v_z, 1)
                if not before(u, 1):
                    reduce_product(u - 1, q - 1)
                dve.wait_ge(v_z, u + 1)
                dve.wait_ge(a_u, u + 1)
                if not before(u, 3):
                    dve.wait_ge(st[q % 3], 16 * (i * 2 + q // 3))
                    dve.wait_ge(v_m, u - 2)
                vec.tensor_tensor(pr[q % 3][:], gz[par][:], uq[par][:], ALU.mult).then_inc(v_p, 1)

            quantise_sigmoid(0, 0)
            steps(dve, body)
            reduce_product(NU - 1, NQ - 1)

        @block.scalar
        def _(act):
            def body(u, q, i):
                par = q % 2
                act.wait_ge(ld[q % 3], 16 * (i * 2 + q // 3 + 1))
                if not before(u, 3):
                    act.wait_ge(v_z, u - 2)
                nc.scalar.activation(gq[q % 3][:], gf[q % 3][:], ACT.Copy, scale=sc[:, KG:KG + 1]).then_inc(a_q, 1)
                act.wait_ge(a_q, u + 1)
                nc.scalar.activation(gf[q % 3][:], gq[q % 3][:], ACT.Sigmoid, scale=sc[:, SG:SG + 1]).then_inc(a_s, 1)
                act.wait_ge(p_u, u + 1)
                if not before(u, 2):
                    act.wait_ge(v_p, u - 1)
                nc.scalar.activation(uq[par][:].rearrange("p (a c) -> p a c", a=2), pair(q % NP), ACT.Copy,
                                     scale=sc[:, KU:KU + 1]).then_inc(a_u, 1)

            steps(act, body)

        @block.tensor
        def _(pe):
            def body(u, q, i):
                if not before(u, NP):
                    pe.wait_ge(a_u, u - NP + 1)
                j = q % NP
                for m in range(2):
                    o = pair(j)[:, m, :]
                    for k in range(KC):
                        col = k * FT * P + (2 * j + m) * P
                        x3 = tokens(i * 2 + q // NP, k)
                        for pas, (lhs, part) in enumerate(((wh, 0), (wl, 0), (wh, 1))):
                            last = nc.tensor.matmul(o, lhs[:, 1, col:col + P], x3[:, part, :],
                                                    start=(k == 0 and pas == 0), stop=(k == KC - 1 and pas == 2))
                last.then_inc(p_u, 1)

            steps(pe, body)

    xstack.close()

    with ExitStack() as stack:
        sb, sem = sb_in(stack), sem_in(stack)
        G = FC // NP
        pf = [[sb(f"ef{i}_{h}", [P, G], F32) for h in range(NP)] for i in range(2)]
        oq = [sb(f"eq{i}", [P, FC], I16) for i in range(2)]
        oh = [sb(f"eh{i}", [P, FC], F16) for i in range(2)]
        ol = [sb(f"el{i}", [P, FC], F16) for i in range(2)]
        xr = [sb(f"ex{i}", [P, BT * 2, D], F32) for i in range(2)]
        xo = [sb(f"eo{i}", [P, BT * 2, D], F32) for i in range(2)]
        free = sb("free", [P, 2], F32)
        pm = sb("pm4", [P, 1], F32)
        pa = sb("pa4", [P, 1], F32)
        done, g_all, v_pm = sem("e_done"), sem("e_all"), sem("e_pm")
        ld = [sem(f"e_ld{i}") for i in range(2)]
        ldx, st = ([sem(f"e_{n}{i}") for i in range(2)] for n in ("ldx", "st"))
        v_q, a_h, v_l, p_o, v_o = sem("e_vq"), sem("e_ah"), sem("e_vl"), sem("e_po"), sem("e_vo")
        block = stack.enter_context(nc.Block())

        def before(n, m):
            return isinstance(n, int) and n < m

        def steps(eng, body):
            body(0, 0, 0)
            body(1, 1, 0)
            with eng.Fori(1, NCH // 2 - 1) as i:
                body(i * 2, 0, i)
                body(i * 2 + 1, 1, i)
            body(NCH - 2, 0, NCH // 2 - 1)
            body(NCH - 1, 1, NCH // 2 - 1)

        @block.sync
        def _(sp):
            def body(n, par, i):
                for h in range(NP):
                    if not before(n, 2):
                        sp.wait_ge(v_q, NP * (n - 2) + h + 1)
                    sp.dma_start(pf[par][h][:], p_d[NP * n + h]).then_inc(ld[par], 16)
                if not before(n, 1):
                    load_x(n - 1, 1 - par)

            def load_x(n, par):
                if not before(n, 2):
                    sp.wait_ge(v_o, n - 1)
                for k in range(BT):
                    sp.dma_start(xr[par][:, 2 * k:2 * k + 2, :], x2_d[BT * n + k].rearrange("p (t d) -> p t d", t=2)).then_inc(ldx[par], 16)

            steps(sp, body)
            load_x(NCH - 1, 1)

        @block.gpsimd
        def _(gp):
            gp.wait_ge(v_pm, 1)
            nc.gpsimd.partition_all_reduce(pa[:], pm[:], P, RMAX).then_inc(g_all, 1)

        @block.scalar
        def _(act):
            def high(n, par):
                for h in range(NP):
                    act.wait_ge(v_q, NP * n + h + 1)
                    if h == 0 and not before(n, 2):
                        act.wait_ge(p_o, n - 1)
                    nc.scalar.activation(oh[par][:, h * G:(h + 1) * G], oq[par][:, h * G:(h + 1) * G], ACT.Copy).then_inc(a_h, 1)

            def store(n, par):
                act.wait_ge(v_o, n + 1)
                for k in range(BT):
                    act.dma_start(out[BT * n + k].rearrange("(p t) d -> p t d", t=2), xo[par][:, 2 * k:2 * k + 2, :]).then_inc(st[par], 16)

            def body(n, par, i):
                high(n, par)
                if not before(n, 2):
                    store(n - 2, par)

            steps(act, body)
            store(NCH - 2, 0)
            store(NCH - 1, 1)
            for i in range(2):
                act.wait_ge(st[i], 16 * BT * (NCH // 2 + 1))

        @block.vector
        def _(dve):
            vec = nc.vector
            for i in range(2):
                vec.memset(free[:, i:i + 1], 0.0).then_inc(st[i], 16 * BT)
            vec.tensor_reduce(pm[:], pmax[:], AX.X, ALU.max).then_inc(v_pm, 1)
            vec.tensor_scalar(sc[:, TD:TD + 1], sc[:, SS:SS + 1], sc[:, SU:SU + 1], None, ALU.mult).then_inc(done, 1)
            dve.wait_ge(done, 1)
            dve.wait_ge(g_all, 1)
            c = scale_of(dve, done, 1, pa[:], TD, SO, KO)
            c = times(dve, done, c, KO, sc[:, KO:KO + 1], sc[:, TD:TD + 1])
            c = times(dve, done, c, TD, sc[:, SO:SO + 1], wscale[:, 2:3])

            def finish(n, par, use):
                dve.wait_ge(p_o, n + 1)
                dve.wait_ge(ldx[par], 16 * BT * use)
                o = ps[:, 2 * par:2 * par + 2, :].rearrange("p a c -> p (a c)")
                xf = xr[par][:].rearrange("p a c -> p (a c)")
                dve.wait_ge(st[par], 16 * BT * use)
                vec.scalar_tensor_tensor(out=xo[par][:].rearrange("p a c -> p (a c)"), in0=o, scalar=sc[:, TD:TD + 1], in1=xf, op0=ALU.mult, op1=ALU.add).then_inc(v_o, 1)

            def body(n, par, i):
                dve.wait_ge(ld[par], 16 * NP * (i + 1))
                for h in range(NP):
                    if h == 0 and not before(n, 2):
                        dve.wait_ge(a_h, NP * (n - 1))
                        dve.wait_ge(v_l, NP * (n - 1))
                    vec.tensor_scalar(oq[par][:, h * G:(h + 1) * G], pf[par][h][:], sc[:, KO:KO + 1], None, ALU.mult).then_inc(v_q, 1)
                if not before(n, 2):
                    finish(n - 2, par, i)
                for h in range(NP):
                    dve.wait_ge(a_h, NP * n + h + 1)
                    if h == 0 and not before(n, 2):
                        dve.wait_ge(p_o, n - 1)
                    vec.tensor_tensor(ol[par][:, h * G:(h + 1) * G], oq[par][:, h * G:(h + 1) * G], oh[par][:, h * G:(h + 1) * G],
                                      ALU.subtract).then_inc(v_l, 1)

            steps(dve, body)
            finish(NCH - 2, 0, NCH // 2)
            finish(NCH - 1, 1, NCH // 2)

        @block.tensor
        def _(pe):
            def body(n, par, i):
                pe.wait_ge(v_l, NP * (n + 1))
                if not before(n, 2):
                    pe.wait_ge(v_o, n - 1)
                for t in range(CH // P):
                    o = ps[:, 2 * par + t // 2, (t % 2) * D:(t % 2 + 1) * D]
                    for k in range(FT):
                        w0 = k * D
                        c0 = k * CH + t * P
                        for q, (lhs, rhs) in enumerate(((oh, wh), (oh, wl), (ol, wh))):
                            last = nc.tensor.matmul(o, lhs[par][:, c0:c0 + P], rhs[:, 2, w0:w0 + D],
                                                    start=(k == 0 and q == 0), stop=(k == FT - 1 and q == 2))
                last.then_inc(p_o, 1)

            steps(pe, body)


_INS = ["x", "ctx_768", "mask_BxS2_bf1", "L0_attn_Wqkv", "L0_attn_Wout", "L0_attn_bout", "L0_xattn_Wq", "L0_xattn_Wk",
        "L0_xattn_Wv", "L0_xattn_Wo", "L0_ffn_w_gate", "L0_ffn_w_up", "L0_ffn_w_down"]


def kernel(**inputs):
    import numpy as np
    import concourse.bacc as bacc
    from concourse.bass_utils import run_bass_kernel_spmd

    nc = bacc.Bacc("TRN2", target_bir_lowering=False, num_devices=1)
    arrays, args = {}, []
    for name in _INS:
        a = np.ascontiguousarray(inputs[name])
        if a.dtype == np.bool_:
            a = a.view(np.uint8)
        arrays[f"in_{name}"] = a
        args.append(nc.dram_tensor(f"in_{name}", a.shape, mybir.dt.from_np(a.dtype), kind="ExternalInput").ap())
    shape = tuple(inputs["x"].shape)
    args.append(nc.dram_tensor("out_x", shape, F32, kind="ExternalOutput").ap())
    decoder_layer(nc, *args)
    r = run_bass_kernel_spmd(nc, [arrays], core_ids=[0])
    return r.results[0]["out_x"]
```
